# Optimizing a Trainium2 kernel written in Bass

```python
import numpy as np
import jax
import jax.numpy as jnp

def _softmax(x, axis=-1):
    return jax.nn.softmax(x, axis=axis)

def _gelu(x):
    return jax.nn.gelu(x, approximate=True)

def _silu(x):
    return jax.nn.silu(x)

def _sigmoid(x):
    return jax.nn.sigmoid(x)

def _layernorm(x, axis=-1, eps=1e-05):
    m = jnp.mean(x, axis=axis, keepdims=True)
    v = jnp.var(x, axis=axis, keepdims=True)
    return (x - m) / jnp.sqrt(v + eps)

def _scatter_add(tgt, idx, src, axis=0):
    return tgt.at[idx].add(src)

def _segment_sum(src, seg, n):
    return jax.ops.segment_sum(src, seg, n)
kernel_name = 'mk_gnn_ffn_d2_gnn_r16_5e4a3f'

def setup_inputs(seed: int=0):
    np.random.seed(seed)
    _w = jnp.asarray

    def _rec_inputs():
        import jax
        import jax.numpy as jnp
        _gk = jax.random.key(seed)
        x = -0.0003713 + 1 * jax.random.normal(jax.random.fold_in(_gk, 1), (3125, 256), jnp.float32)
        _s = jax.random.randint(jax.random.fold_in(_gk, 2), (25000,), 0, 3125, jnp.int32)
        _d = jax.random.randint(jax.random.fold_in(_gk, 3), (25000,), 0, 3125, jnp.int32)
        _loop = jnp.arange(3125, dtype=jnp.int32)
        src = jnp.concatenate([_s, _d, _loop])
        dst = jnp.concatenate([_d, _s, _loop])
        _o = jnp.argsort(dst, stable=True)
        src = src[_o]
        dst = dst[_o]
        return (x, src, dst)
    x, src, dst = _rec_inputs()

    def _L0_gnn_setup():
        import jax, jax.numpy as jnp
        import numpy as np
        N = 3125
        E = 25000
        DIMS = [(256, 512), (512, 512), (512, 256)]
        EPS = 1e-05

        def _sage_bn_relu(h, src, dst, Wl, bl, Wr, gamma, beta):
            agg = jax.ops.segment_sum(h[src], dst, num_segments=N)
            deg = jax.ops.segment_sum(jnp.ones((src.shape[0],), h.dtype), dst, num_segments=N)
            mean_agg = agg / jnp.maximum(deg, 1.0)[:, None]
            out = mean_agg @ Wl + bl + h @ Wr
            mu = out.mean(axis=0)
            var = out.var(axis=0)
            out = (out - mu) * jax.lax.rsqrt(var + EPS) * gamma + beta
            return jax.nn.relu(out)
        key = jax.random.key(seed)
        ks = jax.random.split(key, 2 + 3 * len(DIMS))
        inp = {}
        inp['x'] = jax.random.normal(ks[0], (N, DIMS[0][0]), jnp.float32)
        inp['edge_index'] = jax.random.randint(ks[1], (2, E), 0, N, dtype=jnp.int64)
        for i, (di, do) in enumerate(DIMS):
            s = 1.0 / np.sqrt(di)
            k0, k1, k2 = jax.random.split(ks[2 + i], 3)
            inp[f'Wl{i}'] = jax.random.uniform(k0, (di, do), jnp.float32, -s, s)
            inp[f'bl{i}'] = jax.random.uniform(k1, (do,), jnp.float32, -s, s)
            inp[f'Wr{i}'] = jax.random.uniform(k2, (di, do), jnp.float32, -s, s)
            inp[f'gamma{i}'] = jnp.ones((do,), jnp.float32)
            inp[f'beta{i}'] = jnp.zeros((do,), jnp.float32)
        return inp
    _L0_gnn_all = _L0_gnn_setup()
    _L0_gnn_in = {k: v for k, v in _L0_gnn_all.items() if k in ('Wl0', 'bl0', 'Wr0', 'gamma0', 'beta0', 'Wl1', 'bl1', 'Wr1', 'gamma1', 'beta1', 'Wl2', 'bl2', 'Wr2', 'gamma2', 'beta2')}
    del _L0_gnn_all

    def _L0_ffn_setup():
        import jax, jax.numpy as jnp
        import numpy as np
        DIM = 256
        H = 8
        D = 64
        G = 64
        INNER = H * D
        SCALE = D ** (-0.5)
        key = jax.random.key(seed)
        ks = jax.random.split(key, 12)
        B, N = (4, 1024)
        x = jax.random.normal(ks[0], (B, N, DIM), dtype=jnp.float32)
        s = lambda fan_in: 1.0 / np.sqrt(fan_in)
        W_fx = jax.random.normal(ks[1], (DIM, INNER), dtype=jnp.float32) * s(DIM)
        b_fx = jnp.zeros((INNER,), dtype=jnp.float32)
        W_x = jax.random.normal(ks[2], (DIM, INNER), dtype=jnp.float32) * s(DIM)
        b_x = jnp.zeros((INNER,), dtype=jnp.float32)
        A = jax.random.normal(ks[3], (G, D), dtype=jnp.float32)
        Q, _ = jnp.linalg.qr(A.T)
        W_slice = Q[:, :G].astype(jnp.float32)
        b_slice = jnp.zeros((G,), dtype=jnp.float32)
        W_q = jax.random.normal(ks[4], (D, D), dtype=jnp.float32) * s(D)
        W_k = jax.random.normal(ks[5], (D, D), dtype=jnp.float32) * s(D)
        W_v = jax.random.normal(ks[6], (D, D), dtype=jnp.float32) * s(D)
        W_out = jax.random.normal(ks[7], (INNER, DIM), dtype=jnp.float32) * s(INNER)
        b_out = jnp.zeros((DIM,), dtype=jnp.float32)
        temperature = jnp.ones((1, H, 1, 1), dtype=jnp.float32) * 0.5
        return {'x': x, 'W_fx': W_fx, 'b_fx': b_fx, 'W_x': W_x, 'b_x': b_x, 'W_slice': W_slice, 'b_slice': b_slice, 'W_q': W_q, 'W_k': W_k, 'W_v': W_v, 'W_out': W_out, 'b_out': b_out, 'temperature': temperature}
    _L0_ffn_all = _L0_ffn_setup()
    _L0_ffn_in = {k: v for k, v in _L0_ffn_all.items() if k in ('W_fx', 'b_fx', 'W_x', 'b_x', 'W_slice', 'b_slice', 'W_q', 'W_k', 'W_v', 'W_out', 'b_out', 'temperature')}
    del _L0_ffn_all

    def _L1_gnn_setup():
        import jax, jax.numpy as jnp
        import numpy as np
        N_NODES = 6250
        F_DIM = 256
        NNZ = 100000

        def _prelu(x, a):
            return jnp.where(x >= 0, x, a * x)

        def _hconv(x, W, b, src, dst, n):
            xt = x @ W
            ones = jnp.ones(src.shape, xt.dtype)
            D = jax.ops.segment_sum(ones, src, num_segments=n)
            B = jax.ops.segment_sum(ones, dst, num_segments=n)
            Dinv = jnp.where(D > 0, 1.0 / D, 0.0)
            Binv = jnp.where(B > 0, 1.0 / B, 0.0)
            m = jax.ops.segment_sum(xt[src], dst, num_segments=n) * Binv[:, None]
            out = jax.ops.segment_sum(m[dst], src, num_segments=n) * Dinv[:, None]
            return out + b
        key = jax.random.key(seed)
        k0, k1, k2, k3 = jax.random.split(key, 4)
        x = jax.random.normal(k0, (N_NODES, F_DIM), dtype=jnp.float32)
        edge_index = jax.random.randint(k1, (2, NNZ), 0, N_NODES, dtype=jnp.int32)
        scale = (2.0 / F_DIM) ** 0.5
        W1 = jax.random.normal(k2, (F_DIM, F_DIM), dtype=jnp.float32) * scale
        W2 = jax.random.normal(k3, (F_DIM, F_DIM), dtype=jnp.float32) * scale
        b1 = jnp.zeros((F_DIM,), jnp.float32)
        b2 = jnp.zeros((F_DIM,), jnp.float32)
        a = jnp.full((1,), 0.25, jnp.float32)
        return {'x': x, 'edge_index': edge_index, 'W1': W1, 'b1': b1, 'W2': W2, 'b2': b2, 'a': a}
    _L1_gnn_all = _L1_gnn_setup()
    _L1_gnn_in = {k: v for k, v in _L1_gnn_all.items() if k in ('W1', 'b1', 'W2', 'b2', 'a')}
    del _L1_gnn_all

    def _L1_ffn_setup():
        import jax, jax.numpy as jnp
        import numpy as np
        TOP_K = 2
        LN_EPS = 1e-05
        key = jax.random.key(seed)
        ks = jax.random.split(key, 8)
        B, S, D, E, H = (16, 1024, 256, 8, 1024)
        x = jax.random.normal(ks[0], (B, S, D), dtype=jnp.float32)
        Wr = jax.random.normal(ks[1], (D, E), dtype=jnp.float32) * 0.1
        br = jnp.zeros((E,), dtype=jnp.float32)
        ln_g = jnp.ones((E, D), dtype=jnp.float32)
        ln_b = jnp.zeros((E, D), dtype=jnp.float32)
        W1 = jax.random.normal(ks[2], (E, D, H), dtype=jnp.float32) * (1.0 / np.sqrt(D))
        b1 = jnp.zeros((E, H), dtype=jnp.float32)
        W2 = jax.random.normal(ks[3], (E, H, D), dtype=jnp.float32) * (1.0 / np.sqrt(H))
        b2 = jnp.zeros((E, D), dtype=jnp.float32)
        return {'x': x, 'Wr': Wr, 'br': br, 'ln_g': ln_g, 'ln_b': ln_b, 'W1': W1, 'b1': b1, 'W2': W2, 'b2': b2}
    _L1_ffn_all = _L1_ffn_setup()
    _L1_ffn_in = {k: v for k, v in _L1_ffn_all.items() if k in ('Wr', 'br', 'ln_g', 'ln_b', 'W1', 'b1', 'W2', 'b2')}
    del _L1_ffn_all
    return {'x': x, 'src': src, 'dst': dst, 'L0_gnn_Wl0': _L0_gnn_in['Wl0'], 'L0_gnn_bl0': _L0_gnn_in['bl0'], 'L0_gnn_Wr0': _L0_gnn_in['Wr0'], 'L0_gnn_gamma0': _L0_gnn_in['gamma0'], 'L0_gnn_beta0': _L0_gnn_in['beta0'], 'L0_gnn_Wl1': _L0_gnn_in['Wl1'], 'L0_gnn_bl1': _L0_gnn_in['bl1'], 'L0_gnn_Wr1': _L0_gnn_in['Wr1'], 'L0_gnn_gamma1': _L0_gnn_in['gamma1'], 'L0_gnn_beta1': _L0_gnn_in['beta1'], 'L0_gnn_Wl2': _L0_gnn_in['Wl2'], 'L0_gnn_bl2': _L0_gnn_in['bl2'], 'L0_gnn_Wr2': _L0_gnn_in['Wr2'], 'L0_gnn_gamma2': _L0_gnn_in['gamma2'], 'L0_gnn_beta2': _L0_gnn_in['beta2'], 'L0_ffn_W_fx': _L0_ffn_in['W_fx'], 'L0_ffn_b_fx': _L0_ffn_in['b_fx'], 'L0_ffn_W_x': _L0_ffn_in['W_x'], 'L0_ffn_b_x': _L0_ffn_in['b_x'], 'L0_ffn_W_slice': _L0_ffn_in['W_slice'], 'L0_ffn_b_slice': _L0_ffn_in['b_slice'], 'L0_ffn_W_q': _L0_ffn_in['W_q'], 'L0_ffn_W_k': _L0_ffn_in['W_k'], 'L0_ffn_W_v': _L0_ffn_in['W_v'], 'L0_ffn_W_out': _L0_ffn_in['W_out'], 'L0_ffn_b_out': _L0_ffn_in['b_out'], 'L0_ffn_temperature': _L0_ffn_in['temperature'], 'L1_gnn_W1': _L1_gnn_in['W1'], 'L1_gnn_b1': _L1_gnn_in['b1'], 'L1_gnn_W2': _L1_gnn_in['W2'], 'L1_gnn_b2': _L1_gnn_in['b2'], 'L1_gnn_a': _L1_gnn_in['a'], 'L1_ffn_Wr': _L1_ffn_in['Wr'], 'L1_ffn_br': _L1_ffn_in['br'], 'L1_ffn_ln_g': _L1_ffn_in['ln_g'], 'L1_ffn_ln_b': _L1_ffn_in['ln_b'], 'L1_ffn_W1': _L1_ffn_in['W1'], 'L1_ffn_b1': _L1_ffn_in['b1'], 'L1_ffn_W2': _L1_ffn_in['W2'], 'L1_ffn_b2': _L1_ffn_in['b2']}

def reference(x, src, dst, L0_gnn_Wl0, L0_gnn_bl0, L0_gnn_Wr0, L0_gnn_gamma0, L0_gnn_beta0, L0_gnn_Wl1, L0_gnn_bl1, L0_gnn_Wr1, L0_gnn_gamma1, L0_gnn_beta1, L0_gnn_Wl2, L0_gnn_bl2, L0_gnn_Wr2, L0_gnn_gamma2, L0_gnn_beta2, L0_ffn_W_fx, L0_ffn_b_fx, L0_ffn_W_x, L0_ffn_b_x, L0_ffn_W_slice, L0_ffn_b_slice, L0_ffn_W_q, L0_ffn_W_k, L0_ffn_W_v, L0_ffn_W_out, L0_ffn_b_out, L0_ffn_temperature, L1_gnn_W1, L1_gnn_b1, L1_gnn_W2, L1_gnn_b2, L1_gnn_a, L1_ffn_Wr, L1_ffn_br, L1_ffn_ln_g, L1_ffn_ln_b, L1_ffn_W1, L1_ffn_b1, L1_ffn_W2, L1_ffn_b2):
    import jax
    import jax.numpy as jnp

    def _L0_gnn_ref(x, edge_index, Wl0, bl0, Wr0, gamma0, beta0, Wl1, bl1, Wr1, gamma1, beta1, Wl2, bl2, Wr2, gamma2, beta2):
        import jax, jax.numpy as jnp
        import numpy as np
        N = 3125
        E = 25000
        DIMS = [(256, 512), (512, 512), (512, 256)]
        EPS = 1e-05

        def _sage_bn_relu(h, src, dst, Wl, bl, Wr, gamma, beta):
            agg = jax.ops.segment_sum(h[src], dst, num_segments=N)
            deg = jax.ops.segment_sum(jnp.ones((src.shape[0],), h.dtype), dst, num_segments=N)
            mean_agg = agg / jnp.maximum(deg, 1.0)[:, None]
            out = mean_agg @ Wl + bl + h @ Wr
            mu = out.mean(axis=0)
            var = out.var(axis=0)
            out = (out - mu) * jax.lax.rsqrt(var + EPS) * gamma + beta
            return jax.nn.relu(out)
        src, dst = (edge_index[0], edge_index[1])
        params = [(Wl0, bl0, Wr0, gamma0, beta0), (Wl1, bl1, Wr1, gamma1, beta1), (Wl2, bl2, Wr2, gamma2, beta2)]
        h = x
        for Wl, bl, Wr, g, b in params:
            h = _sage_bn_relu(h, src, dst, Wl, bl, Wr, g, b)
        return h

    def _L0_ffn_ref(x, W_fx, b_fx, W_x, b_x, W_slice, b_slice, W_q, W_k, W_v, W_out, b_out, temperature):
        import jax, jax.numpy as jnp
        import numpy as np
        DIM = 256
        H = 8
        D = 64
        G = 64
        INNER = H * D
        SCALE = D ** (-0.5)
        B, N, _ = x.shape
        fx_mid = (x @ W_fx + b_fx).reshape(B, N, H, D).transpose(0, 2, 1, 3)
        x_mid = (x @ W_x + b_x).reshape(B, N, H, D).transpose(0, 2, 1, 3)
        temp = jnp.clip(temperature, 0.1, 5.0)
        slice_weights = jax.nn.softmax((x_mid @ W_slice + b_slice) / temp, axis=-1)
        slice_norm = slice_weights.sum(axis=2)
        slice_token = jnp.einsum('bhnc,bhng->bhgc', fx_mid, slice_weights)
        slice_token = slice_token / (slice_norm[..., None] + 1e-05)
        q = slice_token @ W_q
        k = slice_token @ W_k
        v = slice_token @ W_v
        attn = jax.nn.softmax(jnp.einsum('bhgc,bhkc->bhgk', q, k) * SCALE, axis=-1)
        out_slice = jnp.einsum('bhgk,bhkc->bhgc', attn, v)
        out_x = jnp.einsum('bhgc,bhng->bhnc', out_slice, slice_weights)
        out_x = out_x.transpose(0, 2, 1, 3).reshape(B, N, INNER)
        return out_x @ W_out + b_out

    def _L1_gnn_ref(x, edge_index, W1, b1, W2, b2, a):
        import jax, jax.numpy as jnp
        import numpy as np
        N_NODES = 6250
        F_DIM = 256
        NNZ = 100000

        def _prelu(x, a):
            return jnp.where(x >= 0, x, a * x)

        def _hconv(x, W, b, src, dst, n):
            xt = x @ W
            ones = jnp.ones(src.shape, xt.dtype)
            D = jax.ops.segment_sum(ones, src, num_segments=n)
            B = jax.ops.segment_sum(ones, dst, num_segments=n)
            Dinv = jnp.where(D > 0, 1.0 / D, 0.0)
            Binv = jnp.where(B > 0, 1.0 / B, 0.0)
            m = jax.ops.segment_sum(xt[src], dst, num_segments=n) * Binv[:, None]
            out = jax.ops.segment_sum(m[dst], src, num_segments=n) * Dinv[:, None]
            return out + b
        src, dst = (edge_index[0], edge_index[1])
        n = x.shape[0]
        h = _prelu(_hconv(x, W1, b1, src, dst, n), a)
        h = _hconv(h, W2, b2, src, dst, n) + x
        return _prelu(h, a)

    def _L1_ffn_ref(x, Wr, br, ln_g, ln_b, W1, b1, W2, b2):
        import jax, jax.numpy as jnp
        import numpy as np
        TOP_K = 2
        LN_EPS = 1e-05
        B, S, D = x.shape
        N = B * S
        xt = x.reshape(N, D)
        logits = xt @ Wr + br
        probs = jax.nn.softmax(logits, axis=-1)
        top_p, top_idx = jax.lax.top_k(probs, TOP_K)
        weights = top_p / top_p.sum(axis=-1, keepdims=True)
        mu = xt.mean(axis=-1, keepdims=True)
        var = ((xt - mu) ** 2).mean(axis=-1, keepdims=True)
        xn = (xt - mu) * jax.lax.rsqrt(var + LN_EPS)
        xe = xn[None, :, :] * ln_g[:, None, :] + ln_b[:, None, :]
        h = jax.nn.gelu(jnp.einsum('end,edh->enh', xe, W1) + b1[:, None, :], approximate=False)
        y = jnp.einsum('enh,ehd->end', h, W2) + b2[:, None, :]
        y_tok = jnp.transpose(y, (1, 0, 2))
        sel = jnp.take_along_axis(y_tok, top_idx[:, :, None], axis=1)
        out = (weights[:, :, None] * sel).sum(axis=1)
        return out.reshape(B, S, D)
    edge_index = jnp.stack([src, dst])
    x = x + _L0_gnn_ref(_layernorm(x, axis=-1), edge_index, L0_gnn_Wl0, L0_gnn_bl0, L0_gnn_Wr0, L0_gnn_gamma0, L0_gnn_beta0, L0_gnn_Wl1, L0_gnn_bl1, L0_gnn_Wr1, L0_gnn_gamma1, L0_gnn_beta1, L0_gnn_Wl2, L0_gnn_bl2, L0_gnn_Wr2, L0_gnn_gamma2, L0_gnn_beta2)
    x = x + _L0_ffn_ref(_layernorm(x, axis=-1)[None], L0_ffn_W_fx, L0_ffn_b_fx, L0_ffn_W_x, L0_ffn_b_x, L0_ffn_W_slice, L0_ffn_b_slice, L0_ffn_W_q, L0_ffn_W_k, L0_ffn_W_v, L0_ffn_W_out, L0_ffn_b_out, L0_ffn_temperature)[0]
    x = x + _L1_gnn_ref(_layernorm(x, axis=-1), edge_index, L1_gnn_W1, L1_gnn_b1, L1_gnn_W2, L1_gnn_b2, L1_gnn_a)
    x = x + _L1_ffn_ref(_layernorm(x, axis=-1)[None], L1_ffn_Wr, L1_ffn_br, L1_ffn_ln_g, L1_ffn_ln_b, L1_ffn_W1, L1_ffn_b1, L1_ffn_W2, L1_ffn_b2)[0]
    return x

_drawn_inputs = setup_inputs


def setup_inputs(seed=0):
    import zlib

    import numpy as np

    out = dict(_drawn_inputs(seed))
    spreads = {'L0_gnn_gamma0': (1.0, 0.2),
     'L0_gnn_beta0': (0.0, 0.1),
     'L0_gnn_gamma1': (1.0, 0.2),
     'L0_gnn_beta1': (0.0, 0.1),
     'L0_gnn_gamma2': (1.0, 0.2),
     'L0_gnn_beta2': (0.0, 0.1),
     'L0_ffn_b_fx': (0.0, 0.1),
     'L0_ffn_b_x': (0.0, 0.591),
     'L0_ffn_b_slice': (0.0, 0.8),
     'L0_ffn_b_out': (0.0, 0.1),
     'L0_ffn_temperature': (0.5, 0.6),
     'L1_gnn_b1': (0.0, 0.1),
     'L1_gnn_b2': (0.0, 0.1),
     'L1_ffn_br': (0.0, 0.1),
     'L1_ffn_ln_g': (1.0, 0.2),
     'L1_ffn_ln_b': (0.0, 0.297),
     'L1_ffn_b1': (0.0, 0.307),
     'L1_ffn_b2': (0.0, 0.1)}
    factors = {'L0_gnn_bl0': 8.0,
     'L0_gnn_bl1': 8.0,
     'L0_gnn_bl2': 8.0,
     'L0_ffn_W_x': 6.377,
     'L0_ffn_W_slice': 6.522,
     'L0_ffn_W_q': 8.0,
     'L0_ffn_W_k': 8.0}
    for name, (base, spread) in spreads.items():
        noise = np.random.default_rng([zlib.crc32(name.encode()), seed]).standard_normal(out[name].shape)
        drawn = base * np.exp(spread * noise) if base else spread * noise
        out[name] = jnp.asarray(drawn.astype(out[name].dtype))
    for name, factor in factors.items():
        out[name] = (out[name] * factor).astype(out[name].dtype)
    return out
```

```python
import concourse.bass as bass
from concourse import mybir
from contextlib import ExitStack, contextmanager

P = 128
N = 3125
EDGES = 53125
F = 256
HID = 512
T = -(-N // P)
TAIL = N - (T - 1) * P
BT = 5
NB = T // BT
BC = BT * P
HB = BC // 2
EC = -(-EDGES // P)
GQ = 4
GE = GQ * P
NG = EC // GQ
LOOK = 4
AROW = T * BC
ASIZE = NB * P * AROW
EPS = 1e-5
LN_SCALE = 1024.0
BN_BOUND = 56.0
HEADS, DH, G = 8, 64, 64
EXPERTS, EH = 8, 1024
CAP = 256
CHUNKS = (2 * N + EXPERTS * (CAP - 1)) // CAP
SLOTS = CHUNKS * CAP
fp32, fp16, i32, u32 = mybir.dt.float32, mybir.dt.float16, mybir.dt.int32, mybir.dt.uint32
ALU, ACT, AX = mybir.AluOpType, mybir.ActivationFunctionType, mybir.AxisListType


class Order:

    def __init__(self, eng, sem):
        self.eng, self.sem, self.base, self.n, self.turn, self.per = eng, sem, 0, 0, None, 0

    def mark(self, ins):
        ins.then_inc(self.sem, 1)
        self.n += 1

    def settle(self):
        if self.turn is None:
            self.eng.wait_ge(self.sem, self.base + self.n)
        else:
            self.eng.wait_ge(self.sem, self.turn * self.per + (self.base + self.n))

    @contextmanager
    def loop(self, count, per):
        self.base, self.n = self.base + self.n, 0
        with self.eng.Fori(0, count) as i:
            self.turn, self.per = i, per
            yield i
            assert self.n == per, (self.n, per)
        self.base, self.n, self.turn = self.base + count * per, 0, None

    @contextmanager
    def loop_from(self, first, end, per):
        self.base, self.n = self.base + self.n - first * per, 0
        with self.eng.Fori(first, end) as i:
            self.turn, self.per = i, per
            yield i
            assert self.n == per, (self.n, per)
        self.base, self.n, self.turn = self.base + end * per, 0, None


def build(nc, x, src, dst, w, out):
    ctx = ExitStack()
    with ctx:
        def sb(name, shape, dt=fp32):
            return ctx.enter_context(nc.sbuf_tensor(name, shape, dt))

        def sem(name):
            return ctx.enter_context(nc.semaphore(name))

        def dram(name, shape, dt):
            return nc.dram_tensor(name, shape, dt, kind="Internal").ap()

        def runs(ap, **k):
            return ap.rearrange("p (a b) -> p a b", **k)

        at_flat = dram("at_counts", (ASIZE + GE, 1), fp16)
        ad_flat = dram("ad_counts", (ASIZE, 1), fp16)
        at = at_flat[0:ASIZE, :].rearrange("(b p r) a -> p b (r a)", b=NB, p=P)
        ad = ad_flat.rearrange("(b p r) a -> p b (r a)", b=NB, p=P)
        key_rows = dram("key_rows", (EC * P,), fp32)

        ring = sb("ring", [P, 8192])
        harena = sb("harena", [P, 12864])
        tarena = sb("tarena", [P, 4 * T * P])
        xrows = sb("xrows", [P, T, F])
        wl = sb("wl", [P, 2048])
        wr = sb("wr", [P, 2048])
        feat = sb("feat", [P, 4, BC])
        late = sb("late", [P, T * P])
        wxs = sb("wxs", [P, 2, HID])
        ident = sb("ident", [P, P])
        ident16 = sb("ident16", [P, P], fp16)
        ones = sb("ones", [P, P])
        ones16 = sb("ones16", [P, P], fp16)
        tri = sb("tri", [P, P])
        ln_st = sb("ln_st", [P, T, 6])
        ln_mv = sb("ln_mv", [P, T, 2])
        ln_r = sb("ln_r", [P, T])
        ln_s = sb("ln_s", [P, T])
        rowmask = sb("rowmask", [P, T])
        bn_st = sb("bn_st", [P, 4, 2 * NB, 6])
        bn_mv = sb("bn_mv", [P, 4, 2])
        bn_k = sb("bn_k", [P, 4, 4])
        vec = [sb(f"vec{l}", [P, 3, 4]) for l in range(3)]
        amax = sb("amax", [P, T])
        sc = sb("sc", [P, 4])
        sc1 = sb("sc1", [1, 4])
        slice_bias = sb("slice_bias", [1, HID])

        chunk = [ring[:, :].bitcast(fp16)[:, q * BT * BC:(q + 1) * BT * BC].rearrange("p (s c) -> p s c", s=BT)
                 for q in range(NB)]
        chunk_flat = [ring[:, :].bitcast(fp16)[:, q * BT * BC:(q + 1) * BT * BC] for q in range(NB)]
        h16 = harena[:, :].bitcast(fp16)

        def halves(d):
            return (runs(h16[:, 0:T * d], a=T), runs(h16[:, T * d:2 * T * d], a=T))

        tfeat = tarena[:, :].rearrange("p (f n) -> p f n", f=4)
        zeros16 = tarena[:, :].bitcast(fp16)[:, 0:AROW]
        deginv = late[:, :]
        ps = ctx.enter_context(nc.psum_tensor("ps", [P, 8, 512], fp32))
        ps16 = ps[:, :, :].bitcast(fp16)

        astore = [harena[:, 6432 + s * 1600:6432 + (s + 1) * 1600].bitcast(fp16).rearrange("p (i c) -> p i c", i=BT) for s in range(2)]

        eint = harena[:, 6432:6432 + 3 * EC].bitcast(i32).rearrange("p (a c) -> p a c", a=3)
        eflt = harena[:, 7680:7680 + 4 * EC].rearrange("p (a c) -> p a c", a=4)
        keyT = harena[0:EC // GQ, 9344:9344 + GE]
        ekey = ring[:, 0:EC]
        espare = ring[:, EC:2 * EC]
        eweight = ring[:, 1024:1024 + GQ * GE].rearrange("p (a c) -> p a c", a=GQ)
        krow = ring[:, 3072:3072 + LOOK * GE].rearrange("p (a c) -> p a c", a=LOOK)
        ejunk = ring[:, 5120:5120 + GQ * GE].rearrange("p (a c) -> p a c", a=GQ)
        ecount = ring[:, 7168:7168 + 4 * GQ].rearrange("p (a c) -> p a c", a=4)
        eshift = ring[:, 7200:7200 + 4 * GQ].rearrange("p (a c) -> p a c", a=4)
        eidx = ring[:, 7232:7232 + 4 * GQ].bitcast(i32).rearrange("p (a c) -> p a c", a=4)
        evalue = ring[:, 7264:7264 + 4 * GQ].bitcast(fp16)[:, 0:4 * GQ].rearrange("p (a c) -> p a c", a=4)
        etrash_i = ring[:, 7296:7296 + GQ].bitcast(i32)
        etrash = ring[:, 7304:7304 + GQ]
        wx_in = tarena[:, 8192:8192 + 2 * HID].rearrange("p (a c) -> p a c", a=2)
        wxT = tarena[0:DH, 9216:9216 + HEADS * F].rearrange("p (h d) -> p h d", h=HEADS)
        wsl = tarena[0:DH, 11264:11264 + G]
        bxT = tarena[0:DH, 11328:11328 + HEADS]
        temp_row = tarena[0:1, 11336:11336 + HEADS]
        rtemp = tarena[:, 11344:11344 + HEADS]
        bsl_row = tarena[0:1, 11352:11352 + G]
        bias_raw = tarena[0:1, 11416:11416 + HID]

        wl2 = wl[:, :].rearrange("p (d f) -> p d f", f=HID)
        wr2 = wr[:, :].rearrange("p (d f) -> p d f", f=HID)
        wr3 = wr[:, 0:1024].rearrange("p (d f) -> p d f", f=F)
        wl3 = wr[:, 1024:2048].rearrange("p (d f) -> p d f", f=F)
        urow = feat[:, 2:4, :].rearrange("p a b -> p (a b)").rearrange("p (t c) -> p t c", c=F)
        stage_rows = runs(harena[:, 6432:6432 + T * F], a=T)

        logit = harena[:, 0:2 * HID].rearrange("p (s c) -> p s c", s=2)
        sweight = harena[:, 1024:1024 + 2 * HID].rearrange("p (s c) -> p s c", s=2)
        tokT = harena[:, 2048:2048 + 2 * HID].rearrange("p (d c) -> p d c", d=2)
        norm = harena[0:DH, 3072:3072 + HID]
        rnorm = harena[0:DH, 3584:3584 + HID]
        slT, qT, kT, vS, att, attT, outT = (harena[0:DH, 4096 + k * HID:4096 + (k + 1) * HID] for k in range(7))
        pmat = harena[:, 7680:7680 + 4 * F].rearrange("p (k o) -> p k o", k=4)
        wqkv = harena[0:DH, 8704:8704 + 3 * DH].rearrange("p (k c) -> p k c", k=3)
        bfx = harena[0:1, 8896:8896 + HID]
        hmax = harena[:, 9416:9416 + 2 * HEADS].rearrange("p (s h) -> p s h", s=2)
        hsum = harena[:, 9432:9432 + 2 * HEADS].rearrange("p (s h) -> p s h", s=2)
        hrec = harena[:, 9448:9448 + 2 * HEADS].rearrange("p (s h) -> p s h", s=2)
        bout = harena[:, 9472:9472 + F]
        zero_row = harena[0:1, 9728:9728 + HID]
        wout = wl[0:DH, :].rearrange("p (h o) -> p h o", h=HEADS)
        wfx = wr[:, 0:1024].rearrange("p (d c) -> p d c", d=2)
        wconv = [wr[:, 1024 + k * 512:1536 + k * 512].rearrange("p (d c) -> p d c", d=2) for k in range(2)]
        bconv = [late[:, k * F:(k + 1) * F] for k in range(2)]
        slope = late[:, 512:513]
        rdeg = late[:, 520:520 + BT]
        rows2 = tarena[:, 0:T * F].rearrange("p (t c) -> p t c", t=T)
        zrows, negrows, urows = (runs(tarena[:, (T + k * BT) * F:(T + (k + 1) * BT) * F], a=BT) for k in range(3))
        hh1 = h16[:, 0:T * (F + 2)].rearrange("p (t c) -> p t c", t=T)
        hl1 = h16[:, T * (F + 2):T * (F + 2) + T * F].rearrange("p (t c) -> p t c", t=T)
        wroute = late[:, 600:600 + 2 * EXPERTS].rearrange("p (d e) -> p d e", d=2)
        broute = late[0:1, 616:616 + EXPERTS]
        evec_rows = late[0:96, 640:640 + P]
        evec = late[:, 768:768 + 96]
        b2_rows = late[0:1, 896:896 + EXPERTS * F]
        xnT = tarena[:, T * F:2 * T * F].rearrange("p (d n) -> p d n", d=2)
        w1e = [ring[:, s * 4096:s * 4096 + 2048].rearrange("p (d h) -> p d h", d=2) for s in range(2)]
        w2e = [ring[:, s * 4096 + 2048:(s + 1) * 4096].rearrange("p (k o) -> p k o", k=EH // P) for s in range(2)]
        hT = harena[:, 0:EH // P * BC].rearrange("p (k n) -> p k n", k=EH // P)
        lgt, pri, sel1, sel2, wgt = (harena[:, 6000 + k * T * EXPERTS:6000 + (k + 1) * T * EXPERTS].rearrange("p (t e) -> p t e", t=T) for k in range(5))
        top1, top2, gate1, gate2, first = (harena[:, 7000 + k * T:7000 + (k + 1) * T] for k in range(5))
        rank = harena[:, 7200:7200 + EXPERTS]

        consts_ready, filled, edges_in, x_in, zero_ready, zeroed, vec_in = map(sem, (
            "consts_ready", "filled", "edges_in", "x_in", "zero_ready", "zeroed", "vec_in"))
        fold_in, fold_pe, fold_dve = map(sem, ("fold_in", "fold_pe", "fold_dve"))
        keyT_psum, keyT_ready, key_ready, key_stored = map(sem, ("keyT_psum", "keyT_ready", "key_ready", "key_stored"))
        krow_in = [sem(f"krow_in{s}") for s in range(LOOK)]
        compared, idx_ready, scattered = map(sem, ("compared", "idx_ready", "scattered"))
        chunk_in = [sem(f"chunk_in{q}") for q in range(NB)]
        chunk_used = [sem(f"chunk_used{q}") for q in range(NB)]
        wr_in, wl_in, wr1_in, wl1_in, w2_in = map(sem, ("wr_in", "wl_in", "wr1_in", "wl1_in", "w2_in"))
        dve_order, act_order, pool_order = map(sem, ("dve_order", "act_order", "pool_order"))
        ln_var, ln_std, bn_done = map(sem, ("ln_var", "ln_std", "bn_done"))
        sc_col, sc_row, sc_pow, sc_all, sc_ready = map(sem, ("scale_columns", "scale_across", "scale_power", "scale_spread", "scale_ready"))
        ad_ps, ad_sb = sem("ad_transposed"), sem("ad_copied")
        ad_out = [sem(f"ad_stored{s}") for s in range(2)]

        def fresh(tag, *names):
            return [sem(f"{tag}_{n}") for n in names]

        ent = [fresh(f"in{l}", "rows", "hi", "lo", "tps", "tcopied", "rps", "rdone") for l in range(4)]
        agg = [fresh(f"agg{l}", "mean", "ops", "odone", "deg", "degdone") for l in range(3)]
        ffn_w, conv_w, moe_w = sem("ffn_weights_in"), sem("conv_weights_in"), sem("moe_weights_in")
        f_zero, f_rows, f_tps, f_tcp, f_lg, f_sub, f_exp, f_sw, f_used, f_swc = fresh(
            "ffn", "zeros", "rows", "transposed", "copied", "logits", "shifted", "exps", "weights", "weights_used", "weightsT_copied")
        f_pe, f_dve, f_act, f_bias, f_slot, f_rps, f_x = fresh("ffn", "pe", "dve", "act", "bias_added", "slots_filled", "out_rows", "x")
        conv = [fresh(f"conv{k}", "rows", "transposed", "copied", "products", "staged", "largest") for k in range(2)]
        c_ones, c_hi, c_lo, c_read, c_stage, c_max, c_h, c_x = fresh("conv", "ones", "hi", "lo", "sums_read", "staged", "largest", "hidden", "x")
        r_rows, r_tps, r_tcp, r_lg, r_lgc = fresh("route", "rows", "transposed", "copied", "logits", "logits_copied")
        r_gap, r_exp = fresh("route", "gap", "exps")
        e_vec, e_vecT = fresh("expert", "vectors", "vectors_copied")
        e_rows, e_tps, e_tcp = fresh("expert", "rows", "transposed", "copied")
        w_in = [sem(f"expert_weights_in{s}") for s in range(2)]
        e_xe, e_hps, e_gelu, e_yps, e_x = fresh("expert", "inputs", "hidden", "gelus", "outputs", "x")
        block = ctx.enter_context(nc.Block())

        def nodes(b):
            return bass.ds(b * BC, BC)

        def two(ap):
            return ap.rearrange("p (h c) -> p h c", h=2)

        DIMS = [(2, 4), (4, 4), (4, 2)]
        PASSES = [1, 2, 1]
        FIRST = [0, NB, 3 * NB, 4 * NB]

        @block.sync
        def _(sp):
            sp.wait_ge(filled, 2)
            cut = (P - 1) * EC
            for a, e in ((0, src), (1, dst)):
                for p0, p1 in ((0, 112), (112, P - 1)):
                    sp.dma_start(eint[p0:p1, a, :], e[p0 * EC:p1 * EC].rearrange("(p c) -> p c", c=EC)).then_inc(edges_in, 16)
                sp.dma_start(eint[P - 1:P, a, 0:EDGES - cut], e[cut:EDGES].rearrange("(p c) -> p c", p=1)).then_inc(edges_in, 16)
            sp.dma_start(xrows[:, 0:T - 1, :], x[0:(T - 1) * P, :].rearrange("(t p) d -> p t d", p=P)).then_inc(x_in, 16)
            sp.dma_start(xrows[0:TAIL, T - 1, :], x[(T - 1) * P:N, :]).then_inc(x_in, 16)
            sp.wait_ge(zero_ready, 1)
            for b in range(NB):
                sp.dma_start(at[:, b, :], zeros16).then_inc(zeroed, 16)
            sp.dma_start(at_flat[ASIZE:ASIZE + GE, :].rearrange("(p n) a -> p (n a)", p=P), zeros16[:, 0:GE // P]).then_inc(zeroed, 16)
            sp.wait_ge(keyT_ready, 1)
            sp.dma_start(key_rows.rearrange("(q r n) -> r q n", q=GQ, n=P), keyT.rearrange("r (q n) -> r q n", q=GQ)).then_inc(key_stored, 16)
            sp.wait_ge(key_stored, 16)
            for s in range(LOOK):
                sp.dma_start(krow[:, s, :], key_rows[s * GE:(s + 1) * GE].partition_broadcast(P)).then_inc(krow_in[s], 16)
            with sp.Fori(0, NG // LOOK - 1) as i:
                for s in range(LOOK):
                    sp.wait_ge(compared, LOOK * i + (s + 1))
                    sp.dma_start(krow[:, s, :], key_rows[bass.ds(i * (LOOK * GE) + (s + LOOK) * GE, GE)].partition_broadcast(P)).then_inc(krow_in[s], 16)
            sp.wait_ge(scattered, NG * GQ * 16)

            def load_chunks(table, b, done):
                for q in range(NB):
                    sp.wait_ge(chunk_used[q], done)
                    sp.dma_start(chunk_flat[q], table[:, bass.ds(b, 1), q * BT * BC:(q + 1) * BT * BC].rearrange("p o e -> p (o e)")).then_inc(chunk_in[q], 16)

            for l in range(3):
                with sp.Fori(0, NB) as b:
                    for k in range(PASSES[l]):
                        load_chunks(at, b, b * PASSES[l] + (FIRST[l] + k + 1))
            for s, n in ((0, 3), (1, 2)):
                sp.wait_ge(ad_out[s], 16 * (n * NB + 1))
            for c in range(4):
                with sp.Fori(0, NB) as b:
                    load_chunks(at if c % 2 == 0 else ad, b, b + (FIRST[3] + c * NB + 1))
            for q in range(NB):
                sp.wait_ge(chunk_used[q], FIRST[3] + 4 * NB + 1)
            with sp.Fori(0, EXPERTS // 2) as g:
                for s in range(2):
                    sp.wait_ge(e_yps, g * (2 * T) + (s + 1) * T)
                    e = bass.ds(g * 2 + s, 1)
                    sp.dma_start(w1e[s], w["L1_ffn_W1"][e, :, :].rearrange("e (d p) h -> p (e d) h", p=P)).then_inc(w_in[s], 16)
                    sp.dma_start(w2e[s], w["L1_ffn_W2"][e, :, :].rearrange("e (k p) o -> p (e k) o", p=P)).then_inc(w_in[s], 16)
            sp.wait_ge(e_x, EXPERTS * T + 1)
            sp.dma_start(out[0:(T - 1) * P, :].rearrange("(t p) d -> p t d", p=P), xrows[:, 0:T - 1, :]).then_inc(x_in, 16)
            sp.dma_start(out[(T - 1) * P:N, :], xrows[0:TAIL, T - 1, :]).then_inc(x_in, 16)
            sp.wait_ge(x_in, 64)

        @block.gpsimd
        def _(pool):
            o = Order(pool, pool_order)
            nc.gpsimd.memset(eint[:, 0:2, :], T * P - 1).then_inc(filled, 1)
            nc.gpsimd.memset(xrows[:, T - 1, :], 0.0).then_inc(filled, 1)
            for q in range(NB):
                pool.sem_inc(chunk_used[q], 1)
            o.mark(nc.gpsimd.memset(ident[:, :], 0.0))
            o.mark(nc.gpsimd.memset(tri[:, :], 1.0))
            o.mark(nc.gpsimd.memset(rowmask[:, :], 1.0))
            o.mark(nc.gpsimd.memset(eweight, 1025.0))
            o.mark(nc.gpsimd.memset(ones[:, :], 1.0))
            o.mark(nc.gpsimd.memset(ones16[:, :], 1.0))
            o.mark(nc.gpsimd.iota(etrash_i, pattern=[[P, GQ]], base=ASIZE, channel_multiplier=1))
            o.settle()
            o.mark(nc.gpsimd.affine_select(out=ident[:, :], in_=ident[:, :], compare_op=ALU.not_equal, fill=1.0, base=0,
                                           pattern=[[-1, P]], channel_multiplier=1))
            o.mark(nc.gpsimd.affine_select(out=tri[:, :], in_=tri[:, :], compare_op=ALU.is_gt, fill=0.0, base=0,
                                           pattern=[[1, P]], channel_multiplier=-1))
            o.mark(nc.gpsimd.affine_select(out=rowmask[:, T - 1:T], in_=rowmask[:, T - 1:T], compare_op=ALU.is_gt, fill=0.0,
                                           base=TAIL, pattern=[[0, 1]], channel_multiplier=-1))
            o.mark(nc.gpsimd.affine_select(out=eweight, in_=eweight, compare_op=ALU.is_gt, fill=1.0, base=0,
                                           pattern=[[P, GQ], [-1, GE]], channel_multiplier=1))
            o.settle()
            nc.gpsimd.tensor_copy(ident16[:, :], ident[:, :]).then_inc(consts_ready, 1)
            pool.wait_ge(zeroed, 16 * (NB + 1))
            with pool.Fori(0, NG // LOOK) as i:
                for s in range(LOOK):
                    pool.wait_ge(idx_ready, LOOK * i + (s + 1))
                    pool.nop(nofuse=True)
                    for q in range(GQ):
                        nc.gpsimd.indirect_dma_start(
                            out=at_flat, out_offset=bass.IndirectOffsetOnAxis(ap=eidx[:, s, q:q + 1], axis=0),
                            in_=evalue[:, s, q:q + 1], in_offset=None, compute_op=ALU.add).then_inc(scattered, 16)
                    pool.wait_ge(scattered, i * (LOOK * GQ * 16) + (s + 1) * (GQ * 16))
            pool.wait_ge(ent[0][5], NB * 4 + 1)
            pool.dma_start(wr2, w["L0_gnn_Wr1"].rearrange("(d p) f -> p d f", p=P)).then_inc(wr1_in, 16)
            pool.wait_ge(agg[0][1], NB * 4 + 1)
            pool.dma_start(wl2, w["L0_gnn_Wl1"].rearrange("(d p) f -> p d f", p=P)).then_inc(wl1_in, 16)
            pool.wait_ge(ent[1][5], NB * 4 + 1)
            pool.dma_start(wr3, w["L0_gnn_Wr2"].rearrange("(d p) f -> p d f", p=P)).then_inc(w2_in, 16)
            pool.dma_start(wl3, w["L0_gnn_Wl2"].rearrange("(d p) f -> p d f", p=P)).then_inc(w2_in, 16)
            pool.wait_ge(chunk_used[NB - 1], FIRST[3] + 1)
            pool.wait_ge(agg[2][0], 2 * NB + 1)
            pool.dma_start(wout, w["L0_ffn_W_out"].rearrange("(h c) o -> c h o", c=DH)).then_inc(ffn_w, 16)
            pool.dma_start(wfx, w["L0_ffn_W_fx"].rearrange("(d p) f -> p d f", p=P)).then_inc(ffn_w, 16)
            for k, name in enumerate("qkv"):
                pool.dma_start(wqkv[:, k, :], w[f"L0_ffn_W_{name}"]).then_inc(ffn_w, 16)
            pool.dma_start(bfx, w["L0_ffn_b_fx"].rearrange("(a c) -> a c", a=1)).then_inc(ffn_w, 16)
            pool.dma_start(bout, w["L0_ffn_b_out"].partition_broadcast(P)).then_inc(ffn_w, 16)
            for k in range(2):
                pool.dma_start(wconv[k], w[f"L1_gnn_W{k + 1}"].rearrange("(d p) f -> p d f", p=P)).then_inc(conv_w, 16)
                pool.dma_start(bconv[k], w[f"L1_gnn_b{k + 1}"].partition_broadcast(P)).then_inc(conv_w, 16)
            pool.dma_start(slope, w["L1_gnn_a"].partition_broadcast(P)).then_inc(conv_w, 16)
            pool.dma_start(wroute, w["L1_ffn_Wr"].rearrange("(d p) e -> p d e", p=P)).then_inc(moe_w, 16)
            pool.dma_start(broute, w["L1_ffn_br"].rearrange("(a e) -> a e", a=1)).then_inc(moe_w, 16)
            pool.dma_start(evec_rows[0:64, :], w["L1_ffn_b1"].rearrange("e (k p) -> (e k) p", p=P)).then_inc(moe_w, 16)
            pool.dma_start(evec_rows[64:80, :], w["L1_ffn_ln_g"].rearrange("e (d p) -> (e d) p", p=P)).then_inc(moe_w, 16)
            pool.dma_start(evec_rows[80:96, :], w["L1_ffn_ln_b"].rearrange("e (d p) -> (e d) p", p=P)).then_inc(moe_w, 16)
            pool.dma_start(b2_rows, w["L1_ffn_b2"].rearrange("(a e) o -> a (e o)", a=1)).then_inc(moe_w, 16)
            pool.wait_ge(f_rows, T)
            pool.wait_ge(ffn_w, 16 * 7)
            nc.gpsimd.tensor_tensor(xrows[:, :, :], xrows[:, :, :], bout.unsqueeze(1).to_broadcast([P, T, F]), ALU.add).then_inc(f_bias, 1)
            rows, tps = conv[1][0:2]
            pool.wait_ge(c_h, NB)
            with pool.Fori(0, NB) as b:
                for i in range(BT):
                    pool.wait_ge(tps, b * BT + (i + 1))
                    pool.nop(nofuse=True)
                    nc.gpsimd.tensor_copy(urow[:, i:i + 1, :], rows2[:, bass.ds(b * BT + i, 1), :]).then_inc(rows, 1)

        @block.scalar
        def _(act):
            def wait(s, value):
                act.wait_ge(s, value)
                if not isinstance(value, int):
                    act.nop(nofuse=True)

            act.sem_inc(ad_out[0], 16)
            act.sem_inc(ad_out[1], 16)
            act.sem_inc(ad_sb, 1)
            for l in range(4):
                act.sem_inc(ent[l][1], 1)
                act.sem_inc(ent[l][4], 1)
                act.sem_inc(ent[l][6], 1)
            for l in range(3):
                for k, name in enumerate(("bl", "gamma", "beta")):
                    act.dma_start(vec[l][:, k, 0:DIMS[l][1]], w[f"L0_gnn_{name}{l}"].rearrange("(f p) -> p f", p=P), allow_slow_non_contiguous=True).then_inc(vec_in, 16)
            act.dma_start(wr2[:, 0:2, :], w["L0_gnn_Wr0"].rearrange("(d p) f -> p d f", p=P)).then_inc(wr_in, 16)
            act.dma_start(wl2[:, 0:2, :], w["L0_gnn_Wl0"].rearrange("(d p) f -> p d f", p=P)).then_inc(wl_in, 16)
            act.dma_start(wx_in, w["L0_ffn_W_x"].rearrange("(d p) f -> p d f", p=P)).then_inc(fold_in, 16)
            act.dma_start(wsl, w["L0_ffn_W_slice"]).then_inc(fold_in, 16)
            act.dma_start(bxT, w["L0_ffn_b_x"].rearrange("(h c) -> c h", c=DH), allow_slow_non_contiguous=True).then_inc(fold_in, 16)
            act.dma_start(temp_row, w["L0_ffn_temperature"].rearrange("a h b c -> a (h b c)")).then_inc(fold_in, 16)
            act.dma_start(bsl_row, w["L0_ffn_b_slice"].rearrange("(a g) -> a g", a=1)).then_inc(fold_in, 16)

            def ln_sqrt(k):
                wait(ln_var, k)
                nc.scalar.activation(ln_s[:, :], ln_r[:, :], ACT.Sqrt).then_inc(ln_std, 1)

            def bn_sqrt(k, n):
                wait(ln_var, k)
                nc.scalar.activation(bn_k[:, 1, 0:n], bn_k[:, 0, 0:n], ACT.Sqrt).then_inc(ln_std, 1)

            def products_done(l, b, fo, nfo):
                _, _, _, _, _, rps, rdone = ent[l]
                wait(rps, b * nfo + (fo + 2))
                k = 4 + 2 * (fo % 2)
                nc.scalar.activation(two(tfeat[:, fo, nodes(b)]), ps[:, k:k + 2, 0:HB],
                                     ACT.Identity, bias=vec[l][:, 0, fo:fo + 1]).then_inc(rdone, 1)

            ln_sqrt(1)
            wait(vec_in, 16 * 9)
            wait(zeroed, 16 * (NB + 1))
            wait(fold_dve, 5)
            rows, hi, lo, tps, tcopied, rps, rdone = ent[0]
            hh, _ = halves(F)
            with act.Fori(0, NB) as b:
                for i in range(BT):
                    wait(rows, b * BT + (i + 1))
                    nc.scalar.activation(hh[:, bass.ds(b * BT + i, 1), :], urow[:, i:i + 1, :], ACT.Copy, scale=LN_SCALE).then_inc(hi, 1)
                wait(tps, b + 2)
                wait(rps, b * 4 + 1)
                nc.scalar.activation(feat[:, 0:2, :], ps[:, 0:4, :].rearrange("p (f k) c -> p f (k c)", f=2)[:, :, 0:BC], ACT.Copy).then_inc(tcopied, 1)
                for fo in range(4):
                    products_done(0, b, fo, 4)
            with act.Fori(0, NB) as b:
                for q in range(NB):
                    store, s = astore[q % 2], q % 2
                    wait(ad_out[s], b * (16 * (3 - s)) + 16 * (q // 2 + 1))
                    for i in range(BT):
                        n = q * BT + i
                        wait(ad_ps, b * (NB * BT) + (n + 1))
                        nc.scalar.activation(store[:, i, :], ps16[:, 6 + n % 2, 0:BC], ACT.Copy).then_inc(ad_sb, 1)
                    wait(ad_sb, b * (NB * BT) + ((q + 1) * BT + 1))
                    act.dma_start(ad[:, q, bass.ds(b * (BT * BC), BT * BC)], store.rearrange("p i c -> p (i c)")).then_inc(ad_out[s], 16)
            bn_sqrt(2, 4)
            for l in (1, 2):
                rows, hi, lo, tps, tcopied, rps, rdone = ent[l]
                nfo = DIMS[l][1]
                hh, _ = halves(HID)
                wait(bn_done, l)
                if l == 1:
                    wait(sc_ready, 1)
                with act.Fori(0, NB) as b:
                    wait(tps, b * BT + 1)
                    wait(rps, b * nfo + 1)
                    for f in range(4):
                        nc.scalar.activation(feat[:, f, :], tfeat[:, f, nodes(b)], ACT.Relu,
                                             bias=bn_k[:, 3, f:f + 1], scale=bn_k[:, 0, f:f + 1]).then_inc(rows, 1)
                    for i in range(BT):
                        wait(tps, b * BT + (i + 2))
                        t = bass.ds(b * BT + i, 1)
                        if l == 1:
                            nc.scalar.activation(hh[:, t, :], ps[:, i % 4:i % 4 + 1, :], ACT.Copy, scale=sc[:, 0:1]).then_inc(hi, 1)
                        else:
                            nc.scalar.activation(stage_rows[:, t, :], ps[:, i % 4:i % 4 + 1, 0:F], ACT.Copy).then_inc(hi, 1)
                    for fo in range(nfo):
                        products_done(l, b, fo, nfo)
                if l == 2:
                    hh, _ = halves(F)
                    wait(sc_ready, 2)
                    with act.Fori(0, T) as t:
                        nc.scalar.activation(hh[:, bass.ds(t, 1), :], stage_rows[:, bass.ds(t, 1), :], ACT.Copy, scale=sc[:, 0:1]).then_inc(tcopied, 1)
                bn_sqrt(2 + l, nfo)
            rows, hi, lo, tps, tcopied, rps, rdone = ent[3]
            wait(bn_done, 3)
            with act.Fori(0, NB) as b:
                wait(tps, b * BT + 1)
                for f in range(2):
                    nc.scalar.activation(feat[:, f, :], tfeat[:, f, nodes(b)], ACT.Relu,
                                         bias=bn_k[:, 3, f:f + 1], scale=bn_k[:, 0, f:f + 1]).then_inc(rows, 1)
            act.sem_inc(f_tcp, 1)
            act.sem_inc(f_swc, 2)
            for k in range(2):
                act.sem_inc(conv[k][2], 1)
                act.sem_inc(conv[k][4], 1)
            for s in (r_tcp, e_tcp, e_gelu):
                act.sem_inc(s, 1)
            ln_sqrt(5)

            def transposed_copy(b, i, tps, tcp, bank, columns):
                wait(tps, b * BT + (BT + i + 1))
                nc.scalar.activation(columns, ps[:, bank, 0:F].rearrange("p (f c) -> p f c", f=2), ACT.Copy).then_inc(tcp, 1)

            with act.Fori(0, NB) as b:
                for i in range(BT + 2):
                    if i < BT:
                        wait(f_tps, b * BT + (i + 1))
                        nc.scalar.activation(feat[:, 0:2, i * P:(i + 1) * P], ps[:, 7, 0:F].rearrange("p (f c) -> p f c", f=2), ACT.Copy).then_inc(f_tcp, 1)
                    if 1 <= i <= BT:
                        wait(f_sub, b * BT + (i + 1))
                        nc.scalar.activation(logit[:, (i - 1) % 2, :], logit[:, (i - 1) % 2, :], ACT.Exp).then_inc(f_exp, 1)
                    if i >= 2:
                        wait(f_used, b * BT + (BT + i - 1))
                        nc.scalar.activation(tfeat[:, :, bass.ds(b * BC + (i - 2) * P, P)], ps[:, 2 + i % 2, :].rearrange("p (k c) -> p k c", k=4), ACT.Copy).then_inc(f_swc, 1)
            wait(f_dve, 6)
            nc.scalar.activation(att, att, ACT.Exp, scale=DH ** -0.5).then_inc(f_act, 1)
            wait(f_swc, T + 2)
            with act.Fori(0, NB) as b:
                for i in range(BT):
                    wait(f_rps, b * BT + (i + 1))
                    nc.scalar.activation(feat[:, :, i * P:(i + 1) * P], tfeat[:, :, bass.ds(b * BC + i * P, P)], ACT.Copy).then_inc(f_slot, 1)
            ln_sqrt(6)

            def conv_rows(k):
                _, tps, tcp, xps, stage, _ = conv[k]
                with act.Fori(0, NB) as b:
                    for i in range(BT + 1):
                        if i < BT:
                            transposed_copy(b, i, tps, tcp, i % 2, feat[:, 0:2, i * P:(i + 1) * P])
                        if i >= 1:
                            wait(xps, b * BT + i)
                            nc.scalar.activation(stage_rows[:, bass.ds(b * BT + i - 1, 1), :], ps[:, 2 + (i - 1) % 2, 0:F].unsqueeze(1), ACT.Copy).then_inc(stage, 1)

            for c in range(4):
                if c % 2 == 0:
                    conv_rows(c // 2)
                wait(sc_ready, 3 + c)
                if c == 0:
                    wait(c_ones, 1)
                else:
                    wait(chunk_used[NB - 1], FIRST[3] + c * NB + 1)
                with act.Fori(0, T) as t:
                    nc.scalar.activation(hh1[:, bass.ds(t, 1), 0:F], stage_rows[:, bass.ds(t, 1), :], ACT.Copy, scale=sc[:, 0:1]).then_inc(c_hi, 1)
            ln_sqrt(7)
            with act.Fori(0, NB) as b:
                for i in range(BT):
                    transposed_copy(b, i, r_tps, r_tcp, i % 2, feat[:, 0:2, i * P:(i + 1) * P])
            ln_sqrt(8)
            with act.Fori(0, NB) as b:
                for i in range(BT):
                    transposed_copy(b, i, e_tps, e_tcp, i % 2, xnT[:, :, bass.ds(b * BC + i * P, P)])
            wait(r_gap, 1)
            nc.scalar.activation(gate2, gate2, ACT.Exp).then_inc(r_exp, 1)
            wait(e_vec, 1)
            nc.scalar.activation(evec, ps[:, 6, 0:96], ACT.Copy).then_inc(e_vecT, 1)
            wait(e_vecT, 1)
            wait(e_tcp, T + 1)
            with act.Fori(0, EXPERTS // 2) as g:
                for s in range(2):
                    with act.Fori(0, NB) as b:
                        n = g * (2 * NB) + b + s * NB
                        for d in range(2):
                            col = g * 4 + (2 * s + d)
                            wait(e_hps, n * (EH // P) + 1)
                            nc.scalar.activation(feat[:, d, :], xnT[:, d, nodes(b)], ACT.Identity, scale=evec[:, bass.ds(col + 64, 1)],
                                                 bias=evec[:, bass.ds(col + 80, 1)]).then_inc(e_xe, 1)
                        for k in range(EH // P):
                            wait(e_hps, n * (EH // P) + (k + 2))
                            nc.scalar.activation(two(hT[:, k, :]), ps[:, 2 * (k % 2):2 * (k % 2) + 2, 0:HB], ACT.Gelu,
                                                 bias=evec[:, bass.ds(g * 16 + s * 8 + k, 1)]).then_inc(e_gelu, 1)

        @block.vector
        def _(dve):
            o = Order(dve, dve_order)
            V = nc.vector
            V.memset(zeros16, 0.0).then_inc(zero_ready, 1)
            for l in range(4):
                dve.sem_inc(ent[l][2], 1)
            for l in range(3):
                dve.sem_inc(agg[l][0], 1)
                dve.sem_inc(agg[l][2], 1)
                dve.sem_inc(agg[l][4], 1)

            def step(ins):
                o.mark(ins)
                o.settle()

            dve.wait_ge(edges_in, 16 * 6)
            step(V.tensor_scalar(eint[:, 2, :], eint[:, 0, :], 7, None, ALU.arith_shift_right))
            o.mark(V.tensor_copy(eflt[:, 0:3, :], eint[:, 0:3, :]))
            o.settle()
            step(V.tensor_scalar(eflt[:, 3, :], eflt[:, 1, :], float(BC), None, ALU.is_ge))
            for k in range(2, NB):
                step(V.scalar_tensor_tensor(out=eflt[:, 3, :], in0=eflt[:, 1, :], scalar=float(k * BC), in1=eflt[:, 3, :], op0=ALU.is_ge, op1=ALU.add))
            step(V.tensor_scalar(ekey, eflt[:, 0, :], float(AROW), None, ALU.mult))
            step(V.scalar_tensor_tensor(out=ekey, in0=eflt[:, 2, :], scalar=float(BC - P * AROW), in1=ekey, op0=ALU.mult, op1=ALU.add))
            step(V.scalar_tensor_tensor(out=ekey, in0=eflt[:, 3, :], scalar=float(P * AROW - BC), in1=ekey, op0=ALU.mult, op1=ALU.add))
            V.tensor_tensor(ekey, ekey, eflt[:, 1, :], ALU.add).then_inc(key_ready, 1)
            dve.wait_ge(key_ready, 1)
            dve.wait_ge(consts_ready, 1)
            step(V.tensor_copy(etrash, etrash_i))
            o.mark(V.tensor_tensor(espare.rearrange("p (g q) -> p g q", q=GQ), etrash.unsqueeze(1).to_broadcast([P, NG, GQ]),
                                   ekey.rearrange("p (g q) -> p g q", q=GQ), ALU.subtract))
            dve.wait_ge(keyT_psum, 1)
            V.tensor_copy(keyT, ps[0:EC // GQ, 0, :]).then_inc(keyT_ready, 1)
            dve.wait_ge(fold_in, 16 * 5)
            step(V.tensor_scalar(temp_row, temp_row, 0.1, 5.0, ALU.max, ALU.min))
            V.reciprocal(rtemp[0:1, :], temp_row).then_inc(fold_dve, 1)
            dve.wait_ge(fold_pe, 1)
            V.tensor_copy(wxT.rearrange("p h d -> p (h d)"), ps[0:DH, 1:5, :].rearrange("p k c -> p (k c)")).then_inc(fold_dve, 1)
            dve.wait_ge(fold_pe, 2)
            V.tensor_copy(rtemp, ps[:, 7, 0:HEADS]).then_inc(fold_dve, 1)
            dve.wait_ge(fold_pe, 3)
            dve.wait_ge(fold_dve, 3)
            o.mark(V.tensor_tensor(bias_raw.rearrange("p (h g) -> p h g", h=HEADS), ps[0:1, 7, :].rearrange("p (h g) -> p h g", h=HEADS),
                                   bsl_row.unsqueeze(1).to_broadcast([1, HEADS, G]), ALU.add))
            for d in range(2):
                V.tensor_tensor(wxs[:, d, :].rearrange("p (h g) -> p h g", h=HEADS), ps[:, 5 + d, :].rearrange("p (h g) -> p h g", h=HEADS),
                                rtemp.unsqueeze(2).to_broadcast([P, HEADS, G]), ALU.mult).then_inc(fold_dve, 1)
            o.settle()
            o.mark(V.tensor_tensor(slice_bias[:, :].rearrange("p (h g) -> p h g", h=HEADS), bias_raw.rearrange("p (h g) -> p h g", h=HEADS),
                                   rtemp[0:1, :].unsqueeze(2).to_broadcast([1, HEADS, G]), ALU.mult))

            def layernorm_stats(k, rows=xrows):
                with o.loop(T, 1) as t:
                    o.mark(V.bn_stats(ln_st[:, bass.ds(t, 1), :].rearrange("p o s -> p (o s)"), rows[:, bass.ds(t, 1), :].rearrange("p o c -> p (o c)")))
                o.settle()
                st = [ln_st[:, :, j] for j in range(6)]
                mean, var = ln_mv[:, :, 0], ln_mv[:, :, 1]
                o.mark(V.tensor_tensor(mean, st[1], st[4], ALU.add))
                o.mark(V.tensor_tensor(ln_r[:, :], st[1], st[4], ALU.subtract))
                o.mark(V.tensor_tensor(var, st[2], st[5], ALU.add))
                o.settle()
                o.mark(V.tensor_scalar(mean, mean, 0.5, None, ALU.mult))
                step(V.scalar_tensor_tensor(out=ln_s[:, :], in0=ln_r[:, :], scalar=0.25, in1=ln_r[:, :], op0=ALU.mult, op1=ALU.mult))
                step(V.scalar_tensor_tensor(out=var, in0=var, scalar=1.0 / F, in1=ln_s[:, :], op0=ALU.mult, op1=ALU.add))
                V.tensor_scalar(ln_r[:, :], var, EPS, None, ALU.add).then_inc(ln_var, 1)
                dve.wait_ge(ln_std, k)
                step(V.reciprocal(ln_r[:, :], ln_s[:, :]))

            def normalized(dst_ap, t, rows=xrows):
                return V.tensor_scalar(dst_ap, rows[:, bass.ds(t, 1), :].rearrange("p o c -> p (o c)"), ln_mv[:, bass.ds(t, 1), 0], ln_r[:, bass.ds(t, 1)],
                                       ALU.subtract, ALU.mult)

            def half_scale(k, cols):
                V.tensor_reduce(sc[:, 2:3], amax[:, 0:cols], AX.X, ALU.max).then_inc(sc_col, 1)
                dve.wait_ge(sc_row, k)
                step(V.tensor_reduce(sc1[:, 0:1], ps[0:1, 7, 0:P], AX.X, ALU.max))
                step(V.tensor_scalar(sc1[:, 1:2], sc1[:, 0:1], 1e-30, None, ALU.max))
                V.tensor_scalar(sc1[:, 2:3].bitcast(i32), sc1[:, 1:2].bitcast(i32), 0x7F800000, None, ALU.bitwise_and).then_inc(sc_pow, 1)
                dve.wait_ge(sc_all, k)
                step(V.tensor_scalar(sc[:, 1:2], ps[:, 7, P:P + 1], 2.0 ** -13, None, ALU.mult))
                V.reciprocal(sc[:, 0:1], sc[:, 1:2]).then_inc(sc_ready, 1)

            def edges_of(i, first):
                for s in range(LOOK):
                    dve.wait_ge(krow_in[s], 16 * (i + 1) if first else i * 16 + 16)
                    if not first:
                        dve.wait_ge(scattered, i * (LOOK * GQ * 16) + (s + 1 - LOOK) * (GQ * 16))
                    g = i * LOOK + s
                    for q in range(GQ):
                        key1 = ekey[:, g * GQ + q:g * GQ + q + 1] if first else ekey[:, bass.ds(i * (LOOK * GQ) + s * GQ + q, 1)]
                        ins = V.scalar_tensor_tensor(out=ejunk[:, q, :], in0=krow[:, s, :], scalar=key1, in1=eweight[:, q, :],
                                                     op0=ALU.is_equal, op1=ALU.mult, accum_out=ecount[:, s, q:q + 1])
                    ins.then_inc(compared, 1)
                    four = slice(g * GQ, g * GQ + GQ) if first else bass.ds(i * (LOOK * GQ) + s * GQ, GQ)
                    dve.wait_ge(compared, (s + 1) if first else i * LOOK + (s + 1))
                    step(V.scalar_tensor_tensor(out=eshift[:, s, :], in0=ecount[:, s, :], scalar=1024.0, in1=espare[:, four], op0=ALU.is_ge, op1=ALU.mult))
                    o.mark(V.tensor_scalar(evalue[:, s, :], ecount[:, s, :], 1024.0, None, ALU.min))
                    V.tensor_tensor(eidx[:, s, :], eshift[:, s, :], ekey[:, four], ALU.add).then_inc(idx_ready, 1)

            dve.wait_ge(x_in, 32)
            layernorm_stats(1)
            o.settle()
            edges_of(0, True)
            with o.loop_from(1, NG // LOOK, 2 * LOOK) as i:
                edges_of(i, False)

            rows, hi, lo, tps, tcopied, rps, rdone = ent[0]
            hh, hl = halves(F)
            with dve.Fori(0, NB) as b:
                dve.wait_ge(tps, b + 1)
                dve.wait_ge(hi, b * BT + 1)
                dve.wait_ge(lo, b * BT + 1)
                for i in range(BT):
                    normalized(urow[:, i, :], b * BT + i).then_inc(rows, 1)
                for i in range(BT):
                    dve.wait_ge(hi, b * BT + (i + 2))
                    t = bass.ds(b * BT + i, 1)
                    V.scalar_tensor_tensor(out=hl[:, t, :], in0=urow[:, i:i + 1, :], scalar=LN_SCALE, in1=hh[:, t, :],
                                           op0=ALU.mult, op1=ALU.subtract).then_inc(lo, 1)

            for l in range(3):
                nfi, nfo = DIMS[l]
                np_ = PASSES[l]
                mean, ops, odone, deg, degdone = agg[l]
                rdone = ent[l][6]
                dve.wait_ge(rdone, NB * nfo + 1)
                inv = 1.0 / LN_SCALE if l == 0 else sc[:, 1:2]

                def aggregated(b, width):
                    if l == 0:
                        dve.wait_ge(deg, b + 1)
                        d2 = two(deginv[:, nodes(b)])
                        step(V.tensor_scalar(d2, ps[:, 4:6, 0:HB], 1.0, None, ALU.max))
                        dve.nop(nofuse=True)
                        V.reciprocal(deginv[:, nodes(b)], deginv[:, nodes(b)]).then_inc(degdone, 1)
                        dve.wait_ge(degdone, b + 2)
                    if l < 2:
                        dve.wait_ge(ops, b * nfo + 1)
                    for k in range(np_):
                        dve.wait_ge(chunk_used[NB - 1], b * np_ + (FIRST[l] + k + 2))
                        for j in range(2):
                            V.scalar_tensor_tensor(out=two(feat[:, 2 * k + j, :]), in0=ps[:, 2 * j:2 * j + 2, 0:HB], scalar=inv,
                                                   in1=two(deginv[:, nodes(b)]), op0=ALU.mult, op1=ALU.mult).then_inc(mean, 1)
                    for fo in range(nfo):
                        if l < 2:
                            dve.wait_ge(ops, b * nfo + (fo + 2))
                            k = 4 + 2 * (fo % 2)
                            V.tensor_tensor(two(tfeat[:, fo, nodes(b)]), ps[:, k:k + 2, 0:HB], two(tfeat[:, fo, nodes(b)]), ALU.add).then_inc(odone, 1)
                        else:
                            dve.wait_ge(mean, b * 2 + (fo + 2))
                            V.tensor_tensor(tfeat[:, fo, nodes(b)], feat[:, fo, :], tfeat[:, fo, nodes(b)], ALU.add).then_inc(odone, 1)
                    for fo in range(nfo):
                        dve.wait_ge(odone, b * nfo + (fo + 2))
                        for h in range(2):
                            c = HB if h == 0 else width
                            o.mark(V.bn_stats(bn_st[:, fo, bass.ds(b * 2 + h, 1), :].rearrange("p a s -> p (a s)"),
                                              tfeat[:, fo, bass.ds(b * BC + h * HB, c)]))

                with o.loop(NB - 1, 2 * nfo + (1 if l == 0 else 0)) as b:
                    aggregated(b, HB)
                aggregated(NB - 1, N - (NB - 1) * BC - HB)
                o.settle()
                for fo in range(nfo):
                    o.mark(V.bn_aggr(bn_mv[:, fo, :], bn_st[:, fo, :, :].rearrange("p a s -> p (a s)")))
                o.settle()
                V.tensor_scalar(bn_k[:, 0, 0:nfo], bn_mv[:, 0:nfo, 1], EPS, None, ALU.add).then_inc(ln_var, 1)
                dve.wait_ge(ln_std, 2 + l)
                step(V.reciprocal(bn_k[:, 2, 0:nfo], bn_k[:, 1, 0:nfo]))
                step(V.tensor_tensor(bn_k[:, 0, 0:nfo], bn_k[:, 2, 0:nfo], vec[l][:, 1, 0:nfo], ALU.mult))
                step(V.tensor_tensor(bn_k[:, 1, 0:nfo], bn_mv[:, 0:nfo, 0], bn_k[:, 0, 0:nfo], ALU.mult))
                V.tensor_tensor(bn_k[:, 3, 0:nfo], vec[l][:, 2, 0:nfo], bn_k[:, 1, 0:nfo], ALU.subtract).then_inc(bn_done, 1)
                if l == 0:
                    o.mark(V.scalar_tensor_tensor(out=amax[:, 0:4], in0=vec[0][:, 1, :], scalar=-1.0, in1=vec[0][:, 1, :], op0=ALU.mult, op1=ALU.max))
                    o.mark(V.scalar_tensor_tensor(out=amax[:, 4:8], in0=vec[0][:, 2, :], scalar=-1.0, in1=vec[0][:, 2, :], op0=ALU.mult, op1=ALU.max))
                    o.settle()
                    step(V.scalar_tensor_tensor(out=amax[:, 0:4], in0=amax[:, 0:4], scalar=BN_BOUND, in1=amax[:, 4:8], op0=ALU.mult, op1=ALU.add))
                    half_scale(1, 4)
                    rows, hi, lo, tps, tcopied, rps, rdone = ent[1]
                    hh, hl = halves(HID)
                    dve.wait_ge(sc_ready, 1)
                    for k, n in ((0, 3), (1, 2)):
                        dve.wait_ge(ad_out[k], 16 * (n * NB + 1))
                    with dve.Fori(0, NB) as b:
                        for i in range(BT):
                            dve.wait_ge(hi, b * BT + (i + 2))
                            t = bass.ds(b * BT + i, 1)
                            V.scalar_tensor_tensor(out=hl[:, t, :], in0=ps[:, i % 4:i % 4 + 1, :], scalar=sc[:, 0:1], in1=hh[:, t, :],
                                                   op0=ALU.mult, op1=ALU.subtract).then_inc(lo, 1)
                elif l == 1:
                    rows, hi, lo, tps, tcopied, rps, rdone = ent[2]
                    with dve.Fori(0, NB) as b:
                        for i in range(BT):
                            dve.wait_ge(hi, b * BT + (i + 2))
                            V.tensor_reduce(amax[:, bass.ds(b * BT + i, 1)], ps[:, i % 4, 0:F], AX.X, ALU.max,
                                            apply_absolute_value=True).then_inc(lo, 1)
                    dve.wait_ge(lo, T + 1)
                    half_scale(2, T)
                    hh, hl = halves(F)
                    dve.wait_ge(sc_ready, 2)
                    with dve.Fori(0, T) as t:
                        dve.wait_ge(tcopied, t + 2)
                        V.scalar_tensor_tensor(out=hl[:, bass.ds(t, 1), :], in0=stage_rows[:, bass.ds(t, 1), :], scalar=sc[:, 0:1],
                                               in1=hh[:, bass.ds(t, 1), :], op0=ALU.mult, op1=ALU.subtract).then_inc(lo, 1)
                else:
                    rows, hi, lo, tps, tcopied, rps, rdone = ent[3]
                    with dve.Fori(0, NB) as b:
                        for i in range(BT):
                            dve.wait_ge(tps, b * BT + (i + 2))
                            t = bass.ds(b * BT + i, 1)
                            V.tensor_tensor(xrows[:, t, :], ps[:, i % 4:i % 4 + 1, 0:F], xrows[:, t, :], ALU.add).then_inc(lo, 1)
            H8 = "p (h g) -> p h g"
            dve.sem_inc(f_sub, 1)
            dve.sem_inc(f_x, 1)
            dve.sem_inc(c_read, 1)
            dve.sem_inc(r_lgc, 1)
            dve.sem_inc(e_x, 1)
            dve.wait_ge(ent[3][2], T + 1)
            dve.wait_ge(chunk_used[NB - 1], FIRST[3] + 1)
            V.memset(zero_row, 0.0).then_inc(f_zero, 1)
            layernorm_stats(5)

            def f_shift(b, i):
                s = i % 2
                dve.wait_ge(f_lg, b * BT + (i + 1))
                step(V.tensor_reduce(hmax[:, s, :], ps[:, s, :].rearrange(H8, h=HEADS), AX.X, ALU.max))
                V.tensor_tensor(logit[:, s, :].rearrange(H8, h=HEADS), ps[:, s, :].rearrange(H8, h=HEADS),
                                hmax[:, s, :].unsqueeze(2).to_broadcast([P, HEADS, G]), ALU.subtract).then_inc(f_sub, 1)

            def f_softmax(b, i):
                s = i % 2
                dve.wait_ge(f_exp, b * BT + (i + 1))
                step(V.tensor_reduce(hsum[:, s, :], logit[:, s, :].rearrange(H8, h=HEADS), AX.X, ALU.add))
                step(V.reciprocal(hrec[:, s, :], hsum[:, s, :]))
                dve.wait_ge(f_used, b * BT + (BT + max(i - 1, 0)))
                V.scalar_tensor_tensor(out=sweight[:, s, :].rearrange(H8, h=HEADS), in0=logit[:, s, :].rearrange(H8, h=HEADS),
                                       scalar=rowmask[:, bass.ds(b * BT + i, 1)], in1=hrec[:, s, :].unsqueeze(2).to_broadcast([P, HEADS, G]),
                                       op0=ALU.mult, op1=ALU.mult).then_inc(f_sw, 1)

            with o.loop(NB, 3 * BT) as b:
                for i in range(BT + 2):
                    if i < BT:
                        dve.wait_ge(f_used, b * BT + (i + 1))
                        normalized(urow[:, i, :], b * BT + i).then_inc(f_rows, 1)
                    if 1 <= i <= BT:
                        f_shift(b, i - 1)
                    if i >= 2:
                        f_softmax(b, i - 2)
            dve.wait_ge(f_pe, 1)
            o.mark(V.tensor_copy(tokT, ps[:, 4:6, :]))
            o.mark(V.tensor_copy(norm, ps[0:DH, 6, :]))
            step(V.tensor_scalar(rnorm, ps[0:DH, 6, :], 1e-5, None, ALU.add))
            V.reciprocal(rnorm, rnorm).then_inc(f_dve, 1)
            dve.wait_ge(f_pe, 2)
            dve.wait_ge(f_dve, 1)
            V.tensor_tensor(slT, ps[0:DH, 0, :], rnorm, ALU.mult).then_inc(f_dve, 1)
            dve.wait_ge(f_pe, 3)
            for k, part in enumerate((qT, kT, vS)):
                V.tensor_copy(part, ps[0:DH, 1 + k, :]).then_inc(f_dve, 1)
            dve.wait_ge(f_pe, 4)
            lg4 = ps[0:DH, 0, :].rearrange(H8, h=HEADS)
            a4 = att.rearrange(H8, h=HEADS)
            step(V.tensor_reduce(hmax[0:DH, 0, :], lg4, AX.X, ALU.max))
            V.tensor_tensor(a4, lg4, hmax[0:DH, 0, :].unsqueeze(2).to_broadcast([DH, HEADS, G]), ALU.subtract).then_inc(f_dve, 1)
            dve.wait_ge(f_act, 1)
            step(V.tensor_reduce(hsum[0:DH, 0, :], a4, AX.X, ALU.add))
            step(V.reciprocal(hrec[0:DH, 0, :], hsum[0:DH, 0, :]))
            V.tensor_tensor(a4, a4, hrec[0:DH, 0, :].unsqueeze(2).to_broadcast([DH, HEADS, G]), ALU.mult).then_inc(f_dve, 1)
            dve.wait_ge(f_pe, 5)
            V.tensor_copy(attT, ps[0:DH, 1, :]).then_inc(f_dve, 1)
            dve.wait_ge(f_pe, 6)
            V.tensor_copy(outT, ps[0:DH, 2, :]).then_inc(f_dve, 1)
            dve.wait_ge(f_pe, 7)
            for k in range(2):
                half = slice(k * DH, (k + 1) * DH)
                V.tensor_copy(pmat[half, :, :].rearrange("p k o -> p (k o)"), ps[half, 3 + 2 * k:5 + 2 * k, :].rearrange("p k c -> p (k c)")).then_inc(f_dve, 1)
            dve.wait_ge(f_bias, 1)
            with dve.Fori(0, NB) as b:
                for i in range(BT):
                    dve.wait_ge(f_rps, b * BT + (BT + i + 1))
                    t = bass.ds(b * BT + i, 1)
                    V.tensor_tensor(xrows[:, t, :], ps[:, i % 4:i % 4 + 1, 0:F], xrows[:, t, :], ALU.add).then_inc(f_x, 1)

            dve.wait_ge(f_x, T + 1)
            layernorm_stats(6)
            V.memset(hh1[:, :, F:F + 2], 1.0).then_inc(c_ones, 1)

            def conv_largest(k, b, i):
                dve.wait_ge(conv[k][4], b * BT + (i + 2))
                V.tensor_reduce(amax[:, bass.ds(b * BT + i, 1)], stage_rows[:, bass.ds(b * BT + i, 1), :].rearrange("p o c -> p (o c)"), AX.X, ALU.max,
                                apply_absolute_value=True).then_inc(conv[k][5], 1)

            with dve.Fori(0, NB) as b:
                for i in range(BT + 2):
                    if i < BT:
                        dve.wait_ge(conv[0][1], b * BT + (i + 1))
                        normalized(urow[:, i, :], b * BT + i).then_inc(conv[0][0], 1)
                    if i >= 2:
                        conv_largest(0, b, i - 2)
            dve.wait_ge(conv_w, 16 * 5)
            for c in range(4):
                if c == 2:
                    with dve.Fori(0, NB) as b:
                        for i in range(BT):
                            conv_largest(1, b, i)
                if c % 2 == 0:
                    dve.wait_ge(conv[c // 2][5], T)
                else:
                    dve.wait_ge(c_max, NB * (c // 2 + 1))
                half_scale(3 + c, T)
                dve.wait_ge(sc_ready, 3 + c)
                with dve.Fori(0, T) as t:
                    dve.wait_ge(c_hi, t + (c * T + 1))
                    V.scalar_tensor_tensor(out=hl1[:, bass.ds(t, 1), :], in0=stage_rows[:, bass.ds(t, 1), :], scalar=sc[:, 0:1],
                                           in1=hh1[:, bass.ds(t, 1), 0:F], op0=ALU.mult, op1=ALU.subtract).then_inc(c_lo, 1)
                with o.loop(NB, {0: 6, 1: 8, 2: 6, 3: 15}[c]) as b:
                    blk = bass.ds(b * BT, BT)
                    dve.wait_ge(chunk_used[NB - 1], b + (FIRST[3] + c * NB + 2))
                    step(V.tensor_scalar(rdeg, ps[:, 0:BT, F], 1.0, None, ALU.max))
                    step(V.reciprocal(rdeg, rdeg))
                    if c % 2 == 0:
                        for i in range(BT):
                            ins = V.tensor_scalar(stage_rows[:, bass.ds(b * BT + i, 1), :].rearrange("p o c -> p (o c)"), ps[:, i, 0:F],
                                                  rdeg[:, i:i + 1], sc[:, 1:2], ALU.mult, ALU.mult)
                            if i < BT - 1:
                                o.mark(ins)
                        ins.then_inc(c_read, 1)
                        dve.wait_ge(c_read, b + (c * NB + 2))
                        V.tensor_reduce(amax[:, blk], stage_rows[:, blk, :], AX.X, ALU.max, apply_absolute_value=True).then_inc(c_max, 1)
                    else:
                        step(V.tensor_scalar(rdeg, rdeg, sc[:, 1:2], None, ALU.mult))
                        for i in range(BT):
                            ins = V.scalar_tensor_tensor(out=zrows[:, i, :], in0=ps[:, i, 0:F], scalar=rdeg[:, i:i + 1], in1=bconv[c // 2],
                                                         op0=ALU.mult, op1=ALU.add)
                            if i < BT - 1:
                                o.mark(ins)
                        ins.then_inc(c_read, 1)
                        dve.wait_ge(c_read, b + (c * NB + 2))
                        if c == 3:
                            for i in range(BT):
                                o.mark(normalized(urows[:, i, :], b * BT + i))
                            o.settle()
                            step(V.tensor_tensor(zrows, zrows, urows, ALU.add))
                        step(V.tensor_scalar(negrows, zrows, 0.0, slope, ALU.min, ALU.mult))
                        if c == 1:
                            V.scalar_tensor_tensor(out=rows2[:, blk, :], in0=zrows, scalar=0.0, in1=negrows, op0=ALU.max, op1=ALU.add).then_inc(c_h, 1)
                        else:
                            step(V.scalar_tensor_tensor(out=zrows, in0=zrows, scalar=0.0, in1=negrows, op0=ALU.max, op1=ALU.add))
                            V.tensor_tensor(xrows[:, blk, :], xrows[:, blk, :], zrows, ALU.add).then_inc(c_x, 1)

            dve.wait_ge(c_x, NB)
            layernorm_stats(7)
            with o.loop(NB, BT) as b:
                for i in range(BT + 2):
                    if i < BT:
                        dve.wait_ge(r_tps, b * BT + (i + 1))
                        normalized(urow[:, i, :], b * BT + i).then_inc(r_rows, 1)
                        o.mark(normalized(rows2[:, bass.ds(b * BT + i, 1), :].rearrange("p o c -> p (o c)"), b * BT + i))
                    if i >= 2:
                        dve.wait_ge(r_lg, b * BT + (i - 1))
                        V.tensor_copy(lgt[:, bass.ds(b * BT + i - 2, 1), :].rearrange("p o e -> p (o e)"), ps[:, 2 + i % 2, 0:EXPERTS]).then_inc(r_lgc, 1)
            o.settle()
            layernorm_stats(8, rows2)
            with dve.Fori(0, NB) as b:
                for i in range(BT):
                    dve.wait_ge(e_tps, b * BT + (i + 1))
                    normalized(urow[:, i, :], b * BT + i, rows2).then_inc(e_rows, 1)
            dve.wait_ge(r_lgc, T + 1)
            for e in range(EXPERTS):
                o.mark(V.memset(rank[:, e:e + 1], float(EXPERTS - e)))

            def each(ap):
                return ap.unsqueeze(2).to_broadcast([P, T, EXPERTS])

            for top, sel in ((top1, sel1), (top2, sel2)):
                step(V.tensor_reduce(top, lgt, AX.X, ALU.max))
                step(V.tensor_tensor(pri, lgt, each(top), ALU.is_equal))
                step(V.tensor_tensor(pri, pri, rank.unsqueeze(1).to_broadcast([P, T, EXPERTS]), ALU.mult))
                step(V.tensor_reduce(first, pri, AX.X, ALU.max))
                step(V.tensor_tensor(sel, pri, each(first), ALU.is_equal))
                if sel is sel1:
                    step(V.scalar_tensor_tensor(out=lgt, in0=sel, scalar=-3e38, in1=lgt, op0=ALU.mult, op1=ALU.add))
            V.tensor_tensor(gate2, top2, top1, ALU.subtract).then_inc(r_gap, 1)
            dve.wait_ge(r_exp, 1)
            step(V.tensor_scalar(gate1, gate2, 1.0, None, ALU.add))
            step(V.reciprocal(gate1, gate1))
            step(V.tensor_tensor(gate2, gate2, gate1, ALU.mult))
            o.mark(V.tensor_tensor(sel1, sel1, each(gate1), ALU.mult))
            step(V.tensor_tensor(sel2, sel2, each(gate2), ALU.mult))
            step(V.tensor_tensor(wgt, sel1, sel2, ALU.add))
            wflat = wgt.rearrange("p t e -> p (t e)")
            with dve.Fori(0, EXPERTS // 2) as g:
                for s in range(2):
                    with dve.Fori(0, NB) as b:
                        for i in range(BT):
                            n = g * (2 * T) + b * BT + (s * T + i)
                            dve.wait_ge(e_yps, n + (2 * T + 1))
                            dve.wait_ge(e_x, n + 1)
                            t = bass.ds(b * BT + i, 1)
                            V.scalar_tensor_tensor(out=xrows[:, t, :], in0=ps[:, 4 + i % 4:5 + i % 4, 0:F],
                                                   scalar=wflat[:, bass.ds(b * (BT * EXPERTS) + g * 2 + (i * EXPERTS + s), 1)],
                                                   in1=xrows[:, t, :], op0=ALU.mult, op1=ALU.add).then_inc(e_x, 1)

        @block.tensor
        def _(pe):
            M = nc.tensor.matmul
            for l in range(4):
                pe.sem_inc(ent[l][3], 1)
                pe.sem_inc(ent[l][5], 1)
            for l in range(3):
                pe.sem_inc(agg[l][1], 1)

            pe.wait_ge(consts_ready, 1)
            pe.wait_ge(key_ready, 1)
            for q in range(GQ):
                ins = nc.tensor.transpose(ps[0:NG, 0, q * P:(q + 1) * P], ekey[:, q * NG:(q + 1) * NG], ident[:, :])
            ins.then_inc(keyT_psum, 1)
            pe.wait_ge(fold_in, 16 * 5)
            for h in range(HEADS):
                for d in range(2):
                    n = 2 * h + d
                    ins = nc.tensor.transpose(ps[0:DH, 1 + n // 4, (n % 4) * P:(n % 4 + 1) * P], wx_in[:, d, h * DH:(h + 1) * DH], ident[:, :])
            ins.then_inc(fold_pe, 1)
            pe.wait_ge(fold_dve, 1)
            M(ps[:, 7, 0:HEADS], ones[0:1, :], rtemp[0:1, :], start=True, stop=True).then_inc(fold_pe, 1)
            pe.wait_ge(fold_dve, 3)
            for d in range(2):
                for h in range(HEADS):
                    M(ps[:, 5 + d, h * G:(h + 1) * G], wxT[:, h, d * P:(d + 1) * P], wsl, start=True, stop=True)
            for h in range(HEADS):
                ins = M(ps[0:1, 7, h * G:(h + 1) * G], bxT[:, h:h + 1], wsl, start=True, stop=True)
            ins.then_inc(fold_pe, 1)

            def products(l, b, nfi, nfo, weights):
                _, _, _, _, _, rps, rdone = ent[l]
                for fo in range(nfo):
                    k = 4 + 2 * (fo % 2)
                    pe.wait_ge(rdone, b * nfo + (fo if fo >= 2 else 1))
                    for h in range(2):
                        for d in range(nfi):
                            ins = M(ps[:, k + h, 0:HB], weights[:, d, fo * P:(fo + 1) * P], feat[:, d, h * HB:(h + 1) * HB],
                                    start=(d == 0), stop=(d == nfi - 1))
                    ins.then_inc(rps, 1)

            rows, hi, lo, tps, tcopied, rps, rdone = ent[0]
            pe.wait_ge(wr_in, 16)
            pe.wait_ge(fold_dve, 5)
            with pe.Fori(0, NB) as b:
                pe.wait_ge(rows, b * BT + BT)
                pe.wait_ge(tcopied, b + 1)
                for i in range(BT):
                    for f in range(2):
                        c = i * P
                        ins = nc.tensor.transpose(ps[:, 2 * f + c // 512, c % 512:c % 512 + P], urow[:, i, f * P:(f + 1) * P], ident[:, :])
                ins.then_inc(tps, 1)
                pe.wait_ge(tcopied, b + 2)
                products(0, b, 2, 4, wr2)

            def aggregate(l, b, k, width, at_rows=None):
                n = b * PASSES[l] + (FIRST[l] + k)
                hh, hl = halves(width)
                pe.wait_ge(agg[l][0], b * (2 * PASSES[l]) + (2 * k + 1))
                if l == 0:
                    pe.wait_ge(agg[0][2], b * 4 + 1)
                for q in range(NB):
                    pe.wait_ge(chunk_in[q], n * 16 + 16)
                    if l == 0:
                        for i in range(BT):
                            m = q * BT + i
                            pe.wait_ge(ad_sb, b * (NB * BT) + (m if m >= 2 else 1))
                            for s in range(BT):
                                ins = nc.tensor.transpose(ps16[:, 6 + m % 2, s * P:(s + 1) * P], chunk[q][:, s, i * P:(i + 1) * P], ident16[:, :])
                            ins.then_inc(ad_ps, 1)
                        if q == 0:
                            pe.wait_ge(agg[0][4], b + 1)
                        for s in range(BT):
                            for h in range(2):
                                ins = M(ps[:, 4 + h, 0:HB], ones16[:, :], chunk[q][:, s, h * HB:(h + 1) * HB],
                                        start=(q == 0 and s == 0), stop=(q == NB - 1 and s == BT - 1))
                        if q == NB - 1:
                            ins.then_inc(agg[0][3], 1)
                    for s in range(BT):
                        t = q * BT + s
                        for f in range(2):
                            for part in (hh, hl):
                                for h in range(2):
                                    ins = M(ps[:, 2 * f + h, 0:HB], part[:, t, (2 * k + f) * P:(2 * k + f + 1) * P], chunk[q][:, s, h * HB:(h + 1) * HB],
                                            start=(t == 0 and part is hh), stop=(t == T - 1 and part is hl))
                    ins.then_inc(chunk_used[q], 1)

            def mean_products(l, b, nfi, nfo):
                mean, ops, odone, _, degdone = agg[l]
                pe.wait_ge(mean, (b + 1) * (2 * PASSES[l]) + 1)
                if l == 0:
                    pe.wait_ge(degdone, b + 2)
                    pe.wait_ge(ad_sb, (b + 1) * (NB * BT) + 1)
                for fo in range(nfo):
                    pe.wait_ge(odone, b * nfo + (fo if fo >= 2 else 1))
                    k = 4 + 2 * (fo % 2)
                    for h in range(2):
                        for d in range(nfi):
                            ins = M(ps[:, k + h, 0:HB], wl2[:, d, fo * P:(fo + 1) * P], feat[:, d, h * HB:(h + 1) * HB],
                                    start=(d == 0), stop=(d == nfi - 1))
                    ins.then_inc(ops, 1)

            def half_scale(k):
                pe.wait_ge(sc_col, k)
                M(ps[0:1, 7, 0:P], sc[:, 2:3], ident[:, :], start=True, stop=True).then_inc(sc_row, 1)
                pe.wait_ge(sc_pow, k)
                M(ps[:, 7, P:P + 1], ones[0:1, :], sc1[:, 2:3], start=True, stop=True).then_inc(sc_all, 1)

            pe.wait_ge(ent[0][1], T + 1)
            pe.wait_ge(ent[0][2], T + 1)
            pe.wait_ge(ent[0][6], NB * 4 + 1)
            pe.wait_ge(wl_in, 16)
            with pe.Fori(0, NB) as b:
                aggregate(0, b, 0, F)
                mean_products(0, b, 2, 4)

            pe.wait_ge(agg[0][2], NB * 4 + 1)
            half_scale(1)
            rows, hi, lo, tps, tcopied, rps, rdone = ent[1]
            pe.wait_ge(wr1_in, 16)
            pe.wait_ge(sc_ready, 1)
            with pe.Fori(0, NB) as b:
                pe.wait_ge(rows, b * 4 + 4)
                for i in range(BT):
                    pe.wait_ge(lo, b * BT + (2 if i == 4 else 1))
                    for f in range(4):
                        ins = nc.tensor.transpose(ps[:, i % 4, f * P:(f + 1) * P], feat[:, f, i * P:(i + 1) * P], ident[:, :])
                    ins.then_inc(tps, 1)
                products(1, b, 4, 4, wr2)
            pe.wait_ge(lo, T + 1)
            pe.wait_ge(rdone, NB * 4 + 1)
            pe.wait_ge(wl1_in, 16)
            with pe.Fori(0, NB) as b:
                aggregate(1, b, 0, HID)
                aggregate(1, b, 1, HID)
                mean_products(1, b, 4, 4)
            rows, hi, lo, tps, tcopied, rps, rdone = ent[2]
            pe.wait_ge(w2_in, 32)
            pe.wait_ge(agg[1][2], NB * 4 + 1)
            with pe.Fori(0, NB) as b:
                pe.wait_ge(rows, b * 4 + 4)
                for i in range(BT):
                    pe.wait_ge(lo, b * BT + (2 if i == 4 else 1))
                    for d in range(4):
                        ins = M(ps[:, i % 4, 0:F], feat[:, d, i * P:(i + 1) * P], wl3[:, d, :], start=(d == 0), stop=(d == 3))
                    ins.then_inc(tps, 1)
                products(2, b, 4, 2, wr3)
            pe.wait_ge(rdone, NB * 2 + 1)
            half_scale(2)
            pe.wait_ge(lo, 2 * T + 1)
            with pe.Fori(0, NB) as b:
                aggregate(2, b, 0, F)
            rows, hi, lo, tps, tcopied, rps, rdone = ent[3]
            pe.wait_ge(agg[2][0], NB * 2 + 1)
            with pe.Fori(0, NB) as b:
                pe.wait_ge(rows, b * 2 + 2)
                for i in range(BT):
                    pe.wait_ge(lo, b * BT + (2 if i == 4 else 1))
                    for f in range(2):
                        ins = nc.tensor.transpose(ps[:, i % 4, f * P:(f + 1) * P], feat[:, f, i * P:(i + 1) * P], ident[:, :])
                    ins.then_inc(tps, 1)

            pe.sem_inc(f_used, BT)
            pe.sem_inc(f_rps, BT)
            for k in range(2):
                pe.sem_inc(conv[k][1], BT)
            for s in (r_tps, e_tps):
                pe.sem_inc(s, BT)
            pe.sem_inc(e_hps, 1)
            pe.sem_inc(e_yps, 2 * T)
            pe.wait_ge(f_zero, 1)
            pe.wait_ge(lo, T + 1)
            for k in range(2):
                M(ps[:, 4 + k, :], zero_row[:, 0:P], zero_row, start=True, stop=False)
            M(ps[0:DH, 6, :], zero_row[:, 0:DH], zero_row, start=True, stop=False)
            with pe.Fori(0, NB) as b:
                for i in range(BT + 2):
                    if i < BT:
                        pe.wait_ge(f_rows, b * BT + (i + 1))
                        pe.wait_ge(f_tcp, b * BT + (i + 1))
                        for f in range(2):
                            ins = nc.tensor.transpose(ps[:, 7, f * P:(f + 1) * P], urow[:, i, f * P:(f + 1) * P], ident[:, :])
                        ins.then_inc(f_tps, 1)
                    if 1 <= i <= BT:
                        j = i - 1
                        pe.wait_ge(f_tcp, b * BT + (j + 2))
                        pe.wait_ge(f_sub, b * BT + (max(j - 1, 0) + 1))
                        for d in range(2):
                            M(ps[:, j % 2, :], feat[:, d, j * P:(j + 1) * P], wxs[:, d, :], start=(d == 0), stop=False)
                        M(ps[:, j % 2, :], ones[0:1, :], slice_bias[:, :], start=False, stop=True).then_inc(f_lg, 1)
                    if i >= 2:
                        j = i - 2
                        pe.wait_ge(f_sw, b * BT + (j + 1))
                        pe.wait_ge(f_swc, b * BT + (max(j - 1, 0) + 2))
                        for k in range(2):
                            M(ps[:, 4 + k, :], urow[:, j, k * P:(k + 1) * P], sweight[:, j % 2, :], start=False, stop=False)
                        M(ps[0:DH, 6, :], ones[:, 0:DH], sweight[:, j % 2, :], start=False, stop=False)
                        for k in range(4):
                            ins = nc.tensor.transpose(ps[:, 2 + j % 2, k * P:(k + 1) * P], sweight[:, j % 2, k * P:(k + 1) * P], ident[:, :])
                        ins.then_inc(f_used, 1)
            for k in range(2):
                M(ps[:, 4 + k, :], zero_row[:, 0:P], zero_row, start=False, stop=True)
            M(ps[0:DH, 6, :], zero_row[:, 0:DH], zero_row, start=False, stop=True).then_inc(f_pe, 1)

            def head(h):
                return slice(h * G, (h + 1) * G)

            pe.wait_ge(ffn_w, 16 * 7)
            pe.wait_ge(f_dve, 1)
            pe.wait_ge(f_swc, T + 2)
            for h in range(HEADS):
                for d in range(2):
                    M(ps[0:DH, 0, head(h)], wfx[:, d, head(h)], tokT[:, d, head(h)], start=(d == 0), stop=False)
                ins = M(ps[0:DH, 0, head(h)], bfx[:, head(h)], norm[0:1, head(h)], start=False, stop=True)
            ins.then_inc(f_pe, 1)
            pe.wait_ge(f_dve, 2)
            for k in range(2):
                M(ps[0:DH, 1 + k, :], wqkv[:, k, :], slT, start=True, stop=True)
            for h in range(HEADS):
                ins = M(ps[0:DH, 3, head(h)], slT[:, head(h)], wqkv[:, 2, :], start=True, stop=True)
            ins.then_inc(f_pe, 1)
            pe.wait_ge(f_dve, 5)
            for h in range(HEADS):
                ins = M(ps[0:DH, 0, head(h)], qT[:, head(h)], kT[:, head(h)], start=True, stop=True)
            ins.then_inc(f_pe, 1)
            pe.wait_ge(f_dve, 7)
            for h in range(HEADS):
                ins = nc.tensor.transpose(ps[0:DH, 1, head(h)], att[:, head(h)], ident[0:DH, 0:DH])
            ins.then_inc(f_pe, 1)
            pe.wait_ge(f_dve, 8)
            for h in range(HEADS):
                ins = M(ps[0:DH, 2, head(h)], vS[:, head(h)], attT[:, head(h)], start=True, stop=True)
            ins.then_inc(f_pe, 1)
            pe.wait_ge(f_dve, 9)
            for h in range(HEADS):
                c = (h // 2) * F
                ins = M(ps[:, 3 + 2 * (h % 2) + c // 512, c % 512:c % 512 + F], outT[:, (h // 2) * P:(h // 2 + 1) * P], wout[:, h, :], start=True, stop=True)
            ins.then_inc(f_pe, 1)
            pe.wait_ge(f_dve, 11)
            with pe.Fori(0, NB) as b:
                for i in range(BT):
                    pe.wait_ge(f_slot, b * BT + (i + 1))
                    pe.wait_ge(f_x, b * BT + (2 if i == 4 else 1))
                    for k in range(4):
                        ins = M(ps[:, i % 4, 0:F], feat[:, k, i * P:(i + 1) * P], pmat[:, k, :], start=(k == 0), stop=(k == 3))
                    ins.then_inc(f_rps, 1)

            def turned(b, i, rows, tps, tcp, token=1):
                pe.wait_ge(rows, b * BT + (i + 1))
                pe.wait_ge(tcp, b * BT + (max(i - 1, 0) + token))
                for f in range(2):
                    ins = nc.tensor.transpose(ps[:, i % 2, f * P:(f + 1) * P], urow[:, i, f * P:(f + 1) * P], ident[:, :])
                ins.then_inc(tps, 1)

            def conv_rows(k):
                rows, tps, tcp, xps, stage, _ = conv[k]
                with pe.Fori(0, NB) as b:
                    for i in range(BT + 1):
                        if i < BT:
                            turned(b, i, rows, tps, tcp)
                        if i >= 1:
                            j = i - 1
                            pe.wait_ge(tcp, b * BT + (j + 2))
                            pe.wait_ge(stage, b * BT + (max(j - 1, 0) + 1))
                            for d in range(2):
                                ins = M(ps[:, 2 + j % 2, 0:F], feat[:, d, j * P:(j + 1) * P], wconv[k][:, d, :], start=(d == 0), stop=(d == 1))
                            ins.then_inc(xps, 1)

            pe.wait_ge(f_x, T + 1)
            pe.wait_ge(conv_w, 16 * 5)
            for c in range(4):
                if c % 2 == 0:
                    conv_rows(c // 2)
                half_scale(3 + c)
                pe.wait_ge(c_lo, (c + 1) * T)
                with pe.Fori(0, NB) as b:
                    pe.wait_ge(c_read, b + (c * NB + 1))
                    for q in range(NB):
                        pe.wait_ge(chunk_in[q], b * 16 + 16 * (FIRST[3] + c * NB + 1))
                        for s in range(BT):
                            t = q * BT + s
                            for i in range(BT):
                                lhs = chunk[q][:, s, i * P:(i + 1) * P]
                                M(ps[:, i, 0:F + 1], lhs, hh1[:, t, 0:F + 1], start=(t == 0), stop=False)
                                ins = M(ps[:, i, 0:F], lhs, hl1[:, t, :], start=False, stop=(t == T - 1))
                        ins.then_inc(chunk_used[q], 1)

            pe.wait_ge(moe_w, 16 * 6)
            pe.wait_ge(c_read, 4 * NB + 1)
            rows, tps, tcp = r_rows, r_tps, r_tcp
            with pe.Fori(0, NB) as b:
                for i in range(BT + 1):
                    if i < BT:
                        turned(b, i, r_rows, r_tps, r_tcp)
                    if i >= 1:
                        j = i - 1
                        pe.wait_ge(r_tcp, b * BT + (j + 2))
                        pe.wait_ge(r_lgc, b * BT + (max(j - 1, 0) + 1))
                        for d in range(2):
                            M(ps[:, 2 + j % 2, 0:EXPERTS], feat[:, d, j * P:(j + 1) * P], wroute[:, d, :], start=(d == 0), stop=False)
                        M(ps[:, 2 + j % 2, 0:EXPERTS], ones[0:1, :], broute, start=False, stop=True).then_inc(r_lg, 1)
            nc.tensor.transpose(ps[:, 6, 0:96], evec_rows, ident[0:96, 0:96]).then_inc(e_vec, 1)
            pe.wait_ge(r_tcp, T + 1)
            with pe.Fori(0, NB) as b:
                for i in range(BT):
                    turned(b, i, e_rows, e_tps, e_tcp)
            pe.wait_ge(e_tcp, T + 1)
            pe.wait_ge(r_lgc, T + 1)
            pe.wait_ge(e_vecT, 1)
            with pe.Fori(0, EXPERTS // 2) as g:
                for s in range(2):
                    pe.wait_ge(w_in[s], g * 32 + 32)
                    pe.nop(nofuse=True)
                    with pe.Fori(0, NB) as b:
                        n = g * (2 * NB) + b + s * NB
                        pe.wait_ge(e_xe, n * 2 + 2)
                        for k in range(EH // P):
                            pe.wait_ge(e_gelu, n * (EH // P) + (max(k - 1, 0) + 1))
                            for h in range(2):
                                for d in range(2):
                                    ins = M(ps[:, 2 * (k % 2) + h, 0:HB], w1e[s][:, d, k * P:(k + 1) * P], feat[:, d, h * HB:(h + 1) * HB],
                                            start=(d == 0), stop=(d == 1))
                            ins.then_inc(e_hps, 1)
                        for i in range(BT):
                            pe.wait_ge(e_x, n * BT + (2 if i == 4 else 1))
                            if i == 0:
                                pe.wait_ge(e_gelu, n * (EH // P) + (EH // P + 1))
                            for k in range(EH // P):
                                M(ps[:, 4 + i % 4, 0:F], hT[:, k, i * P:(i + 1) * P], w2e[s][:, k, :], start=(k == 0), stop=False)
                            M(ps[:, 4 + i % 4, 0:F], ones[0:1, :], b2_rows[:, bass.ds(g * (2 * F) + s * F, F)], start=False, stop=True).then_inc(e_yps, 1)

_INS = ["x", "src", "dst"]


def kernel(**inputs):
    import numpy as _np
    import concourse.bacc as _bacc
    from concourse import mybir as _mybir
    from concourse.bass_utils import run_bass_kernel_spmd as _run

    nc = _bacc.Bacc("TRN2", target_bir_lowering=False, num_devices=1)
    arrays, aps = {}, {}
    for name, value in inputs.items():
        a = _np.ascontiguousarray(value)
        arrays[name] = a
        aps[name] = nc.dram_tensor(name, a.shape, _mybir.dt.from_np(a.dtype), kind="ExternalInput").ap()
    out = nc.dram_tensor("out", (N, F), _mybir.dt.float32, kind="ExternalOutput").ap()
    weights = {k: v for k, v in aps.items() if k not in _INS}
    build(nc, aps["x"], aps["src"], aps["dst"], weights, out)
    r = _run(nc, [arrays], core_ids=[0])
    return r.results[0]["out"]
```

```python
import concourse.bass as bass
from concourse import mybir
from contextlib import ExitStack, contextmanager

P = 128
N = 3125
EDGES = 53125
F = 256
HID = 512
T = -(-N // P)
TAIL = N - (T - 1) * P
BT = 5
NB = T // BT
BC = BT * P
HB = BC // 2
EC = -(-EDGES // P)
GQ = 4
GE = GQ * P
NG = EC // GQ
LOOK = 4
AROW = T * BC
ASIZE = NB * P * AROW
EPS = 1e-5
LN_SCALE = 1024.0
BN_BOUND = 56.0
HEADS, DH, G = 8, 64, 64
EXPERTS, EH = 8, 1024
CAP = 256
CHUNKS = (2 * N + EXPERTS * (CAP - 1)) // CAP
SLOTS = CHUNKS * CAP
CT = CAP // P
EK = EH // P
EV = EK + 4
fp32, fp16, i32, u32 = mybir.dt.float32, mybir.dt.float16, mybir.dt.int32, mybir.dt.uint32
ALU, ACT, AX = mybir.AluOpType, mybir.ActivationFunctionType, mybir.AxisListType


class Order:

    def __init__(self, eng, sem):
        self.eng, self.sem, self.base, self.n, self.turn, self.per = eng, sem, 0, 0, None, 0

    def mark(self, ins):
        ins.then_inc(self.sem, 1)
        self.n += 1

    def settle(self):
        if self.turn is None:
            self.eng.wait_ge(self.sem, self.base + self.n)
        else:
            self.eng.wait_ge(self.sem, self.turn * self.per + (self.base + self.n))

    @contextmanager
    def loop(self, count, per):
        self.base, self.n = self.base + self.n, 0
        with self.eng.Fori(0, count) as i:
            self.turn, self.per = i, per
            yield i
            assert self.n == per, (self.n, per)
        self.base, self.n, self.turn = self.base + count * per, 0, None

    @contextmanager
    def loop_from(self, first, end, per):
        self.base, self.n = self.base + self.n - first * per, 0
        with self.eng.Fori(first, end) as i:
            self.turn, self.per = i, per
            yield i
            assert self.n == per, (self.n, per)
        self.base, self.n, self.turn = self.base + end * per, 0, None


def build(nc, x, src, dst, w, out):
    ctx = ExitStack()
    with ctx:
        def sb(name, shape, dt=fp32):
            return ctx.enter_context(nc.sbuf_tensor(name, shape, dt))

        def sem(name):
            return ctx.enter_context(nc.semaphore(name))

        def dram(name, shape, dt):
            return nc.dram_tensor(name, shape, dt, kind="Internal").ap()

        def runs(ap, **k):
            return ap.rearrange("p (a b) -> p a b", **k)

        at_flat = dram("at_counts", (ASIZE + GE, 1), fp16)
        ad_flat = dram("ad_counts", (ASIZE, 1), fp16)
        at = at_flat[0:ASIZE, :].rearrange("(b p r) a -> p b (r a)", b=NB, p=P)
        ad = ad_flat.rearrange("(b p r) a -> p b (r a)", b=NB, p=P)
        key_rows = dram("key_rows", (EC * P,), fp32)
        tok_in = dram("tok_in", (SLOTS + 2 * P, F), fp32)
        tok_out = dram("tok_out", (SLOTS, F), fp32)
        evec_rows = dram("expert_vectors", (EXPERTS, P, EV), fp32)

        ring = sb("ring", [P, 8192])
        harena = sb("harena", [P, 12864])
        tarena = sb("tarena", [P, 4 * T * P])
        xrows = sb("xrows", [P, T, F])
        wl = sb("wl", [P, 2048])
        wr = sb("wr", [P, 2048])
        feat = sb("feat", [P, 4, BC])
        late = sb("late", [P, T * P])
        wxs = sb("wxs", [P, 2, HID])
        ident = sb("ident", [P, P])
        ident16 = sb("ident16", [P, P], fp16)
        ones = sb("ones", [P, P])
        ones16 = sb("ones16", [P, P], fp16)
        tri = sb("tri", [P, P])
        ln_st = sb("ln_st", [P, T, 6])
        ln_mv = sb("ln_mv", [P, T, 2])
        ln_r = sb("ln_r", [P, T])
        ln_s = sb("ln_s", [P, T])
        rowmask = sb("rowmask", [P, T])
        bn_st = sb("bn_st", [P, 4, 2 * NB, 6])
        bn_mv = sb("bn_mv", [P, 4, 2])
        bn_k = sb("bn_k", [P, 4, 4])
        vec = [sb(f"vec{l}", [P, 3, 4]) for l in range(3)]
        amax = sb("amax", [P, T])
        sc = sb("sc", [P, 4])
        sc1 = sb("sc1", [1, 4])
        slice_bias = sb("slice_bias", [1, HID])

        chunk = [ring[:, :].bitcast(fp16)[:, q * BT * BC:(q + 1) * BT * BC].rearrange("p (s c) -> p s c", s=BT)
                 for q in range(NB)]
        chunk_flat = [ring[:, :].bitcast(fp16)[:, q * BT * BC:(q + 1) * BT * BC] for q in range(NB)]
        h16 = harena[:, :].bitcast(fp16)

        def halves(d):
            return (runs(h16[:, 0:T * d], a=T), runs(h16[:, T * d:2 * T * d], a=T))

        tfeat = tarena[:, :].rearrange("p (f n) -> p f n", f=4)
        zeros16 = tarena[:, :].bitcast(fp16)[:, 0:AROW]
        deginv = late[:, :]
        ps = ctx.enter_context(nc.psum_tensor("ps", [P, 8, 512], fp32))
        ps16 = ps[:, :, :].bitcast(fp16)

        astore = [harena[:, 6432 + s * 1600:6432 + (s + 1) * 1600].bitcast(fp16).rearrange("p (i c) -> p i c", i=BT) for s in range(2)]

        eint = harena[:, 6432:6432 + 3 * EC].bitcast(i32).rearrange("p (a c) -> p a c", a=3)
        eflt = harena[:, 7680:7680 + 4 * EC].rearrange("p (a c) -> p a c", a=4)
        keyT = harena[0:EC // GQ, 9344:9344 + GE]
        ekey = ring[:, 0:EC]
        espare = ring[:, EC:2 * EC]
        eweight = ring[:, 1024:1024 + GQ * GE].rearrange("p (a c) -> p a c", a=GQ)
        krow = ring[:, 3072:3072 + LOOK * GE].rearrange("p (a c) -> p a c", a=LOOK)
        ejunk = ring[:, 5120:5120 + GQ * GE].rearrange("p (a c) -> p a c", a=GQ)
        ecount = ring[:, 7168:7168 + 4 * GQ].rearrange("p (a c) -> p a c", a=4)
        eshift = ring[:, 7200:7200 + 4 * GQ].rearrange("p (a c) -> p a c", a=4)
        eidx = ring[:, 7232:7232 + 4 * GQ].bitcast(i32).rearrange("p (a c) -> p a c", a=4)
        evalue = ring[:, 7264:7264 + 4 * GQ].bitcast(fp16)[:, 0:4 * GQ].rearrange("p (a c) -> p a c", a=4)
        etrash_i = ring[:, 7296:7296 + GQ].bitcast(i32)
        etrash = ring[:, 7304:7304 + GQ]
        wx_in = tarena[:, 8192:8192 + 2 * HID].rearrange("p (a c) -> p a c", a=2)
        wxT = tarena[0:DH, 9216:9216 + HEADS * F].rearrange("p (h d) -> p h d", h=HEADS)
        wsl = tarena[0:DH, 11264:11264 + G]
        bxT = tarena[0:DH, 11328:11328 + HEADS]
        temp_row = tarena[0:1, 11336:11336 + HEADS]
        rtemp = tarena[:, 11344:11344 + HEADS]
        bsl_row = tarena[0:1, 11352:11352 + G]
        bias_raw = tarena[0:1, 11416:11416 + HID]

        wl2 = wl[:, :].rearrange("p (d f) -> p d f", f=HID)
        wr2 = wr[:, :].rearrange("p (d f) -> p d f", f=HID)
        wr3 = wr[:, 0:1024].rearrange("p (d f) -> p d f", f=F)
        wl3 = wr[:, 1024:2048].rearrange("p (d f) -> p d f", f=F)
        urow = feat[:, 2:4, :].rearrange("p a b -> p (a b)").rearrange("p (t c) -> p t c", c=F)
        stage_rows = runs(harena[:, 6432:6432 + T * F], a=T)

        logit = harena[:, 10240:10240 + 3 * HID].rearrange("p (s c) -> p s c", s=3)
        sweight = harena[:, 0:3 * HID].rearrange("p (s c) -> p s c", s=3)
        tokT = harena[:, 2048:2048 + 2 * HID].rearrange("p (d c) -> p d c", d=2)
        norm = harena[0:DH, 3072:3072 + HID]
        rnorm = harena[0:DH, 3584:3584 + HID]
        slT, qT, kT, vS, att, attT, outT = (harena[0:DH, 4096 + k * HID:4096 + (k + 1) * HID] for k in range(7))
        pmat = harena[:, 7680:7680 + 4 * F].rearrange("p (k o) -> p k o", k=4)
        wqkv = harena[0:DH, 8704:8704 + 3 * DH].rearrange("p (k c) -> p k c", k=3)
        bfx = harena[0:1, 8896:8896 + HID]
        hmax = harena[:, 11776:11776 + 3 * HEADS].rearrange("p (s h) -> p s h", s=3)
        hsum = harena[:, 11800:11800 + 3 * HEADS].rearrange("p (s h) -> p s h", s=3)
        hrec = harena[:, 11824:11824 + 3 * HEADS].rearrange("p (s h) -> p s h", s=3)
        bout = harena[:, 9472:9472 + F]
        zero_row = harena[0:1, 9728:9728 + HID]
        wout = wl[0:DH, :].rearrange("p (h o) -> p h o", h=HEADS)
        wfx = wr[:, 0:1024].rearrange("p (d c) -> p d c", d=2)
        wconv = [wr[:, 1024 + k * 512:1536 + k * 512].rearrange("p (d c) -> p d c", d=2) for k in range(2)]
        bconv = [late[:, k * F:(k + 1) * F] for k in range(2)]
        slope = late[:, 512:513]
        rdeg = late[:, 520:520 + BT]
        rows2 = tarena[:, 0:T * F].rearrange("p (t c) -> p t c", t=T)
        zrows, negrows, urows = (runs(tarena[:, (T + k * BT) * F:(T + (k + 1) * BT) * F], a=BT) for k in range(3))
        hh1 = h16[:, 0:T * (F + 2)].rearrange("p (t c) -> p t c", t=T)
        hl1 = h16[:, T * (F + 2):T * (F + 2) + T * F].rearrange("p (t c) -> p t c", t=T)
        wroute = late[:, 600:600 + 2 * EXPERTS].rearrange("p (d e) -> p d e", d=2)
        broute = late[0:1, 616:616 + EXPERTS]
        evec_in = late[0:96, 640:640 + P]
        evec = late[:, 768:768 + 96]
        xn = runs(tarena[:, T * F:2 * T * F], a=T)
        got = [runs(tarena[:, k * T * F:(k + 1) * T * F], a=T) for k in range(2)]
        w1e = [ring[:, s * 4096:s * 4096 + 2048].rearrange("p (d h) -> p d h", d=2) for s in range(2)]
        w2e = [ring[:, s * 4096 + 2048:(s + 1) * 4096].rearrange("p (k o) -> p k o", k=EK) for s in range(2)]
        hT = [harena[:, s * 2048:(s + 1) * 2048].rearrange("p (k n) -> p k n", k=EK) for s in range(2)]
        xin = [runs(harena[:, 4096 + s * CT * F:4096 + (s + 1) * CT * F], a=CT) for s in range(2)]
        xeT = [runs(harena[:, 5120 + s * 2 * CAP:5120 + (s + 1) * 2 * CAP], a=2) for s in range(2)]
        yrow = [runs(harena[:, 6144 + s * CT * F:6144 + (s + 1) * CT * F], a=CT) for s in range(2)]
        b2e = [harena[:, 7168 + s * F:7168 + (s + 1) * F] for s in range(2)]
        evc = [harena[:, 7680 + s * EV:7680 + (s + 1) * EV] for s in range(2)]
        ids = harena[0:1, 7712:7712 + CHUNKS].bitcast(i32)
        lgt, pri, sel1, sel2, picked, count, place, seg_start = (
            harena[:, 8000 + k * T * EXPERTS:8000 + (k + 1) * T * EXPERTS].rearrange("p (t e) -> p t e", t=T) for k in range(8))
        top1, top2, gate1, gate2, first, trash = (harena[:, 9600 + k * T:9600 + (k + 1) * T] for k in range(6))
        slot_at, slot_in, slot_out = (harena[:, 9760 + k * 2 * T:9760 + (k + 1) * 2 * T].rearrange("p (k t) -> p k t", k=2) for k in range(3))
        slot_in, slot_out = slot_in.bitcast(i32), slot_out.bitcast(i32)
        trash_i = harena[:, 9920:9921].bitcast(i32)
        rank, total, ends, starts = (harena[:, 9928 + k * EXPERTS:9928 + (k + 1) * EXPERTS] for k in range(4))
        chunks_i = harena[:, 9960:9960 + EXPERTS].bitcast(i32)
        chunk_no_i = harena[0:1, 9968:9968 + CHUNKS].bitcast(i32)
        chunk_no, chunk_of = harena[0:1, 10000:10000 + CHUNKS], harena[0:1, 10032:10032 + CHUNKS]
        passed = harena[0:1, 10064:10064 + CHUNKS * EXPERTS].rearrange("p (c e) -> p c e", c=CHUNKS)

        consts_ready, filled, edges_in, x_in, zero_ready, zeroed, vec_in = map(sem, (
            "consts_ready", "filled", "edges_in", "x_in", "zero_ready", "zeroed", "vec_in"))
        fold_in, fold_pe, fold_dve = map(sem, ("fold_in", "fold_pe", "fold_dve"))
        keyT_psum, keyT_ready, key_ready, key_stored = map(sem, ("keyT_psum", "keyT_ready", "key_ready", "key_stored"))
        krow_in = [sem(f"krow_in{s}") for s in range(LOOK)]
        compared, idx_ready, scattered = map(sem, ("compared", "idx_ready", "scattered"))
        chunk_in = [sem(f"chunk_in{q}") for q in range(NB)]
        chunk_used = [sem(f"chunk_used{q}") for q in range(NB)]
        wr_in, wl_in, wr1_in, wl1_in, w2_in = map(sem, ("wr_in", "wl_in", "wr1_in", "wl1_in", "w2_in"))
        dve_order, pool_order = sem("dve_order"), sem("pool_order")
        ln_var, ln_std, bn_done = map(sem, ("ln_var", "ln_std", "bn_done"))
        sc_col, sc_row, sc_pow, sc_all, sc_ready = map(sem, ("scale_columns", "scale_across", "scale_power", "scale_spread", "scale_ready"))
        ad_ps, ad_sb = sem("ad_transposed"), sem("ad_copied")
        ad_out = [sem(f"ad_stored{s}") for s in range(2)]

        def fresh(tag, *names):
            return [sem(f"{tag}_{n}") for n in names]

        ent = [fresh(f"in{l}", "rows", "hi", "lo", "tps", "tcopied", "rps", "rdone") for l in range(3)] + [fresh("in3", "rows", "lo", "tps")]
        agg = [fresh(f"agg{l}", "mean", "ops", "odone") for l in range(3)]
        deg, degdone = fresh("agg0", "deg", "degdone")
        ffn_w, conv_w, moe_w = sem("ffn_weights_in"), sem("conv_weights_in"), sem("moe_weights_in")
        f_zero, f_rows, f_tps, f_tcp, f_lg, f_sub, f_exp, f_sw, f_used, f_swc = fresh(
            "ffn", "zeros", "rows", "transposed", "copied", "logits", "shifted", "exps", "weights", "weights_used", "weightsT_copied")
        f_pe, f_dve, f_act, f_bias, f_slot, f_rps, f_x = fresh("ffn", "pe", "dve", "act", "bias_added", "slots_filled", "out_rows", "x")
        conv = fresh("conv_entry", "rows", "transposed", "copied", "products", "staged", "largest")
        c_ones, c_hi, c_lo, c_read, c_max, c_h, c_x = fresh("conv", "ones", "hi", "lo", "sums_read", "largest", "hidden", "x")
        r_rows, r_tps, r_tcp, r_lg, r_lgc = fresh("route", "rows", "transposed", "copied", "logits", "logits_copied")
        r_dve, r_pe, r_act, r_trash = fresh("route", "dve", "pe", "act", "trash")
        e_vec_out, tok_zeroed, e_xn, tok_sorted = fresh("expert", "vectors_stored", "rows_zeroed", "rows", "rows_sorted")
        e_in = [sem(f"chunk_rows_in{s}") for s in range(2)]
        w1_in = [sem(f"expert_W1_in{s}") for s in range(2)]
        w2e_in = [sem(f"expert_W2_in{s}") for s in range(2)]
        y_out = [sem(f"chunk_stored{s}") for s in range(2)]
        e_tps, e_xe, e_hps, e_gelu, e_yps, e_y = fresh("expert", "transposed", "inputs", "hidden", "gelus", "outputs", "rows_out")
        gathered = [sem(f"gathered{b}") for b in range(NB)]
        m_x, out_stored = fresh("moe", "x", "out_stored")
        block = ctx.enter_context(nc.Block())

        def nodes(b):
            return bass.ds(b * BC, BC)

        def two(ap):
            return ap.rearrange("p (h c) -> p h c", h=2)

        def three_stages(blocks, first, second, third):
            def turn(t, i):
                first(t, i)
                if not isinstance(t, int) or t >= 1:
                    second(t - 1, (i - 1) % BT)
                if not isinstance(t, int) or t >= 2:
                    third(t - 2, (i - 2) % BT)

            for t in range(BT):
                turn(t, t)
            with blocks as b:
                for i in range(BT):
                    turn(b * BT + i, i)
            second(T - 1, BT - 1)
            third(T - 2, BT - 2)
            third(T - 1, BT - 1)

        def before(i):
            return 2 if i >= 1 else 1

        DIMS = [(2, 4), (4, 4), (4, 2)]
        PASSES = [1, 2, 1]
        FIRST = [0, NB, 3 * NB, 4 * NB]

        @block.sync
        def _(sp):
            sp.wait_ge(filled, 2)
            cut = (P - 1) * EC
            for a, e in ((0, src), (1, dst)):
                for p0, p1 in ((0, 112), (112, P - 1)):
                    sp.dma_start(eint[p0:p1, a, :], e[p0 * EC:p1 * EC].rearrange("(p c) -> p c", c=EC)).then_inc(edges_in, 16)
                sp.dma_start(eint[P - 1:P, a, 0:EDGES - cut], e[cut:EDGES].rearrange("(p c) -> p c", p=1)).then_inc(edges_in, 16)
            sp.dma_start(xrows[:, 0:T - 1, :], x[0:(T - 1) * P, :].rearrange("(t p) d -> p t d", p=P)).then_inc(x_in, 16)
            sp.dma_start(xrows[0:TAIL, T - 1, :], x[(T - 1) * P:N, :]).then_inc(x_in, 16)
            sp.wait_ge(zero_ready, 1)
            for b in range(NB):
                sp.dma_start(at[:, b, :], zeros16).then_inc(zeroed, 16)
            sp.dma_start(at_flat[ASIZE:ASIZE + GE, :].rearrange("(p n) a -> p (n a)", p=P), zeros16[:, 0:GE // P]).then_inc(zeroed, 16)
            tok_zero = tok_in[0:SLOTS, :].rearrange("(p r) d -> p (r d)", p=P)
            for c0 in range(0, SLOTS // P * F, AROW // 2):
                c1 = min(c0 + AROW // 2, SLOTS // P * F)
                sp.dma_start(tok_zero[:, c0:c1], zeros16.bitcast(fp32)[:, 0:c1 - c0]).then_inc(tok_zeroed, 16)
            sp.wait_ge(keyT_ready, 1)
            sp.dma_start(key_rows.rearrange("(q r n) -> r q n", q=GQ, n=P), keyT.rearrange("r (q n) -> r q n", q=GQ)).then_inc(key_stored, 16)
            sp.wait_ge(key_stored, 16)
            for s in range(LOOK):
                sp.dma_start(krow[:, s, :], key_rows[s * GE:(s + 1) * GE].partition_broadcast(P)).then_inc(krow_in[s], 16)
            with sp.Fori(0, NG // LOOK - 1) as i:
                for s in range(LOOK):
                    sp.wait_ge(compared, LOOK * i + (s + 1))
                    sp.dma_start(krow[:, s, :], key_rows[bass.ds(i * (LOOK * GE) + (s + LOOK) * GE, GE)].partition_broadcast(P)).then_inc(krow_in[s], 16)
            sp.wait_ge(scattered, NG * GQ * 16)

            def load_chunks(table, b, done):
                for q in range(NB):
                    sp.wait_ge(chunk_used[q], done)
                    sp.dma_start(chunk_flat[q], table[:, bass.ds(b, 1), q * BT * BC:(q + 1) * BT * BC].rearrange("p o e -> p (o e)")).then_inc(chunk_in[q], 16)

            for l in range(3):
                with sp.Fori(0, NB) as b:
                    for k in range(PASSES[l]):
                        load_chunks(at, b, b * PASSES[l] + (FIRST[l] + k + 1))
            for s, n in ((0, 3), (1, 2)):
                sp.wait_ge(ad_out[s], 16 * (n * NB + 1))
            for c in range(4):
                with sp.Fori(0, NB) as b:
                    load_chunks(at if c % 2 == 0 else ad, b, b + (FIRST[3] + c * NB + 1))
            for q in range(NB):
                sp.wait_ge(chunk_used[q], FIRST[3] + 4 * NB + 1)
            sp.wait_ge(r_act, 2)
            for k0, k1, c0 in ((0, EK, 0), (EK, EK + 2, 64), (EK + 2, EV, 80)):
                sp.dma_start(evec_rows[:, :, k0:k1].rearrange("e p k -> p e k"),
                             evec[:, c0:c0 + EXPERTS * (k1 - k0)].rearrange("p (e k) -> p e k", e=EXPERTS), allow_slow_non_contiguous=True).then_inc(e_vec_out, 16)
            sp.wait_ge(e_vec_out, 16 * 3)
            sp.wait_ge(r_dve, 3)
            def load_rows(c, s):
                e = bass.ds(sp.value_load(ids[:, bass.ds(c, 1)], min_val=0, max_val=EXPERTS - 1), 1)
                sp.dma_start(w1e[s], w["L1_ffn_W1"][e, :, :].rearrange("e (d p) h -> p (e d) h", p=P)).then_inc(w1_in[s], 16)
                sp.dma_start(evc[s], evec_rows[e, :, :].rearrange("e p k -> p (e k)")).then_inc(e_in[s], 16)
                if isinstance(c, int) and c == 0:
                    sp.wait_ge(tok_sorted, 16 * 2 * T)
                sp.dma_start(xin[s], tok_in[bass.ds(c * CAP, CAP), :].rearrange("(i p) d -> p i d", p=P)).then_inc(e_in[s], 16)
                return e

            def load_second(e, s):
                sp.dma_start(w2e[s], w["L1_ffn_W2"][e, :, :].rearrange("e (k p) o -> p (e k) o", p=P)).then_inc(w2e_in[s], 16)
                sp.dma_start(b2e[s], w["L1_ffn_b2"][e, :].rearrange("e o -> (e o)").partition_broadcast(P)).then_inc(w2e_in[s], 16)

            def store_chunk(c, s):
                sp.dma_start(tok_out[bass.ds(c * CAP, CAP), :].rearrange("(i p) d -> p i d", p=P), yrow[s]).then_inc(y_out[s], 16)

            for s in range(2):
                sp.sem_inc(y_out[s], 16)
                load_second(load_rows(s, s), s)
            with sp.Fori(1, CHUNKS // 2) as g:
                for s in range(2):
                    sp.wait_ge(e_gelu, g * (2 * EK) + (s * EK - EK + 1))
                    sp.nop(nofuse=True)
                    e = load_rows(g * 2 + s, s)
                    sp.wait_ge(e_y, g * 2 + (s + 1))
                    sp.nop(nofuse=True)
                    store_chunk(g * 2 + (s - 2), s)
                    load_second(e, s)
            for s in range(2):
                sp.wait_ge(e_y, CHUNKS + 1 + s)
                store_chunk(CHUNKS - 2 + s, s)
            for b in range(NB):
                sp.wait_ge(m_x, b + 1)
                if b < NB - 1:
                    sp.dma_start(out[b * BC:(b + 1) * BC, :].rearrange("(t p) d -> p t d", p=P), xrows[:, b * BT:(b + 1) * BT, :]).then_inc(out_stored, 16)
                else:
                    sp.dma_start(out[b * BC:(T - 1) * P, :].rearrange("(t p) d -> p t d", p=P), xrows[:, b * BT:T - 1, :]).then_inc(out_stored, 16)
                    sp.dma_start(out[(T - 1) * P:N, :], xrows[0:TAIL, T - 1, :]).then_inc(out_stored, 16)
            sp.wait_ge(out_stored, 16 * (NB + 1))

        @block.gpsimd
        def _(pool):
            o = Order(pool, pool_order)
            nc.gpsimd.memset(eint[:, 0:2, :], T * P - 1).then_inc(filled, 1)
            nc.gpsimd.memset(xrows[:, T - 1, :], 0.0).then_inc(filled, 1)
            for q in range(NB):
                pool.sem_inc(chunk_used[q], 1)
            o.mark(nc.gpsimd.memset(ident[:, :], 0.0))
            o.mark(nc.gpsimd.memset(tri[:, :], 1.0))
            o.mark(nc.gpsimd.memset(rowmask[:, :], 1.0))
            o.mark(nc.gpsimd.memset(eweight, 1025.0))
            o.mark(nc.gpsimd.memset(ones[:, :], 1.0))
            o.mark(nc.gpsimd.memset(ones16[:, :], 1.0))
            o.mark(nc.gpsimd.iota(etrash_i, pattern=[[P, GQ]], base=ASIZE, channel_multiplier=1))
            o.settle()
            o.mark(nc.gpsimd.affine_select(out=ident[:, :], in_=ident[:, :], compare_op=ALU.not_equal, fill=1.0, base=0,
                                           pattern=[[-1, P]], channel_multiplier=1))
            o.mark(nc.gpsimd.affine_select(out=tri[:, :], in_=tri[:, :], compare_op=ALU.is_gt, fill=0.0, base=0,
                                           pattern=[[1, P]], channel_multiplier=-1))
            o.mark(nc.gpsimd.affine_select(out=rowmask[:, T - 1:T], in_=rowmask[:, T - 1:T], compare_op=ALU.is_gt, fill=0.0,
                                           base=TAIL, pattern=[[0, 1]], channel_multiplier=-1))
            o.mark(nc.gpsimd.affine_select(out=eweight, in_=eweight, compare_op=ALU.is_gt, fill=1.0, base=0,
                                           pattern=[[P, GQ], [-1, GE]], channel_multiplier=1))
            o.settle()
            nc.gpsimd.tensor_copy(ident16[:, :], ident[:, :]).then_inc(consts_ready, 1)
            pool.wait_ge(zeroed, 16 * (NB + 1))
            with pool.Fori(0, NG // LOOK) as i:
                for s in range(LOOK):
                    pool.wait_ge(idx_ready, LOOK * i + (s + 1))
                    pool.nop(nofuse=True)
                    for q in range(GQ):
                        nc.gpsimd.indirect_dma_start(
                            out=at_flat, out_offset=bass.IndirectOffsetOnAxis(ap=eidx[:, s, q:q + 1], axis=0),
                            in_=evalue[:, s, q:q + 1], in_offset=None, compute_op=ALU.add).then_inc(scattered, 16)
                    pool.wait_ge(scattered, i * (LOOK * GQ * 16) + (s + 1) * (GQ * 16))
            pool.wait_ge(ent[0][5], NB * 4 + 1)
            pool.dma_start(wr2, w["L0_gnn_Wr1"].rearrange("(d p) f -> p d f", p=P)).then_inc(wr1_in, 16)
            pool.wait_ge(agg[0][1], NB * 4 + 1)
            pool.dma_start(wl2, w["L0_gnn_Wl1"].rearrange("(d p) f -> p d f", p=P)).then_inc(wl1_in, 16)
            pool.wait_ge(ent[1][5], NB * 4 + 1)
            pool.dma_start(wr3, w["L0_gnn_Wr2"].rearrange("(d p) f -> p d f", p=P)).then_inc(w2_in, 16)
            pool.dma_start(wl3, w["L0_gnn_Wl2"].rearrange("(d p) f -> p d f", p=P)).then_inc(w2_in, 16)
            pool.wait_ge(chunk_used[NB - 1], FIRST[3] + 1)
            pool.wait_ge(agg[2][0], 2 * NB + 1)
            pool.dma_start(wout, w["L0_ffn_W_out"].rearrange("(h c) o -> c h o", c=DH)).then_inc(ffn_w, 16)
            pool.dma_start(wfx, w["L0_ffn_W_fx"].rearrange("(d p) f -> p d f", p=P)).then_inc(ffn_w, 16)
            for k, name in enumerate("qkv"):
                pool.dma_start(wqkv[:, k, :], w[f"L0_ffn_W_{name}"]).then_inc(ffn_w, 16)
            pool.dma_start(bfx, w["L0_ffn_b_fx"].rearrange("(a c) -> a c", a=1)).then_inc(ffn_w, 16)
            pool.dma_start(bout, w["L0_ffn_b_out"].partition_broadcast(P)).then_inc(ffn_w, 16)
            for k in range(2):
                pool.dma_start(wconv[k], w[f"L1_gnn_W{k + 1}"].rearrange("(d p) f -> p d f", p=P)).then_inc(conv_w, 16)
                pool.dma_start(bconv[k], w[f"L1_gnn_b{k + 1}"].partition_broadcast(P)).then_inc(conv_w, 16)
            pool.dma_start(slope, w["L1_gnn_a"].partition_broadcast(P)).then_inc(conv_w, 16)
            pool.dma_start(wroute, w["L1_ffn_Wr"].rearrange("(d p) e -> p d e", p=P)).then_inc(moe_w, 16)
            pool.dma_start(broute, w["L1_ffn_br"].rearrange("(a e) -> a e", a=1)).then_inc(moe_w, 16)
            pool.dma_start(evec_in[0:64, :], w["L1_ffn_b1"].rearrange("e (k p) -> (e k) p", p=P)).then_inc(moe_w, 16)
            pool.dma_start(evec_in[64:80, :], w["L1_ffn_ln_g"].rearrange("e (d p) -> (e d) p", p=P)).then_inc(moe_w, 16)
            pool.dma_start(evec_in[80:96, :], w["L1_ffn_ln_b"].rearrange("e (d p) -> (e d) p", p=P)).then_inc(moe_w, 16)
            pool.wait_ge(f_rows, T)
            pool.wait_ge(ffn_w, 16 * 7)
            nc.gpsimd.tensor_tensor(xrows[:, :, :], xrows[:, :, :], bout.unsqueeze(1).to_broadcast([P, T, F]), ALU.add).then_inc(f_bias, 1)
            rows, tps = conv[0:2]
            pool.wait_ge(c_h, NB)
            with pool.Fori(0, NB) as b:
                for i in range(BT):
                    pool.wait_ge(tps, b * BT + (T + i + 1))
                    pool.nop(nofuse=True)
                    nc.gpsimd.tensor_copy(urow[:, i:i + 1, :], rows2[:, bass.ds(b * BT + i, 1), :]).then_inc(rows, 1)
            pool.wait_ge(c_x, 1)
            o.mark(nc.gpsimd.iota(trash_i, pattern=[[0, 1]], base=SLOTS, channel_multiplier=1))
            nc.gpsimd.iota(chunk_no_i, pattern=[[1, CHUNKS]], base=0, channel_multiplier=0).then_inc(r_trash, 1)
            pool.wait_ge(e_xn, T)
            pool.wait_ge(r_dve, 5)
            pool.wait_ge(tok_zeroed, 16 * 3)
            for t in range(T):
                for k in range(2):
                    nc.gpsimd.indirect_dma_start(out=tok_in, out_offset=bass.IndirectOffsetOnAxis(ap=slot_in[:, k, t:t + 1], axis=0),
                                                 in_=xn[:, t, :], in_offset=None).then_inc(tok_sorted, 16)
            for s in range(2):
                pool.wait_ge(y_out[s], 16 * (CHUNKS // 2 + 1))
            for t in range(T):
                for k in range(2):
                    nc.gpsimd.indirect_dma_start(out=got[k][:, t, :], out_offset=None, in_=tok_out,
                                                 in_offset=bass.IndirectOffsetOnAxis(ap=slot_out[:, k, t:t + 1], axis=0)).then_inc(gathered[t // BT], 16)

        @block.scalar
        def _(act):
            def wait(s, value):
                act.wait_ge(s, value)
                if not isinstance(value, int):
                    act.nop(nofuse=True)

            act.sem_inc(ad_out[0], 16)
            act.sem_inc(ad_out[1], 16)
            act.sem_inc(ad_sb, 1)
            for l in range(3):
                act.sem_inc(ent[l][1], 1)
                act.sem_inc(ent[l][4], 1)
                act.sem_inc(ent[l][6], 1)
            for l in range(3):
                for k, name in enumerate(("bl", "gamma", "beta")):
                    act.dma_start(vec[l][:, k, 0:DIMS[l][1]], w[f"L0_gnn_{name}{l}"].rearrange("(f p) -> p f", p=P), allow_slow_non_contiguous=True).then_inc(vec_in, 16)
            act.dma_start(wr2[:, 0:2, :], w["L0_gnn_Wr0"].rearrange("(d p) f -> p d f", p=P)).then_inc(wr_in, 16)
            act.dma_start(wl2[:, 0:2, :], w["L0_gnn_Wl0"].rearrange("(d p) f -> p d f", p=P)).then_inc(wl_in, 16)
            act.dma_start(wx_in, w["L0_ffn_W_x"].rearrange("(d p) f -> p d f", p=P)).then_inc(fold_in, 16)
            act.dma_start(wsl, w["L0_ffn_W_slice"]).then_inc(fold_in, 16)
            act.dma_start(bxT, w["L0_ffn_b_x"].rearrange("(h c) -> c h", c=DH), allow_slow_non_contiguous=True).then_inc(fold_in, 16)
            act.dma_start(temp_row, w["L0_ffn_temperature"].rearrange("a h b c -> a (h b c)")).then_inc(fold_in, 16)
            act.dma_start(bsl_row, w["L0_ffn_b_slice"].rearrange("(a g) -> a g", a=1)).then_inc(fold_in, 16)

            def ln_sqrt(k):
                wait(ln_var, k)
                nc.scalar.activation(ln_s[:, :], ln_r[:, :], ACT.Sqrt).then_inc(ln_std, 1)

            def bn_sqrt(k, n):
                wait(ln_var, k)
                nc.scalar.activation(bn_k[:, 1, 0:n], bn_k[:, 0, 0:n], ACT.Sqrt).then_inc(ln_std, 1)

            def products_done(l, b, fo, nfo):
                _, _, _, _, _, rps, rdone = ent[l]
                wait(rps, b * nfo + (fo + 2))
                k = 4 + 2 * (fo % 2)
                nc.scalar.activation(two(tfeat[:, fo, nodes(b)]), ps[:, k:k + 2, 0:HB],
                                     ACT.Identity, bias=vec[l][:, 0, fo:fo + 1]).then_inc(rdone, 1)

            ln_sqrt(1)
            wait(vec_in, 16 * 9)
            wait(zeroed, 16 * (NB + 1))
            wait(fold_dve, 5)
            rows, hi, lo, tps, tcopied, rps, rdone = ent[0]
            hh, _ = halves(F)
            with act.Fori(0, NB) as b:
                for i in range(BT):
                    wait(rows, b * BT + (i + 1))
                    nc.scalar.activation(hh[:, bass.ds(b * BT + i, 1), :], urow[:, i:i + 1, :], ACT.Copy, scale=LN_SCALE).then_inc(hi, 1)
                wait(tps, b + 2)
                wait(rps, b * 4 + 1)
                nc.scalar.activation(feat[:, 0:2, :], ps[:, 0:4, :].rearrange("p (f k) c -> p f (k c)", f=2)[:, :, 0:BC], ACT.Copy).then_inc(tcopied, 1)
                for fo in range(4):
                    products_done(0, b, fo, 4)
            with act.Fori(0, NB) as b:
                for q in range(NB):
                    store, s = astore[q % 2], q % 2
                    wait(ad_out[s], b * (16 * (3 - s)) + 16 * (q // 2 + 1))
                    for i in range(BT):
                        n = q * BT + i
                        wait(ad_ps, b * (NB * BT) + (n + 1))
                        nc.scalar.activation(store[:, i, :], ps16[:, 6 + n % 2, 0:BC], ACT.Copy).then_inc(ad_sb, 1)
                    wait(ad_sb, b * (NB * BT) + ((q + 1) * BT + 1))
                    act.dma_start(ad[:, q, bass.ds(b * (BT * BC), BT * BC)], store.rearrange("p i c -> p (i c)")).then_inc(ad_out[s], 16)
            bn_sqrt(2, 4)
            for l in (1, 2):
                rows, hi, lo, tps, tcopied, rps, rdone = ent[l]
                nfo = DIMS[l][1]
                hh, _ = halves(HID)
                wait(bn_done, l)
                if l == 1:
                    wait(sc_ready, 1)
                with act.Fori(0, NB) as b:
                    wait(tps, b * BT + 1)
                    wait(rps, b * nfo + 1)
                    for f in range(4):
                        nc.scalar.activation(feat[:, f, :], tfeat[:, f, nodes(b)], ACT.Relu,
                                             bias=bn_k[:, 3, f:f + 1], scale=bn_k[:, 0, f:f + 1]).then_inc(rows, 1)
                    for i in range(BT):
                        wait(tps, b * BT + (i + 2))
                        t = bass.ds(b * BT + i, 1)
                        if l == 1:
                            nc.scalar.activation(hh[:, t, :], ps[:, i % 4:i % 4 + 1, :], ACT.Copy, scale=sc[:, 0:1]).then_inc(hi, 1)
                        else:
                            nc.scalar.activation(stage_rows[:, t, :], ps[:, i % 4:i % 4 + 1, 0:F], ACT.Copy).then_inc(hi, 1)
                    for fo in range(nfo):
                        products_done(l, b, fo, nfo)
                if l == 2:
                    hh, _ = halves(F)
                    wait(sc_ready, 2)
                    with act.Fori(0, T) as t:
                        nc.scalar.activation(hh[:, bass.ds(t, 1), :], stage_rows[:, bass.ds(t, 1), :], ACT.Copy, scale=sc[:, 0:1]).then_inc(tcopied, 1)
                bn_sqrt(2 + l, nfo)
            rows, lo, tps = ent[3]
            wait(bn_done, 3)
            with act.Fori(0, NB) as b:
                wait(tps, b * BT + 1)
                for f in range(2):
                    nc.scalar.activation(feat[:, f, :], tfeat[:, f, nodes(b)], ACT.Relu,
                                         bias=bn_k[:, 3, f:f + 1], scale=bn_k[:, 0, f:f + 1]).then_inc(rows, 1)
            act.sem_inc(f_tcp, 1)
            act.sem_inc(f_swc, 2)
            for s in (conv[2], conv[4], r_tcp, e_gelu):
                act.sem_inc(s, 1)
            ln_sqrt(5)

            def transposed_copy(b, i, tps, tcp, bank, columns, base=0):
                wait(tps, b * BT + (base + BT + i + 1))
                nc.scalar.activation(columns, ps[:, bank, 0:F].rearrange("p (f c) -> p f c", f=2), ACT.Copy).then_inc(tcp, 1)

            def f_copy(t, i):
                wait(f_tps, t + 1)
                nc.scalar.activation(feat[:, 0:2, i * P:(i + 1) * P], ps[:, 7, 0:F].rearrange("p (f c) -> p f c", f=2), ACT.Copy).then_inc(f_tcp, 1)

            def f_exps(t, i):
                wait(f_sub, t + 2)
                nc.scalar.activation(logit[:, i % 3, :], logit[:, i % 3, :], ACT.Exp).then_inc(f_exp, 1)

            def f_weights(t, i):
                wait(f_used, t + (BT + 1))
                nc.scalar.activation(tfeat[:, :, bass.ds(t * P, P)], ps[:, 2 + i % 2, :].rearrange("p (k c) -> p k c", k=4), ACT.Copy).then_inc(f_swc, 1)

            three_stages(act.Fori(1, NB), f_copy, f_exps, f_weights)
            wait(f_dve, 6)
            nc.scalar.activation(att, att, ACT.Exp, scale=DH ** -0.5).then_inc(f_act, 1)
            wait(f_swc, T + 2)
            with act.Fori(0, NB) as b:
                for i in range(BT):
                    wait(f_rps, b * BT + (i + 1))
                    nc.scalar.activation(feat[:, :, i * P:(i + 1) * P], tfeat[:, :, bass.ds(b * BC + i * P, P)], ACT.Copy).then_inc(f_slot, 1)
            ln_sqrt(6)

            def conv_rows(k):
                _, tps, tcp, xps, stage, _ = conv
                with act.Fori(0, NB) as b:
                    for i in range(BT + 1):
                        if i < BT:
                            transposed_copy(b, i, tps, tcp, i % 2, feat[:, 0:2, i * P:(i + 1) * P], k * T)
                        if i >= 1:
                            wait(xps, b * BT + (k * T + i))
                            nc.scalar.activation(stage_rows[:, bass.ds(b * BT + i - 1, 1), :], ps[:, 2 + (i - 1) % 2, 0:F].unsqueeze(1), ACT.Copy).then_inc(stage, 1)

            for c in range(4):
                if c % 2 == 0:
                    conv_rows(c // 2)
                wait(sc_ready, 3 + c)
                if c == 0:
                    wait(c_ones, 1)
                else:
                    wait(chunk_used[NB - 1], FIRST[3] + c * NB + 1)
                with act.Fori(0, T) as t:
                    nc.scalar.activation(hh1[:, bass.ds(t, 1), 0:F], stage_rows[:, bass.ds(t, 1), :], ACT.Copy, scale=sc[:, 0:1]).then_inc(c_hi, 1)
            ln_sqrt(7)
            with act.Fori(0, NB) as b:
                for i in range(BT):
                    transposed_copy(b, i, r_tps, r_tcp, i % 2, feat[:, 0:2, i * P:(i + 1) * P])
            ln_sqrt(8)
            wait(r_dve, 1)
            nc.scalar.activation(gate2, gate2, ACT.Exp).then_inc(r_act, 1)
            wait(r_pe, 1)
            nc.scalar.activation(evec, ps[:, 6, 0:96], ACT.Copy).then_inc(r_act, 1)
            with act.Fori(0, CHUNKS // 2) as g:
                for s in range(2):
                    for k in range(EK):
                        wait(e_hps, g * (2 * EK) + (s * EK + k + 1))
                        nc.scalar.activation(hT[s][:, k, :], ps[:, k % 4, 0:CAP], ACT.Gelu, bias=evc[s][:, k:k + 1]).then_inc(e_gelu, 1)

        @block.vector
        def _(dve):
            o = Order(dve, dve_order)
            V = nc.vector
            V.memset(zeros16, 0.0).then_inc(zero_ready, 1)
            for s in (ent[0][2], ent[1][2], ent[2][2], ent[3][1], degdone):
                dve.sem_inc(s, 1)
            for l in range(3):
                dve.sem_inc(agg[l][0], 1)
                dve.sem_inc(agg[l][2], 1)

            def step(ins):
                o.mark(ins)
                o.settle()

            dve.wait_ge(edges_in, 16 * 6)
            step(V.tensor_scalar(eint[:, 2, :], eint[:, 0, :], 7, None, ALU.arith_shift_right))
            o.mark(V.tensor_copy(eflt[:, 0:3, :], eint[:, 0:3, :]))
            o.settle()
            step(V.tensor_scalar(eflt[:, 3, :], eflt[:, 1, :], float(BC), None, ALU.is_ge))
            for k in range(2, NB):
                step(V.scalar_tensor_tensor(out=eflt[:, 3, :], in0=eflt[:, 1, :], scalar=float(k * BC), in1=eflt[:, 3, :], op0=ALU.is_ge, op1=ALU.add))
            step(V.tensor_scalar(ekey, eflt[:, 0, :], float(AROW), None, ALU.mult))
            step(V.scalar_tensor_tensor(out=ekey, in0=eflt[:, 2, :], scalar=float(BC - P * AROW), in1=ekey, op0=ALU.mult, op1=ALU.add))
            step(V.scalar_tensor_tensor(out=ekey, in0=eflt[:, 3, :], scalar=float(P * AROW - BC), in1=ekey, op0=ALU.mult, op1=ALU.add))
            V.tensor_tensor(ekey, ekey, eflt[:, 1, :], ALU.add).then_inc(key_ready, 1)
            dve.wait_ge(key_ready, 1)
            dve.wait_ge(consts_ready, 1)
            step(V.tensor_copy(etrash, etrash_i))
            o.mark(V.tensor_tensor(espare.rearrange("p (g q) -> p g q", q=GQ), etrash.unsqueeze(1).to_broadcast([P, NG, GQ]),
                                   ekey.rearrange("p (g q) -> p g q", q=GQ), ALU.subtract))
            dve.wait_ge(keyT_psum, 1)
            V.tensor_copy(keyT, ps[0:EC // GQ, 0, :]).then_inc(keyT_ready, 1)
            dve.wait_ge(fold_in, 16 * 5)
            step(V.tensor_scalar(temp_row, temp_row, 0.1, 5.0, ALU.max, ALU.min))
            V.reciprocal(rtemp[0:1, :], temp_row).then_inc(fold_dve, 1)
            dve.wait_ge(fold_pe, 1)
            V.tensor_copy(wxT.rearrange("p h d -> p (h d)"), ps[0:DH, 1:5, :].rearrange("p k c -> p (k c)")).then_inc(fold_dve, 1)
            dve.wait_ge(fold_pe, 2)
            V.tensor_copy(rtemp, ps[:, 7, 0:HEADS]).then_inc(fold_dve, 1)
            dve.wait_ge(fold_pe, 3)
            dve.wait_ge(fold_dve, 3)
            o.mark(V.tensor_tensor(bias_raw.rearrange("p (h g) -> p h g", h=HEADS), ps[0:1, 7, :].rearrange("p (h g) -> p h g", h=HEADS),
                                   bsl_row.unsqueeze(1).to_broadcast([1, HEADS, G]), ALU.add))
            for d in range(2):
                V.tensor_tensor(wxs[:, d, :].rearrange("p (h g) -> p h g", h=HEADS), ps[:, 5 + d, :].rearrange("p (h g) -> p h g", h=HEADS),
                                rtemp.unsqueeze(2).to_broadcast([P, HEADS, G]), ALU.mult).then_inc(fold_dve, 1)
            o.settle()
            o.mark(V.tensor_tensor(slice_bias[:, :].rearrange("p (h g) -> p h g", h=HEADS), bias_raw.rearrange("p (h g) -> p h g", h=HEADS),
                                   rtemp[0:1, :].unsqueeze(2).to_broadcast([1, HEADS, G]), ALU.mult))

            def layernorm_stats(k, rows=xrows):
                with o.loop(T, 1) as t:
                    o.mark(V.bn_stats(ln_st[:, bass.ds(t, 1), :].rearrange("p o s -> p (o s)"), rows[:, bass.ds(t, 1), :].rearrange("p o c -> p (o c)")))
                o.settle()
                st = [ln_st[:, :, j] for j in range(6)]
                mean, var = ln_mv[:, :, 0], ln_mv[:, :, 1]
                o.mark(V.tensor_tensor(mean, st[1], st[4], ALU.add))
                o.mark(V.tensor_tensor(ln_r[:, :], st[1], st[4], ALU.subtract))
                o.mark(V.tensor_tensor(var, st[2], st[5], ALU.add))
                o.settle()
                o.mark(V.tensor_scalar(mean, mean, 0.5, None, ALU.mult))
                step(V.scalar_tensor_tensor(out=ln_s[:, :], in0=ln_r[:, :], scalar=0.25, in1=ln_r[:, :], op0=ALU.mult, op1=ALU.mult))
                step(V.scalar_tensor_tensor(out=var, in0=var, scalar=1.0 / F, in1=ln_s[:, :], op0=ALU.mult, op1=ALU.add))
                V.tensor_scalar(ln_r[:, :], var, EPS, None, ALU.add).then_inc(ln_var, 1)
                dve.wait_ge(ln_std, k)
                step(V.reciprocal(ln_r[:, :], ln_s[:, :]))

            def normalized(dst_ap, t, rows=xrows):
                return V.tensor_scalar(dst_ap, rows[:, bass.ds(t, 1), :].rearrange("p o c -> p (o c)"), ln_mv[:, bass.ds(t, 1), 0], ln_r[:, bass.ds(t, 1)],
                                       ALU.subtract, ALU.mult)

            def half_scale(k, cols):
                V.tensor_reduce(sc[:, 2:3], amax[:, 0:cols], AX.X, ALU.max).then_inc(sc_col, 1)
                dve.wait_ge(sc_row, k)
                step(V.tensor_reduce(sc1[:, 0:1], ps[0:1, 7, 0:P], AX.X, ALU.max))
                step(V.tensor_scalar(sc1[:, 1:2], sc1[:, 0:1], 1e-30, None, ALU.max))
                V.tensor_scalar(sc1[:, 2:3].bitcast(i32), sc1[:, 1:2].bitcast(i32), 0x7F800000, None, ALU.bitwise_and).then_inc(sc_pow, 1)
                dve.wait_ge(sc_all, k)
                step(V.tensor_scalar(sc[:, 1:2], ps[:, 7, P:P + 1], 2.0 ** -13, None, ALU.mult))
                V.reciprocal(sc[:, 0:1], sc[:, 1:2]).then_inc(sc_ready, 1)

            def edges_of(i, first):
                for s in range(LOOK):
                    dve.wait_ge(krow_in[s], 16 * (i + 1) if first else i * 16 + 16)
                    if not first:
                        dve.wait_ge(scattered, i * (LOOK * GQ * 16) + (s + 1 - LOOK) * (GQ * 16))
                    g = i * LOOK + s
                    for q in range(GQ):
                        key1 = ekey[:, g * GQ + q:g * GQ + q + 1] if first else ekey[:, bass.ds(i * (LOOK * GQ) + s * GQ + q, 1)]
                        ins = V.scalar_tensor_tensor(out=ejunk[:, q, :], in0=krow[:, s, :], scalar=key1, in1=eweight[:, q, :],
                                                     op0=ALU.is_equal, op1=ALU.mult, accum_out=ecount[:, s, q:q + 1])
                    ins.then_inc(compared, 1)
                    four = slice(g * GQ, g * GQ + GQ) if first else bass.ds(i * (LOOK * GQ) + s * GQ, GQ)
                    dve.wait_ge(compared, (s + 1) if first else i * LOOK + (s + 1))
                    step(V.scalar_tensor_tensor(out=eshift[:, s, :], in0=ecount[:, s, :], scalar=1024.0, in1=espare[:, four], op0=ALU.is_ge, op1=ALU.mult))
                    o.mark(V.tensor_scalar(evalue[:, s, :], ecount[:, s, :], 1024.0, None, ALU.min))
                    V.tensor_tensor(eidx[:, s, :], eshift[:, s, :], ekey[:, four], ALU.add).then_inc(idx_ready, 1)

            dve.wait_ge(x_in, 32)
            layernorm_stats(1)
            o.settle()
            edges_of(0, True)
            with o.loop_from(1, NG // LOOK, 2 * LOOK) as i:
                edges_of(i, False)

            rows, hi, lo, tps, tcopied, rps, rdone = ent[0]
            hh, hl = halves(F)
            with dve.Fori(0, NB) as b:
                dve.wait_ge(tps, b + 1)
                dve.wait_ge(hi, b * BT + 1)
                dve.wait_ge(lo, b * BT + 1)
                for i in range(BT):
                    normalized(urow[:, i, :], b * BT + i).then_inc(rows, 1)
                for i in range(BT):
                    dve.wait_ge(hi, b * BT + (i + 2))
                    t = bass.ds(b * BT + i, 1)
                    V.scalar_tensor_tensor(out=hl[:, t, :], in0=urow[:, i:i + 1, :], scalar=LN_SCALE, in1=hh[:, t, :],
                                           op0=ALU.mult, op1=ALU.subtract).then_inc(lo, 1)

            for l in range(3):
                nfi, nfo = DIMS[l]
                np_ = PASSES[l]
                mean, ops, odone = agg[l]
                rdone = ent[l][6]
                dve.wait_ge(rdone, NB * nfo + 1)
                inv = 1.0 / LN_SCALE if l == 0 else sc[:, 1:2]

                def aggregated(b, width):
                    if l == 0:
                        dve.wait_ge(deg, b + 1)
                        d2 = two(deginv[:, nodes(b)])
                        step(V.tensor_scalar(d2, ps[:, 4:6, 0:HB], 1.0, None, ALU.max))
                        dve.nop(nofuse=True)
                        V.reciprocal(deginv[:, nodes(b)], deginv[:, nodes(b)]).then_inc(degdone, 1)
                        dve.wait_ge(degdone, b + 2)
                    if l < 2:
                        dve.wait_ge(ops, b * nfo + 1)
                    for k in range(np_):
                        dve.wait_ge(chunk_used[NB - 1], b * np_ + (FIRST[l] + k + 2))
                        for j in range(2):
                            V.scalar_tensor_tensor(out=two(feat[:, 2 * k + j, :]), in0=ps[:, 2 * j:2 * j + 2, 0:HB], scalar=inv,
                                                   in1=two(deginv[:, nodes(b)]), op0=ALU.mult, op1=ALU.mult).then_inc(mean, 1)
                    for fo in range(nfo):
                        if l < 2:
                            dve.wait_ge(ops, b * nfo + (fo + 2))
                            k = 4 + 2 * (fo % 2)
                            V.tensor_tensor(two(tfeat[:, fo, nodes(b)]), ps[:, k:k + 2, 0:HB], two(tfeat[:, fo, nodes(b)]), ALU.add).then_inc(odone, 1)
                        else:
                            dve.wait_ge(mean, b * 2 + (fo + 2))
                            V.tensor_tensor(tfeat[:, fo, nodes(b)], feat[:, fo, :], tfeat[:, fo, nodes(b)], ALU.add).then_inc(odone, 1)
                    for fo in range(nfo):
                        dve.wait_ge(odone, b * nfo + (fo + 2))
                        for h in range(2):
                            c = HB if h == 0 else width
                            o.mark(V.bn_stats(bn_st[:, fo, bass.ds(b * 2 + h, 1), :].rearrange("p a s -> p (a s)"),
                                              tfeat[:, fo, bass.ds(b * BC + h * HB, c)]))

                with o.loop(NB - 1, 2 * nfo + (1 if l == 0 else 0)) as b:
                    aggregated(b, HB)
                aggregated(NB - 1, N - (NB - 1) * BC - HB)
                o.settle()
                for fo in range(nfo):
                    o.mark(V.bn_aggr(bn_mv[:, fo, :], bn_st[:, fo, :, :].rearrange("p a s -> p (a s)")))
                o.settle()
                V.tensor_scalar(bn_k[:, 0, 0:nfo], bn_mv[:, 0:nfo, 1], EPS, None, ALU.add).then_inc(ln_var, 1)
                dve.wait_ge(ln_std, 2 + l)
                step(V.reciprocal(bn_k[:, 2, 0:nfo], bn_k[:, 1, 0:nfo]))
                step(V.tensor_tensor(bn_k[:, 0, 0:nfo], bn_k[:, 2, 0:nfo], vec[l][:, 1, 0:nfo], ALU.mult))
                step(V.tensor_tensor(bn_k[:, 1, 0:nfo], bn_mv[:, 0:nfo, 0], bn_k[:, 0, 0:nfo], ALU.mult))
                V.tensor_tensor(bn_k[:, 3, 0:nfo], vec[l][:, 2, 0:nfo], bn_k[:, 1, 0:nfo], ALU.subtract).then_inc(bn_done, 1)
                if l == 0:
                    o.mark(V.scalar_tensor_tensor(out=amax[:, 0:4], in0=vec[0][:, 1, :], scalar=-1.0, in1=vec[0][:, 1, :], op0=ALU.mult, op1=ALU.max))
                    o.mark(V.scalar_tensor_tensor(out=amax[:, 4:8], in0=vec[0][:, 2, :], scalar=-1.0, in1=vec[0][:, 2, :], op0=ALU.mult, op1=ALU.max))
                    o.settle()
                    step(V.scalar_tensor_tensor(out=amax[:, 0:4], in0=amax[:, 0:4], scalar=BN_BOUND, in1=amax[:, 4:8], op0=ALU.mult, op1=ALU.add))
                    half_scale(1, 4)
                    rows, hi, lo, tps, tcopied, rps, rdone = ent[1]
                    hh, hl = halves(HID)
                    dve.wait_ge(sc_ready, 1)
                    for k, n in ((0, 3), (1, 2)):
                        dve.wait_ge(ad_out[k], 16 * (n * NB + 1))
                    with dve.Fori(0, NB) as b:
                        for i in range(BT):
                            dve.wait_ge(hi, b * BT + (i + 2))
                            t = bass.ds(b * BT + i, 1)
                            V.scalar_tensor_tensor(out=hl[:, t, :], in0=ps[:, i % 4:i % 4 + 1, :], scalar=sc[:, 0:1], in1=hh[:, t, :],
                                                   op0=ALU.mult, op1=ALU.subtract).then_inc(lo, 1)
                elif l == 1:
                    rows, hi, lo, tps, tcopied, rps, rdone = ent[2]
                    with dve.Fori(0, NB) as b:
                        for i in range(BT):
                            dve.wait_ge(hi, b * BT + (i + 2))
                            V.tensor_reduce(amax[:, bass.ds(b * BT + i, 1)], ps[:, i % 4, 0:F], AX.X, ALU.max,
                                            apply_absolute_value=True).then_inc(lo, 1)
                    dve.wait_ge(lo, T + 1)
                    half_scale(2, T)
                    hh, hl = halves(F)
                    dve.wait_ge(sc_ready, 2)
                    with dve.Fori(0, T) as t:
                        dve.wait_ge(tcopied, t + 2)
                        V.scalar_tensor_tensor(out=hl[:, bass.ds(t, 1), :], in0=stage_rows[:, bass.ds(t, 1), :], scalar=sc[:, 0:1],
                                               in1=hh[:, bass.ds(t, 1), :], op0=ALU.mult, op1=ALU.subtract).then_inc(lo, 1)
                else:
                    rows, lo, tps = ent[3]
                    with dve.Fori(0, NB) as b:
                        for i in range(BT):
                            dve.wait_ge(tps, b * BT + (i + 2))
                            t = bass.ds(b * BT + i, 1)
                            V.tensor_tensor(xrows[:, t, :], ps[:, i % 4:i % 4 + 1, 0:F], xrows[:, t, :], ALU.add).then_inc(lo, 1)
            H8 = "p (h g) -> p h g"
            dve.sem_inc(f_sub, 1)
            dve.sem_inc(f_x, 1)
            dve.sem_inc(c_read, 1)
            dve.sem_inc(r_lgc, 1)
            dve.sem_inc(e_y, 2)
            dve.wait_ge(ent[3][1], T + 1)
            dve.wait_ge(chunk_used[NB - 1], FIRST[3] + 1)
            V.memset(zero_row, 0.0).then_inc(f_zero, 1)
            layernorm_stats(5)

            def f_normal(t, i):
                dve.wait_ge(f_used, t + 1)
                normalized(urow[:, i, :], t).then_inc(f_rows, 1)

            def f_shift(t, i):
                s = i % 3
                dve.wait_ge(f_lg, t + 1)
                step(V.tensor_reduce(hmax[:, s, :], ps[:, i % 2, :].rearrange(H8, h=HEADS), AX.X, ALU.max))
                V.tensor_tensor(logit[:, s, :].rearrange(H8, h=HEADS), ps[:, i % 2, :].rearrange(H8, h=HEADS),
                                hmax[:, s, :].unsqueeze(2).to_broadcast([P, HEADS, G]), ALU.subtract).then_inc(f_sub, 1)

            def f_softmax(t, i):
                s = i % 3
                dve.wait_ge(f_exp, t + 1)
                step(V.tensor_reduce(hsum[:, s, :], logit[:, s, :].rearrange(H8, h=HEADS), AX.X, ALU.add))
                step(V.reciprocal(hrec[:, s, :], hsum[:, s, :]))
                dve.wait_ge(f_used, t + (BT - 1))
                V.scalar_tensor_tensor(out=sweight[:, s, :].rearrange(H8, h=HEADS), in0=logit[:, s, :].rearrange(H8, h=HEADS),
                                       scalar=rowmask[:, bass.ds(t, 1)], in1=hrec[:, s, :].unsqueeze(2).to_broadcast([P, HEADS, G]),
                                       op0=ALU.mult, op1=ALU.mult).then_inc(f_sw, 1)

            o.settle()
            three_stages(o.loop_from(1, NB, 3 * BT), f_normal, f_shift, f_softmax)
            dve.wait_ge(f_pe, 1)
            o.mark(V.tensor_copy(tokT, ps[:, 4:6, :]))
            o.mark(V.tensor_copy(norm, ps[0:DH, 6, :]))
            step(V.tensor_scalar(rnorm, ps[0:DH, 6, :], 1e-5, None, ALU.add))
            V.reciprocal(rnorm, rnorm).then_inc(f_dve, 1)
            dve.wait_ge(f_pe, 2)
            dve.wait_ge(f_dve, 1)
            V.tensor_tensor(slT, ps[0:DH, 0, :], rnorm, ALU.mult).then_inc(f_dve, 1)
            dve.wait_ge(f_pe, 3)
            for k, part in enumerate((qT, kT, vS)):
                V.tensor_copy(part, ps[0:DH, 1 + k, :]).then_inc(f_dve, 1)
            dve.wait_ge(f_pe, 4)
            lg4 = ps[0:DH, 0, :].rearrange(H8, h=HEADS)
            a4 = att.rearrange(H8, h=HEADS)
            step(V.tensor_reduce(hmax[0:DH, 0, :], lg4, AX.X, ALU.max))
            V.tensor_tensor(a4, lg4, hmax[0:DH, 0, :].unsqueeze(2).to_broadcast([DH, HEADS, G]), ALU.subtract).then_inc(f_dve, 1)
            dve.wait_ge(f_act, 1)
            step(V.tensor_reduce(hsum[0:DH, 0, :], a4, AX.X, ALU.add))
            step(V.reciprocal(hrec[0:DH, 0, :], hsum[0:DH, 0, :]))
            V.tensor_tensor(a4, a4, hrec[0:DH, 0, :].unsqueeze(2).to_broadcast([DH, HEADS, G]), ALU.mult).then_inc(f_dve, 1)
            dve.wait_ge(f_pe, 5)
            V.tensor_copy(attT, ps[0:DH, 1, :]).then_inc(f_dve, 1)
            dve.wait_ge(f_pe, 6)
            V.tensor_copy(outT, ps[0:DH, 2, :]).then_inc(f_dve, 1)
            dve.wait_ge(f_pe, 7)
            for k in range(2):
                half = slice(k * DH, (k + 1) * DH)
                V.tensor_copy(pmat[half, :, :].rearrange("p k o -> p (k o)"), ps[half, 3 + 2 * k:5 + 2 * k, :].rearrange("p k c -> p (k c)")).then_inc(f_dve, 1)
            dve.wait_ge(f_bias, 1)
            with dve.Fori(0, NB) as b:
                for i in range(BT):
                    dve.wait_ge(f_rps, b * BT + (BT + i + 1))
                    t = bass.ds(b * BT + i, 1)
                    V.tensor_tensor(xrows[:, t, :], ps[:, i % 4:i % 4 + 1, 0:F], xrows[:, t, :], ALU.add).then_inc(f_x, 1)

            dve.wait_ge(f_x, T + 1)
            layernorm_stats(6)
            V.memset(hh1[:, :, F:F + 2], 1.0).then_inc(c_ones, 1)

            def conv_largest(k, b, i):
                dve.wait_ge(conv[4], b * BT + (k * T + i + 2))
                V.tensor_reduce(amax[:, bass.ds(b * BT + i, 1)], stage_rows[:, bass.ds(b * BT + i, 1), :].rearrange("p o c -> p (o c)"), AX.X, ALU.max,
                                apply_absolute_value=True).then_inc(conv[5], 1)

            with dve.Fori(0, NB) as b:
                for i in range(BT + 2):
                    if i < BT:
                        dve.wait_ge(conv[1], b * BT + (i + 1))
                        normalized(urow[:, i, :], b * BT + i).then_inc(conv[0], 1)
                    if i >= 2:
                        conv_largest(0, b, i - 2)
            dve.wait_ge(conv_w, 16 * 5)
            for c in range(4):
                if c == 2:
                    with dve.Fori(0, NB) as b:
                        for i in range(BT):
                            conv_largest(1, b, i)
                if c % 2 == 0:
                    dve.wait_ge(conv[5], T * (c // 2 + 1))
                else:
                    dve.wait_ge(c_max, NB * (c // 2 + 1))
                half_scale(3 + c, T)
                dve.wait_ge(sc_ready, 3 + c)
                with dve.Fori(0, T) as t:
                    dve.wait_ge(c_hi, t + (c * T + 1))
                    V.scalar_tensor_tensor(out=hl1[:, bass.ds(t, 1), :], in0=stage_rows[:, bass.ds(t, 1), :], scalar=sc[:, 0:1],
                                           in1=hh1[:, bass.ds(t, 1), 0:F], op0=ALU.mult, op1=ALU.subtract).then_inc(c_lo, 1)
                with o.loop(NB, {0: 6, 1: 8, 2: 6, 3: 15}[c]) as b:
                    blk = bass.ds(b * BT, BT)
                    dve.wait_ge(chunk_used[NB - 1], b + (FIRST[3] + c * NB + 2))
                    step(V.tensor_scalar(rdeg, ps[:, 0:BT, F], 1.0, None, ALU.max))
                    step(V.reciprocal(rdeg, rdeg))
                    if c % 2 == 0:
                        for i in range(BT):
                            ins = V.tensor_scalar(stage_rows[:, bass.ds(b * BT + i, 1), :].rearrange("p o c -> p (o c)"), ps[:, i, 0:F],
                                                  rdeg[:, i:i + 1], sc[:, 1:2], ALU.mult, ALU.mult)
                            if i < BT - 1:
                                o.mark(ins)
                        ins.then_inc(c_read, 1)
                        dve.wait_ge(c_read, b + (c * NB + 2))
                        V.tensor_reduce(amax[:, blk], stage_rows[:, blk, :], AX.X, ALU.max, apply_absolute_value=True).then_inc(c_max, 1)
                    else:
                        step(V.tensor_scalar(rdeg, rdeg, sc[:, 1:2], None, ALU.mult))
                        for i in range(BT):
                            ins = V.scalar_tensor_tensor(out=zrows[:, i, :], in0=ps[:, i, 0:F], scalar=rdeg[:, i:i + 1], in1=bconv[c // 2],
                                                         op0=ALU.mult, op1=ALU.add)
                            if i < BT - 1:
                                o.mark(ins)
                        ins.then_inc(c_read, 1)
                        dve.wait_ge(c_read, b + (c * NB + 2))
                        if c == 3:
                            for i in range(BT):
                                o.mark(normalized(urows[:, i, :], b * BT + i))
                            o.settle()
                            step(V.tensor_tensor(zrows, zrows, urows, ALU.add))
                        step(V.tensor_scalar(negrows, zrows, 0.0, slope, ALU.min, ALU.mult))
                        if c == 1:
                            V.scalar_tensor_tensor(out=rows2[:, blk, :], in0=zrows, scalar=0.0, in1=negrows, op0=ALU.max, op1=ALU.add).then_inc(c_h, 1)
                        else:
                            step(V.scalar_tensor_tensor(out=zrows, in0=zrows, scalar=0.0, in1=negrows, op0=ALU.max, op1=ALU.add))
                            V.tensor_tensor(xrows[:, blk, :], xrows[:, blk, :], zrows, ALU.add).then_inc(c_x, 1)

            dve.wait_ge(c_x, NB)
            layernorm_stats(7)
            with o.loop(NB, BT) as b:
                for i in range(BT + 2):
                    if i < BT:
                        dve.wait_ge(r_tps, b * BT + (i + 1))
                        normalized(urow[:, i, :], b * BT + i).then_inc(r_rows, 1)
                        o.mark(normalized(rows2[:, bass.ds(b * BT + i, 1), :].rearrange("p o c -> p (o c)"), b * BT + i))
                    if i >= 2:
                        dve.wait_ge(r_lg, b * BT + (i - 1))
                        V.tensor_copy(lgt[:, bass.ds(b * BT + i - 2, 1), :].rearrange("p o e -> p (o e)"), ps[:, 2 + i % 2, 0:EXPERTS]).then_inc(r_lgc, 1)
            o.settle()
            layernorm_stats(8, rows2)
            with dve.Fori(0, T) as t:
                normalized(xn[:, bass.ds(t, 1), :].rearrange("p o c -> p (o c)"), t, rows2).then_inc(e_xn, 1)
            dve.wait_ge(r_lgc, T + 1)
            for e in range(EXPERTS):
                o.mark(V.memset(rank[:, e:e + 1], float(EXPERTS - e)))

            def each(ap):
                return ap.unsqueeze(2).to_broadcast([P, T, EXPERTS])

            for top, sel in ((top1, sel1), (top2, sel2)):
                step(V.tensor_reduce(top, lgt, AX.X, ALU.max))
                step(V.tensor_tensor(pri, lgt, each(top), ALU.is_equal))
                step(V.tensor_tensor(pri, pri, rank.unsqueeze(1).to_broadcast([P, T, EXPERTS]), ALU.mult))
                step(V.tensor_reduce(first, pri, AX.X, ALU.max))
                step(V.tensor_tensor(sel, pri, each(first), ALU.is_equal))
                if sel is sel1:
                    step(V.scalar_tensor_tensor(out=lgt, in0=sel, scalar=-3e38, in1=lgt, op0=ALU.mult, op1=ALU.add))
            V.tensor_tensor(gate2, top2, top1, ALU.subtract).then_inc(r_dve, 1)
            dve.wait_ge(r_act, 1)
            step(V.tensor_scalar(gate1, gate2, 1.0, None, ALU.add))
            step(V.reciprocal(gate1, gate1))
            step(V.tensor_tensor(gate2, gate2, gate1, ALU.mult))
            real = each(rowmask[:, :])
            o.mark(V.tensor_tensor(sel1, sel1, real, ALU.mult))
            step(V.tensor_tensor(sel2, sel2, real, ALU.mult))
            V.tensor_tensor(picked, sel1, sel2, ALU.add).then_inc(r_dve, 1)
            dve.wait_ge(r_trash, 1)
            o.mark(V.tensor_copy(trash[:, 0:1], trash_i))
            o.mark(V.tensor_copy(chunk_no, chunk_no_i))
            seg, cnt, plc = (a.rearrange("p t e -> p (t e)").rearrange("p (e t) -> p e t", e=EXPERTS) for a in (seg_start, count, place))
            step(V.memset(seg, 1.0))
            step(V.memset(seg[:, :, 0:1], 0.0))
            dve.wait_ge(r_pe, 2)
            per_tile = ps[:, 5, 0:T * EXPERTS].rearrange("p (t e) -> p e t", e=EXPERTS)
            step(V.tensor_copy(cnt, per_tile))
            step(V.tensor_tensor_scan(plc.rearrange("p e t -> p (e t)"), seg.rearrange("p e t -> p (e t)"), cnt.rearrange("p e t -> p (e t)"),
                                      0.0, ALU.mult, ALU.add))
            step(V.tensor_copy(chunks_i, plc[:, :, T - 1]))
            step(V.tensor_tensor(plc, plc, cnt, ALU.subtract))
            step(V.tensor_scalar(chunks_i, chunks_i, CAP - 1, None, ALU.add))
            step(V.tensor_scalar(chunks_i, chunks_i, CAP.bit_length() - 1, None, ALU.arith_shift_right))
            step(V.tensor_copy(total, chunks_i))
            step(V.tensor_tensor_scan(ends, seg[:, 0, 1:1 + EXPERTS], total, 0.0, ALU.mult, ALU.add))
            step(V.tensor_tensor(starts, ends, total, ALU.subtract))
            step(V.tensor_scalar(starts, starts, float(CAP), None, ALU.mult))
            step(V.tensor_tensor(plc, plc, starts.unsqueeze(2).to_broadcast([P, EXPERTS, T]), ALU.add))
            step(V.tensor_tensor(plc, plc, ps[:, 4, 0:T * EXPERTS].rearrange("p (t e) -> p e t", e=EXPERTS), ALU.add))
            step(V.tensor_tensor(passed, chunk_no.unsqueeze(2).to_broadcast([1, CHUNKS, EXPERTS]),
                                 ends[0:1, :].unsqueeze(1).to_broadcast([1, CHUNKS, EXPERTS]), ALU.is_ge))
            step(V.tensor_reduce(chunk_of, passed, AX.X, ALU.add))
            V.tensor_scalar(ids, chunk_of, float(EXPERTS - 1), None, ALU.min).then_inc(r_dve, 1)
            for k, sel in enumerate((sel1, sel2)):
                step(V.tensor_tensor(pri, sel, plc.rearrange("p e t -> p t e"), ALU.mult))
                step(V.tensor_reduce(slot_at[:, k, :], pri, AX.X, ALU.add))
            V.tensor_copy(slot_out, slot_at).then_inc(r_dve, 1)
            dve.wait_ge(r_dve, 4)
            o.mark(V.tensor_scalar(trash[:, 1:2], trash[:, 0:1], float(P), None, ALU.add))
            step(V.tensor_scalar(trash[:, 2:3], rowmask[:, T - 1:T], -1.0, 1.0, ALU.mult, ALU.add))
            step(V.scalar_tensor_tensor(out=slot_at[:, :, T - 1], in0=trash[:, 0:2], scalar=trash[:, 2:3], in1=slot_at[:, :, T - 1], op0=ALU.mult, op1=ALU.add))
            V.tensor_copy(slot_in, slot_at).then_inc(r_dve, 1)
            def expert_rows(c, uses, s):
                dve.wait_ge(e_tps, c + 1)
                dve.wait_ge(e_in[s], uses)
                for d in range(2):
                    V.tensor_scalar(xeT[s][:, d, :], ps[:, 6 + s, d * CAP:(d + 1) * CAP], evc[s][:, EK + d:EK + d + 1],
                                    evc[s][:, EK + 2 + d:EK + 3 + d], ALU.mult, ALU.add).then_inc(e_xe, 1)

            def chunk_out(c, stored, s):
                dve.wait_ge(e_yps, c + 3)
                dve.wait_ge(y_out[s], stored)
                V.tensor_tensor(yrow[s], ps[:, 4 + s, :].rearrange("p (i c) -> p i c", i=CT), b2e[s].unsqueeze(1).to_broadcast([P, CT, F]), ALU.add).then_inc(e_y, 1)

            expert_rows(0, 32, 0)
            with dve.Fori(0, CHUNKS // 2 - 1) as g:
                expert_rows(g * 2 + 1, g * 32 + 32, 1)
                chunk_out(g * 2, g * 16 + 16, 0)
                expert_rows(g * 2 + 2, g * 32 + 64, 0)
                chunk_out(g * 2 + 1, g * 16 + 16, 1)
            expert_rows(CHUNKS - 1, CHUNKS // 2 * 32, 1)
            chunk_out(CHUNKS - 2, CHUNKS // 2 * 16, 0)
            chunk_out(CHUNKS - 1, CHUNKS // 2 * 16, 1)
            for b in range(NB):
                dve.wait_ge(gathered[b], 16 * 2 * BT)
                for k, gate in enumerate((gate1, gate2)):
                    for i in range(BT):
                        t = b * BT + i
                        ins = V.scalar_tensor_tensor(out=xrows[:, t, :], in0=got[k][:, t, :], scalar=gate[:, t:t + 1], in1=xrows[:, t, :], op0=ALU.mult, op1=ALU.add)
                        if k == 1 and i == BT - 1:
                            ins.then_inc(m_x, 1)
                        else:
                            o.mark(ins)
                    o.settle()

        @block.tensor
        def _(pe):
            M = nc.tensor.matmul
            pe.sem_inc(ent[3][2], 1)
            for l in range(3):
                pe.sem_inc(ent[l][3], 1)
                pe.sem_inc(ent[l][5], 1)
            for l in range(3):
                pe.sem_inc(agg[l][1], 1)

            pe.wait_ge(consts_ready, 1)
            pe.wait_ge(key_ready, 1)
            for q in range(GQ):
                ins = nc.tensor.transpose(ps[0:NG, 0, q * P:(q + 1) * P], ekey[:, q * NG:(q + 1) * NG], ident[:, :])
            ins.then_inc(keyT_psum, 1)
            pe.wait_ge(fold_in, 16 * 5)
            for h in range(HEADS):
                for d in range(2):
                    n = 2 * h + d
                    ins = nc.tensor.transpose(ps[0:DH, 1 + n // 4, (n % 4) * P:(n % 4 + 1) * P], wx_in[:, d, h * DH:(h + 1) * DH], ident[:, :])
            ins.then_inc(fold_pe, 1)
            pe.wait_ge(fold_dve, 1)
            M(ps[:, 7, 0:HEADS], ones[0:1, :], rtemp[0:1, :], start=True, stop=True).then_inc(fold_pe, 1)
            pe.wait_ge(fold_dve, 3)
            for d in range(2):
                for h in range(HEADS):
                    M(ps[:, 5 + d, h * G:(h + 1) * G], wxT[:, h, d * P:(d + 1) * P], wsl, start=True, stop=True)
            for h in range(HEADS):
                ins = M(ps[0:1, 7, h * G:(h + 1) * G], bxT[:, h:h + 1], wsl, start=True, stop=True)
            ins.then_inc(fold_pe, 1)

            def products(l, b, nfi, nfo, weights):
                _, _, _, _, _, rps, rdone = ent[l]
                for fo in range(nfo):
                    k = 4 + 2 * (fo % 2)
                    pe.wait_ge(rdone, b * nfo + (fo if fo >= 2 else 1))
                    for h in range(2):
                        for d in range(nfi):
                            ins = M(ps[:, k + h, 0:HB], weights[:, d, fo * P:(fo + 1) * P], feat[:, d, h * HB:(h + 1) * HB],
                                    start=(d == 0), stop=(d == nfi - 1))
                    ins.then_inc(rps, 1)

            rows, hi, lo, tps, tcopied, rps, rdone = ent[0]
            pe.wait_ge(wr_in, 16)
            pe.wait_ge(fold_dve, 5)
            with pe.Fori(0, NB) as b:
                pe.wait_ge(rows, b * BT + BT)
                pe.wait_ge(tcopied, b + 1)
                for i in range(BT):
                    for f in range(2):
                        c = i * P
                        ins = nc.tensor.transpose(ps[:, 2 * f + c // 512, c % 512:c % 512 + P], urow[:, i, f * P:(f + 1) * P], ident[:, :])
                ins.then_inc(tps, 1)
                pe.wait_ge(tcopied, b + 2)
                products(0, b, 2, 4, wr2)

            def aggregate(l, b, k, width, at_rows=None):
                n = b * PASSES[l] + (FIRST[l] + k)
                hh, hl = halves(width)
                pe.wait_ge(agg[l][0], b * (2 * PASSES[l]) + (2 * k + 1))
                if l == 0:
                    pe.wait_ge(agg[0][2], b * 4 + 1)
                for q in range(NB):
                    pe.wait_ge(chunk_in[q], n * 16 + 16)
                    if l == 0:
                        for i in range(BT):
                            m = q * BT + i
                            pe.wait_ge(ad_sb, b * (NB * BT) + (m if m >= 2 else 1))
                            for s in range(BT):
                                ins = nc.tensor.transpose(ps16[:, 6 + m % 2, s * P:(s + 1) * P], chunk[q][:, s, i * P:(i + 1) * P], ident16[:, :])
                            ins.then_inc(ad_ps, 1)
                        if q == 0:
                            pe.wait_ge(degdone, b + 1)
                        for s in range(BT):
                            for h in range(2):
                                ins = M(ps[:, 4 + h, 0:HB], ones16[:, :], chunk[q][:, s, h * HB:(h + 1) * HB],
                                        start=(q == 0 and s == 0), stop=(q == NB - 1 and s == BT - 1))
                        if q == NB - 1:
                            ins.then_inc(deg, 1)
                    for s in range(BT):
                        t = q * BT + s
                        for f in range(2):
                            for part in (hh, hl):
                                for h in range(2):
                                    ins = M(ps[:, 2 * f + h, 0:HB], part[:, t, (2 * k + f) * P:(2 * k + f + 1) * P], chunk[q][:, s, h * HB:(h + 1) * HB],
                                            start=(t == 0 and part is hh), stop=(t == T - 1 and part is hl))
                    ins.then_inc(chunk_used[q], 1)

            def mean_products(l, b, nfi, nfo):
                mean, ops, odone = agg[l]
                pe.wait_ge(mean, (b + 1) * (2 * PASSES[l]) + 1)
                if l == 0:
                    pe.wait_ge(degdone, b + 2)
                    pe.wait_ge(ad_sb, (b + 1) * (NB * BT) + 1)
                for fo in range(nfo):
                    pe.wait_ge(odone, b * nfo + (fo if fo >= 2 else 1))
                    k = 4 + 2 * (fo % 2)
                    for h in range(2):
                        for d in range(nfi):
                            ins = M(ps[:, k + h, 0:HB], wl2[:, d, fo * P:(fo + 1) * P], feat[:, d, h * HB:(h + 1) * HB],
                                    start=(d == 0), stop=(d == nfi - 1))
                    ins.then_inc(ops, 1)

            def half_scale(k):
                pe.wait_ge(sc_col, k)
                M(ps[0:1, 7, 0:P], sc[:, 2:3], ident[:, :], start=True, stop=True).then_inc(sc_row, 1)
                pe.wait_ge(sc_pow, k)
                M(ps[:, 7, P:P + 1], ones[0:1, :], sc1[:, 2:3], start=True, stop=True).then_inc(sc_all, 1)

            pe.wait_ge(ent[0][1], T + 1)
            pe.wait_ge(ent[0][2], T + 1)
            pe.wait_ge(ent[0][6], NB * 4 + 1)
            pe.wait_ge(wl_in, 16)
            with pe.Fori(0, NB) as b:
                aggregate(0, b, 0, F)
                mean_products(0, b, 2, 4)

            pe.wait_ge(agg[0][2], NB * 4 + 1)
            half_scale(1)
            rows, hi, lo, tps, tcopied, rps, rdone = ent[1]
            pe.wait_ge(wr1_in, 16)
            pe.wait_ge(sc_ready, 1)
            with pe.Fori(0, NB) as b:
                pe.wait_ge(rows, b * 4 + 4)
                for i in range(BT):
                    pe.wait_ge(lo, b * BT + (2 if i == 4 else 1))
                    for f in range(4):
                        ins = nc.tensor.transpose(ps[:, i % 4, f * P:(f + 1) * P], feat[:, f, i * P:(i + 1) * P], ident[:, :])
                    ins.then_inc(tps, 1)
                products(1, b, 4, 4, wr2)
            pe.wait_ge(lo, T + 1)
            pe.wait_ge(rdone, NB * 4 + 1)
            pe.wait_ge(wl1_in, 16)
            with pe.Fori(0, NB) as b:
                aggregate(1, b, 0, HID)
                aggregate(1, b, 1, HID)
                mean_products(1, b, 4, 4)
            rows, hi, lo, tps, tcopied, rps, rdone = ent[2]
            pe.wait_ge(w2_in, 32)
            pe.wait_ge(agg[1][2], NB * 4 + 1)
            with pe.Fori(0, NB) as b:
                pe.wait_ge(rows, b * 4 + 4)
                for i in range(BT):
                    pe.wait_ge(lo, b * BT + (2 if i == 4 else 1))
                    for d in range(4):
                        ins = M(ps[:, i % 4, 0:F], feat[:, d, i * P:(i + 1) * P], wl3[:, d, :], start=(d == 0), stop=(d == 3))
                    ins.then_inc(tps, 1)
                products(2, b, 4, 2, wr3)
            pe.wait_ge(rdone, NB * 2 + 1)
            half_scale(2)
            pe.wait_ge(lo, 2 * T + 1)
            with pe.Fori(0, NB) as b:
                aggregate(2, b, 0, F)
            rows, lo, tps = ent[3]
            pe.wait_ge(agg[2][0], NB * 2 + 1)
            with pe.Fori(0, NB) as b:
                pe.wait_ge(rows, b * 2 + 2)
                for i in range(BT):
                    pe.wait_ge(lo, b * BT + (2 if i == 4 else 1))
                    for f in range(2):
                        ins = nc.tensor.transpose(ps[:, i % 4, f * P:(f + 1) * P], feat[:, f, i * P:(i + 1) * P], ident[:, :])
                    ins.then_inc(tps, 1)

            pe.sem_inc(f_used, BT)
            pe.sem_inc(f_rps, BT)
            pe.sem_inc(conv[1], BT)
            pe.sem_inc(r_tps, BT)
            pe.sem_inc(e_yps, 2)
            pe.wait_ge(f_zero, 1)
            pe.wait_ge(lo, T + 1)
            for k in range(2):
                M(ps[:, 4 + k, :], zero_row[:, 0:P], zero_row, start=True, stop=False)
            M(ps[0:DH, 6, :], zero_row[:, 0:DH], zero_row, start=True, stop=False)

            def f_turn(t, i):
                pe.wait_ge(f_rows, t + 1)
                pe.wait_ge(f_tcp, t + 1)
                for f in range(2):
                    ins = nc.tensor.transpose(ps[:, 7, f * P:(f + 1) * P], urow[:, i, f * P:(f + 1) * P], ident[:, :])
                ins.then_inc(f_tps, 1)

            def f_logits(t, i):
                pe.wait_ge(f_tcp, t + 2)
                pe.wait_ge(f_sub, t + (2 - before(i)))
                for d in range(2):
                    M(ps[:, i % 2, :], feat[:, d, i * P:(i + 1) * P], wxs[:, d, :], start=(d == 0), stop=False)
                M(ps[:, i % 2, :], ones[0:1, :], slice_bias[:, :], start=False, stop=True).then_inc(f_lg, 1)

            def f_tokens(t, i):
                pe.wait_ge(f_sw, t + 1)
                pe.wait_ge(f_swc, t + (3 - before(i)))
                for k in range(2):
                    M(ps[:, 4 + k, :], urow[:, i, k * P:(k + 1) * P], sweight[:, i % 3, :], start=False, stop=False)
                M(ps[0:DH, 6, :], ones[:, 0:DH], sweight[:, i % 3, :], start=False, stop=False)
                for k in range(4):
                    ins = nc.tensor.transpose(ps[:, 2 + i % 2, k * P:(k + 1) * P], sweight[:, i % 3, k * P:(k + 1) * P], ident[:, :])
                ins.then_inc(f_used, 1)

            three_stages(pe.Fori(1, NB), f_turn, f_logits, f_tokens)
            for k in range(2):
                M(ps[:, 4 + k, :], zero_row[:, 0:P], zero_row, start=False, stop=True)
            M(ps[0:DH, 6, :], zero_row[:, 0:DH], zero_row, start=False, stop=True).then_inc(f_pe, 1)

            def head(h):
                return slice(h * G, (h + 1) * G)

            pe.wait_ge(ffn_w, 16 * 7)
            pe.wait_ge(f_dve, 1)
            pe.wait_ge(f_swc, T + 2)
            for h in range(HEADS):
                for d in range(2):
                    M(ps[0:DH, 0, head(h)], wfx[:, d, head(h)], tokT[:, d, head(h)], start=(d == 0), stop=False)
                ins = M(ps[0:DH, 0, head(h)], bfx[:, head(h)], norm[0:1, head(h)], start=False, stop=True)
            ins.then_inc(f_pe, 1)
            pe.wait_ge(f_dve, 2)
            for k in range(2):
                M(ps[0:DH, 1 + k, :], wqkv[:, k, :], slT, start=True, stop=True)
            for h in range(HEADS):
                ins = M(ps[0:DH, 3, head(h)], slT[:, head(h)], wqkv[:, 2, :], start=True, stop=True)
            ins.then_inc(f_pe, 1)
            pe.wait_ge(f_dve, 5)
            for h in range(HEADS):
                ins = M(ps[0:DH, 0, head(h)], qT[:, head(h)], kT[:, head(h)], start=True, stop=True)
            ins.then_inc(f_pe, 1)
            pe.wait_ge(f_dve, 7)
            for h in range(HEADS):
                ins = nc.tensor.transpose(ps[0:DH, 1, head(h)], att[:, head(h)], ident[0:DH, 0:DH])
            ins.then_inc(f_pe, 1)
            pe.wait_ge(f_dve, 8)
            for h in range(HEADS):
                ins = M(ps[0:DH, 2, head(h)], vS[:, head(h)], attT[:, head(h)], start=True, stop=True)
            ins.then_inc(f_pe, 1)
            pe.wait_ge(f_dve, 9)
            for h in range(HEADS):
                c = (h // 2) * F
                ins = M(ps[:, 3 + 2 * (h % 2) + c // 512, c % 512:c % 512 + F], outT[:, (h // 2) * P:(h // 2 + 1) * P], wout[:, h, :], start=True, stop=True)
            ins.then_inc(f_pe, 1)
            pe.wait_ge(f_dve, 11)
            with pe.Fori(0, NB) as b:
                for i in range(BT):
                    pe.wait_ge(f_slot, b * BT + (i + 1))
                    pe.wait_ge(f_x, b * BT + (2 if i == 4 else 1))
                    for k in range(4):
                        ins = M(ps[:, i % 4, 0:F], feat[:, k, i * P:(i + 1) * P], pmat[:, k, :], start=(k == 0), stop=(k == 3))
                    ins.then_inc(f_rps, 1)

            def turned(b, i, rows, tps, tcp, base=0):
                pe.wait_ge(rows, b * BT + (base + i + 1))
                pe.wait_ge(tcp, b * BT + (base + max(i - 1, 0) + 1))
                for f in range(2):
                    ins = nc.tensor.transpose(ps[:, i % 2, f * P:(f + 1) * P], urow[:, i, f * P:(f + 1) * P], ident[:, :])
                ins.then_inc(tps, 1)

            def conv_rows(k):
                rows, tps, tcp, xps, stage, _ = conv
                with pe.Fori(0, NB) as b:
                    for i in range(BT + 1):
                        if i < BT:
                            turned(b, i, rows, tps, tcp, k * T)
                        if i >= 1:
                            j = i - 1
                            pe.wait_ge(tcp, b * BT + (k * T + j + 2))
                            pe.wait_ge(stage, b * BT + (k * T + max(j - 1, 0) + 1))
                            for d in range(2):
                                ins = M(ps[:, 2 + j % 2, 0:F], feat[:, d, j * P:(j + 1) * P], wconv[k][:, d, :], start=(d == 0), stop=(d == 1))
                            ins.then_inc(xps, 1)

            pe.wait_ge(f_x, T + 1)
            pe.wait_ge(conv_w, 16 * 5)
            for c in range(4):
                if c % 2 == 0:
                    conv_rows(c // 2)
                half_scale(3 + c)
                pe.wait_ge(c_lo, (c + 1) * T)
                with pe.Fori(0, NB) as b:
                    pe.wait_ge(c_read, b + (c * NB + 1))
                    for q in range(NB):
                        pe.wait_ge(chunk_in[q], b * 16 + 16 * (FIRST[3] + c * NB + 1))
                        for s in range(BT):
                            t = q * BT + s
                            for i in range(BT):
                                lhs = chunk[q][:, s, i * P:(i + 1) * P]
                                M(ps[:, i, 0:F + 1], lhs, hh1[:, t, 0:F + 1], start=(t == 0), stop=False)
                                ins = M(ps[:, i, 0:F], lhs, hl1[:, t, :], start=False, stop=(t == T - 1))
                        ins.then_inc(chunk_used[q], 1)

            pe.wait_ge(moe_w, 16 * 5)
            pe.wait_ge(c_read, 4 * NB + 1)
            with pe.Fori(0, NB) as b:
                for i in range(BT + 1):
                    if i < BT:
                        turned(b, i, r_rows, r_tps, r_tcp)
                    if i >= 1:
                        j = i - 1
                        pe.wait_ge(r_tcp, b * BT + (j + 2))
                        pe.wait_ge(r_lgc, b * BT + (max(j - 1, 0) + 1))
                        for d in range(2):
                            M(ps[:, 2 + j % 2, 0:EXPERTS], feat[:, d, j * P:(j + 1) * P], wroute[:, d, :], start=(d == 0), stop=False)
                        M(ps[:, 2 + j % 2, 0:EXPERTS], ones[0:1, :], broute, start=False, stop=True).then_inc(r_lg, 1)
            nc.tensor.transpose(ps[:, 6, 0:96], evec_in, ident[0:96, 0:96]).then_inc(r_pe, 1)
            pe.wait_ge(r_dve, 2)
            flat = picked.rearrange("p t e -> p (t e)")
            M(ps[:, 4, 0:T * EXPERTS], tri[:, :], flat, start=True, stop=True)
            M(ps[:, 5, 0:T * EXPERTS], ones[:, :], flat, start=True, stop=True).then_inc(r_pe, 1)
            pe.wait_ge(r_dve, 5)
            pe.wait_ge(r_act, 2)

            def turn_rows(c, s):
                pe.wait_ge(e_in[s], c)
                for i in range(CT):
                    for d in range(2):
                        ins = nc.tensor.transpose(ps[:, 6 + s, d * CAP + i * P:d * CAP + (i + 1) * P], xin[s][:, i, d * P:(d + 1) * P], ident[:, :])
                ins.then_inc(e_tps, 1)

            def hidden(xe, gelu, wi, s):
                pe.wait_ge(w1_in[s], wi)
                pe.wait_ge(e_xe, xe)
                for k in range(EK):
                    if k >= 4:
                        pe.wait_ge(e_gelu, gelu + (k - 3))
                    for d in range(2):
                        ins = M(ps[:, k % 4, 0:CAP], w1e[s][:, d, k * P:(k + 1) * P], xeT[s][:, d, :], start=(d == 0), stop=(d == 1))
                    ins.then_inc(e_hps, 1)

            def outputs(gelu, y, wi, s):
                pe.wait_ge(w2e_in[s], wi)
                pe.wait_ge(e_gelu, gelu)
                pe.wait_ge(e_y, y)
                for i in range(CT):
                    for k in range(EK):
                        ins = M(ps[:, 4 + s, i * F:(i + 1) * F], hT[s][:, k, i * P:(i + 1) * P], w2e[s][:, k, :], start=(k == 0), stop=(k == EK - 1))
                ins.then_inc(e_yps, 1)

            turn_rows(32, 0)
            hidden(2, 1, 16, 0)
            with pe.Fori(0, CHUNKS // 2 - 1) as g:
                turn_rows(g * 32 + 32, 1)
                outputs(g * (2 * EK) + (EK + 1), g * 2 + 1, g * 32 + 32, 0)
                hidden(g * 4 + 4, g * (2 * EK) + (EK + 1), g * 16 + 16, 1)
                turn_rows(g * 32 + 64, 0)
                outputs(g * (2 * EK) + (2 * EK + 1), g * 2 + 2, g * 32 + 32, 1)
                hidden(g * 4 + 6, g * (2 * EK) + (2 * EK + 1), g * 16 + 32, 0)
            turn_rows(32 * (CHUNKS // 2), 1)
            outputs((CHUNKS - 1) * EK + 1, CHUNKS - 1, 32 * (CHUNKS // 2), 0)
            hidden(2 * CHUNKS, (CHUNKS - 1) * EK + 1, 16 * (CHUNKS // 2), 1)
            outputs(CHUNKS * EK + 1, CHUNKS, 32 * (CHUNKS // 2), 1)


_INS = ["x", "src", "dst"]


def kernel(**inputs):
    import numpy as _np
    import concourse.bacc as _bacc
    from concourse import mybir as _mybir
    from concourse.bass_utils import run_bass_kernel_spmd as _run

    nc = _bacc.Bacc("TRN2", target_bir_lowering=False, num_devices=1)
    arrays, aps = {}, {}
    for name, value in inputs.items():
        a = _np.ascontiguousarray(value)
        arrays[name] = a
        aps[name] = nc.dram_tensor(name, a.shape, _mybir.dt.from_np(a.dtype), kind="ExternalInput").ap()
    out = nc.dram_tensor("out", (N, F), _mybir.dt.float32, kind="ExternalOutput").ap()
    weights = {k: v for k, v in aps.items() if k not in _INS}
    build(nc, aps["x"], aps["src"], aps["dst"], weights, out)
    r = _run(nc, [arrays], core_ids=[0])
    return r.results[0]["out"]
```

```python
import concourse.bass as bass
from concourse import mybir
from contextlib import ExitStack, contextmanager

P = 128
N = 3125
EDGES = 53125
F = 256
HID = 512
T = -(-N // P)
TAIL = N - (T - 1) * P
BT = 5
NB = T // BT
BC = BT * P
HB = BC // 2
EC = -(-EDGES // P)
GQ = 8
GE = GQ * P
NG = EC // GQ
LOOK = 4
AROW = T * BC
ASIZE = NB * P * AROW
EPS = 1e-5
LN_SCALE = 1024.0
BN_BOUND = 56.0
HEADS, DH, G = 8, 64, 64
EXPERTS, EH = 8, 1024
CAP = 256
CHUNKS = (2 * N + EXPERTS * (CAP - 1)) // CAP
SLOTS = CHUNKS * CAP
W = F + 2
TZ = 16
TR = SLOTS // TZ
CT = CAP // P
EK = EH // P
EV = EK + 4
fp32, fp16, i32, u32 = mybir.dt.float32, mybir.dt.float16, mybir.dt.int32, mybir.dt.uint32
ALU, ACT, AX = mybir.AluOpType, mybir.ActivationFunctionType, mybir.AxisListType


class Order:

    def __init__(self, eng, sem):
        self.eng, self.sem, self.base, self.n, self.turn, self.per = eng, sem, 0, 0, None, 0

    def mark(self, ins):
        ins.then_inc(self.sem, 1)
        self.n += 1

    def settle(self):
        if self.turn is None:
            self.eng.wait_ge(self.sem, self.base + self.n)
        else:
            self.eng.wait_ge(self.sem, self.turn * self.per + (self.base + self.n))

    @contextmanager
    def loop(self, count, per):
        self.base, self.n = self.base + self.n, 0
        with self.eng.Fori(0, count) as i:
            self.turn, self.per = i, per
            yield i
            assert self.n == per, (self.n, per)
        self.base, self.n, self.turn = self.base + count * per, 0, None

    @contextmanager
    def loop_from(self, first, end, per):
        self.base, self.n = self.base + self.n - first * per, 0
        with self.eng.Fori(first, end) as i:
            self.turn, self.per = i, per
            yield i
            assert self.n == per, (self.n, per)
        self.base, self.n, self.turn = self.base + end * per, 0, None


def build(nc, x, src, dst, w, out):
    ctx = ExitStack()
    with ctx:
        def sb(name, shape, dt=fp32):
            return ctx.enter_context(nc.sbuf_tensor(name, shape, dt))

        def sem(name):
            return ctx.enter_context(nc.semaphore(name))

        def dram(name, shape, dt):
            return nc.dram_tensor(name, shape, dt, kind="Internal").ap()

        def runs(ap, **k):
            return ap.rearrange("p (a b) -> p a b", **k)

        at_flat = dram("at_counts", (ASIZE + GE, 1), fp16)
        ad_flat = dram("ad_counts", (ASIZE, 1), fp16)
        at = at_flat[0:ASIZE, :].rearrange("(b p r) a -> p b (r a)", b=NB, p=P)
        ad = ad_flat.rearrange("(b p r) a -> p b (r a)", b=NB, p=P)
        key_rows = dram("key_rows", (EC * P,), fp32)
        tok_in = dram("tok_in", (SLOTS + 2 * P, W), fp32)
        x_sum = dram("x_sum", (T * P + TR, F), fp32)
        evec_rows = dram("expert_vectors", (EXPERTS, P, EV), fp32)

        ring = sb("ring", [P, 8192])
        harena = sb("harena", [P, 12864])
        tarena = sb("tarena", [P, 4 * T * P + 2 * T])
        xrows = sb("xrows", [P, T, F])
        wl = sb("wl", [P, 2048])
        wr = sb("wr", [P, 2048])
        feat = sb("feat", [P, 4, BC])
        late = sb("late", [P, T * P])
        wxs = sb("wxs", [P, 2, HID])
        ident = sb("ident", [P, P])
        ident16 = sb("ident16", [P, P], fp16)
        ones = sb("ones", [P, P])
        ones16 = sb("ones16", [P, P], fp16)
        tri = sb("tri", [P, P])
        ln_st = sb("ln_st", [P, T, 6])
        ln_mv = sb("ln_mv", [P, T, 2])
        ln_r = sb("ln_r", [P, T])
        ln_s = sb("ln_s", [P, T])
        rowmask = sb("rowmask", [P, T])
        bn_st = sb("bn_st", [P, 4, 2 * NB, 6])
        bn_mv = sb("bn_mv", [P, 4, 2])
        bn_k = sb("bn_k", [P, 4, 4])
        vec = [sb(f"vec{l}", [P, 3, 4]) for l in range(3)]
        amax = sb("amax", [P, T])
        sc = sb("sc", [P, 4])
        sc1 = sb("sc1", [1, 4])
        slice_bias = sb("slice_bias", [1, HID])

        chunk = [ring[:, :].bitcast(fp16)[:, q * BT * BC:(q + 1) * BT * BC].rearrange("p (s c) -> p s c", s=BT)
                 for q in range(NB)]
        chunk_flat = [ring[:, :].bitcast(fp16)[:, q * BT * BC:(q + 1) * BT * BC] for q in range(NB)]
        h16 = harena[:, :].bitcast(fp16)

        def halves(d):
            return (runs(h16[:, 0:T * d], a=T), runs(h16[:, T * d:2 * T * d], a=T))

        tfeat = tarena[:, 0:4 * T * P].rearrange("p (f n) -> p f n", f=4)
        zeros16 = tarena[:, :].bitcast(fp16)[:, 0:AROW]
        deginv = late[:, :]
        ps = ctx.enter_context(nc.psum_tensor("ps", [P, 8, 512], fp32))
        ps16 = ps[:, :, :].bitcast(fp16)

        astore = [harena[:, 6432 + s * 1600:6432 + (s + 1) * 1600].bitcast(fp16).rearrange("p (i c) -> p i c", i=BT) for s in range(2)]

        eint = harena[:, 6432:6432 + 3 * EC].bitcast(i32).rearrange("p (a c) -> p a c", a=3)
        eflt = harena[:, 7680:7680 + 4 * EC].rearrange("p (a c) -> p a c", a=4)
        keyT = harena[0:EC // GQ, 9344:9344 + GE]
        ekey = ring[:, 0:EC]
        espare = ring[:, EC:2 * EC]
        eweight = ring[:, 832:832 + 2 * GE - P]
        krow = ring[:, 2752:2752 + LOOK * GE].rearrange("p (a c) -> p a c", a=LOOK)
        ejunk = [late[:, q * GE // 2:(q + 1) * GE // 2].bitcast(fp16) for q in range(6)] + [
            ring[:, 6848 + q * GE // 2:6848 + (q + 1) * GE // 2].bitcast(fp16) for q in range(GQ - 6)]
        ecount = ring[:, 7872:7872 + 4 * GQ].rearrange("p (a c) -> p a c", a=4)
        eshift = ring[:, 7904:7904 + 4 * GQ].rearrange("p (a c) -> p a c", a=4)
        eidx = ring[:, 7936:7936 + 4 * GQ].bitcast(i32).rearrange("p (a c) -> p a c", a=4)
        evalue = ring[:, 7968:7968 + 4 * GQ].bitcast(fp16)[:, 0:4 * GQ].rearrange("p (a c) -> p a c", a=4)
        etrash_i = ring[:, 8000:8000 + GQ].bitcast(i32)
        etrash = ring[:, 8008:8008 + GQ]
        tok_empty = runs(harena[:, 10400:10400 + TR // P * W], a=TR // P)
        wx_in = tarena[:, 8192:8192 + 2 * HID].rearrange("p (a c) -> p a c", a=2)
        wxT = tarena[0:DH, 9216:9216 + HEADS * F].rearrange("p (h d) -> p h d", h=HEADS)
        wsl = tarena[0:DH, 11264:11264 + G]
        bxT = tarena[0:DH, 11328:11328 + HEADS]
        temp_row = tarena[0:1, 11336:11336 + HEADS]
        rtemp = tarena[:, 11344:11344 + HEADS]
        bsl_row = tarena[0:1, 11352:11352 + G]
        bias_raw = tarena[0:1, 11416:11416 + HID]

        wl2 = wl[:, :].rearrange("p (d f) -> p d f", f=HID)
        wr2 = wr[:, :].rearrange("p (d f) -> p d f", f=HID)
        wr3 = wr[:, 0:1024].rearrange("p (d f) -> p d f", f=F)
        wl3 = wr[:, 1024:2048].rearrange("p (d f) -> p d f", f=F)
        urow = feat[:, 2:4, :].rearrange("p a b -> p (a b)").rearrange("p (t c) -> p t c", c=F)

        logit = harena[:, 10240:10240 + 3 * HID].rearrange("p (s c) -> p s c", s=3)
        sweight = harena[:, 0:3 * HID].rearrange("p (s c) -> p s c", s=3)
        tokT = harena[:, 2048:2048 + 2 * HID].rearrange("p (d c) -> p d c", d=2)
        norm = harena[0:DH, 3072:3072 + HID]
        rnorm = harena[0:DH, 3584:3584 + HID]
        slT, qT, kT, vS, att, attT, outT = (harena[0:DH, 4096 + k * HID:4096 + (k + 1) * HID] for k in range(7))
        pmat = harena[:, 7680:7680 + 4 * F].rearrange("p (k o) -> p k o", k=4)
        wqkv = harena[0:DH, 8704:8704 + 3 * DH].rearrange("p (k c) -> p k c", k=3)
        bfx = harena[0:1, 8896:8896 + HID]
        hmax = harena[:, 11776:11776 + 3 * HEADS].rearrange("p (s h) -> p s h", s=3)
        hsum = harena[:, 11800:11800 + 3 * HEADS].rearrange("p (s h) -> p s h", s=3)
        hrec = harena[:, 11824:11824 + 3 * HEADS].rearrange("p (s h) -> p s h", s=3)
        bout = harena[:, 9472:9472 + F]
        bias_rep = harena[:, 11848:11848 + HID]
        weight_sum = late[:, 2600:2600 + HID]
        zero_row = harena[0:1, 9728:9728 + HID]
        wout = wl[0:DH, :].rearrange("p (h o) -> p h o", h=HEADS)
        wfx = wr[:, 0:1024].rearrange("p (d c) -> p d c", d=2)
        wconv = [wr[:, 1024 + k * 512:1536 + k * 512].rearrange("p (d c) -> p d c", d=2) for k in range(2)]
        bconv = [late[:, k * F:(k + 1) * F] for k in range(2)]
        slope = late[:, 512:513]
        rdeg = late[:, 520:520 + BT]
        rows2 = tarena[:, 0:T * F].rearrange("p (t c) -> p t c", t=T)
        zrows, negrows = (runs(harena[:, T * (F + 2) // 2 + k * BT * F:T * (F + 2) // 2 + (k + 1) * BT * F], a=BT) for k in range(2))
        urows = runs(harena[:, 0:BT * F], a=BT)
        conv_halves = []
        for k in range(2):
            c0 = k * T * (2 * F + 2)
            conv_halves.append((runs(h16[:, c0:c0 + T * (F + 2)], a=T), runs(h16[:, c0 + T * (F + 2):c0 + T * (2 * F + 2)], a=T)))
        w3square, w3norm = sc[:, 3:4], amax[:, T - 1:T]
        wsquare = late[:, 530:532]
        wnorm = late[:, 532:534]
        wroute = late[:, 600:600 + 2 * EXPERTS].rearrange("p (d e) -> p d e", d=2)
        broute = late[0:1, 616:616 + EXPERTS]
        evec_in = late[0:96, 640:640 + P]
        evec = late[:, 768:768 + 96]
        xn = runs(tarena[:, T * F:T * F + T * W], a=T)
        w1e = [ring[:, s * 4096:s * 4096 + 2048].rearrange("p (d h) -> p d h", d=2) for s in range(2)]
        w2e = [ring[:, s * 4096 + 2048:(s + 1) * 4096].rearrange("p (k o) -> p k o", k=EK) for s in range(2)]
        hT = [harena[:, s * 2048:(s + 1) * 2048].rearrange("p (k n) -> p k n", k=EK) for s in range(2)]
        xin = [runs(harena[:, 4096 + s * CT * W:4096 + (s + 1) * CT * W], a=CT) for s in range(2)]
        xeT = [runs(harena[:, 5140 + s * 2 * CAP:5140 + (s + 1) * 2 * CAP], a=2) for s in range(2)]
        yrow = [runs(harena[:, 6170 + s * CT * F:6170 + (s + 1) * CT * F], a=CT) for s in range(2)]
        b2e = [harena[:, 7200 + s * F:7200 + (s + 1) * F] for s in range(2)]
        evc = [harena[:, 7712 + s * EV:7712 + (s + 1) * EV] for s in range(2)]
        node_weight = [runs(harena[:, 7740 + s * 2 * CT:7740 + (s + 1) * 2 * CT], a=CT) for s in range(2)]
        ids = harena[0:1, 7760:7760 + CHUNKS].bitcast(i32)
        lgt = late[:, 1540:1540 + T * EXPERTS].rearrange("p (t e) -> p t e", t=T)
        pri, sel1, sel2, picked, count, place, seg_start = (
            harena[:, 8000 + k * T * EXPERTS:8000 + (k + 1) * T * EXPERTS].rearrange("p (t e) -> p t e", t=T) for k in range(7))
        top1, top2, gate1, gate2, first, trash = (harena[:, 9600 + k * T:9600 + (k + 1) * T] for k in range(6))
        slot_at, slot_in = (harena[:, 9760 + k * 2 * T:9760 + (k + 1) * 2 * T].rearrange("p (k t) -> p k t", k=2) for k in range(2))
        slot_in = slot_in.bitcast(i32)
        trash_i = harena[:, 9920:9921].bitcast(i32)
        rank, total, ends, starts = (harena[:, 9928 + k * EXPERTS:9928 + (k + 1) * EXPERTS] for k in range(4))
        chunks_i = harena[:, 9960:9960 + EXPERTS].bitcast(i32)
        chunk_no_i = harena[0:1, 9968:9968 + CHUNKS].bitcast(i32)
        chunk_no, chunk_of = harena[0:1, 10000:10000 + CHUNKS], harena[0:1, 10032:10032 + CHUNKS]
        passed = harena[0:1, 10064:10064 + CHUNKS * EXPERTS].rearrange("p (c e) -> p c e", c=CHUNKS)

        consts_ready, filled, edges_in, x_in, zero_ready, zeroed, vec_in = map(sem, (
            "consts_ready", "filled", "edges_in", "x_in", "zero_ready", "zeroed", "vec_in"))
        fold_in, fold_pe, fold_dve = map(sem, ("fold_in", "fold_pe", "fold_dve"))
        keyT_psum, keyT_ready, key_ready, key_stored = map(sem, ("keyT_psum", "keyT_ready", "key_ready", "key_stored"))
        krow_in = [sem(f"krow_in{s}") for s in range(LOOK)]
        compared, idx_ready, scattered = map(sem, ("compared", "idx_ready", "scattered"))
        chunk_in = [sem(f"chunk_in{q}") for q in range(NB)]
        chunk_used = [sem(f"chunk_used{q}") for q in range(NB)]
        wr_in, wl_in, wr1_in, wl1_in, w2_in = map(sem, ("wr_in", "wl_in", "wr1_in", "wl1_in", "w2_in"))
        dve_order, pool_order = sem("dve_order"), sem("pool_order")
        ln_var, ln_std, bn_done = map(sem, ("ln_var", "ln_std", "bn_done"))
        sc_col, sc_row, sc_pow, sc_all, sc_ready = map(sem, ("scale_columns", "scale_across", "scale_power", "scale_spread", "scale_ready"))
        ad_ps, ad_sb = sem("ad_transposed"), sem("ad_copied")
        ad_out = [sem(f"ad_stored{s}") for s in range(2)]

        def fresh(tag, *names):
            return [sem(f"{tag}_{n}") for n in names]

        ent = [fresh(f"in{l}", "rows", "hi", "lo", "tps", "tcopied", "rps", "rdone") for l in range(3)] + [fresh("in3", "rows", "lo", "tps")]
        agg = [fresh(f"agg{l}", "mean", "ops", "odone") for l in range(3)]
        deg, degdone = fresh("agg0", "deg", "degdone")
        first_summed = sem("first_features_summed")

        ffn_w, conv_w, moe_w = sem("ffn_weights_in"), sem("conv_weights_in"), sem("moe_weights_in")
        f_zero, f_rows, f_tps, f_tcp, f_lg, f_sub, f_exp, f_sw, f_used, f_swc = fresh(
            "ffn", "zeros", "rows", "transposed", "copied", "logits", "shifted", "exps", "weights", "weights_used", "weightsT_copied")
        f_pe, f_dve, f_act, f_bias, f_sum, f_slot, f_rps, f_x = fresh("ffn", "pe", "dve", "act", "bias_added", "weights_summed", "slots_filled", "out_rows", "x")
        conv = fresh("conv_entry", "rows", "transposed", "copied", "products", "hi", "lo")
        c_bank, c_ones, c_square, c_norm, c_sum, c_deg, c_hi, c_read, c_h, c_x = fresh(
            "conv", "bank_summed", "ones", "squares", "norms", "squares_summed", "degrees", "hi", "sums_read", "hidden", "x")
        r_rows, r_tps, r_tcp, r_lg, r_lgc = fresh("route", "rows", "transposed", "copied", "logits", "logits_copied")
        r_dve, r_pe, r_act, r_trash = fresh("route", "dve", "pe", "act", "trash")
        e_vec_out, tok_zeroed, e_xn, tok_sorted = fresh("expert", "vectors_stored", "rows_zeroed", "rows", "rows_sorted")
        e_in = [sem(f"chunk_rows_in{s}") for s in range(2)]
        w1_in = [sem(f"expert_W1_in{s}") for s in range(2)]
        w2e_in = [sem(f"expert_W2_in{s}") for s in range(2)]
        e_tps, e_xe, e_hps, e_gelu, e_yps, e_b, e_y = fresh("expert", "transposed", "inputs", "hidden", "gelus", "outputs", "biased", "rows_out")
        e_n = sem("expert_weights")
        x_base, y_added, y_used, out_stored = fresh("moe", "x_stored", "rows_added", "rows_used", "out_stored")
        block = ctx.enter_context(nc.Block())

        def nodes(b):
            return bass.ds(b * BC, BC)

        def two(ap):
            return ap.rearrange("p (h c) -> p h c", h=2)

        def three_stages(blocks, first, second, third, third_early=False):
            def turn(t, i):
                first(t, i)
                if third_early and (not isinstance(t, int) or t >= 2):
                    third(t - 2, (i - 2) % BT)
                if not isinstance(t, int) or t >= 1:
                    second(t - 1, (i - 1) % BT)
                if not third_early and (not isinstance(t, int) or t >= 2):
                    third(t - 2, (i - 2) % BT)

            for t in range(BT):
                turn(t, t)
            with blocks as b:
                for i in range(BT):
                    turn(b * BT + i, i)
            if third_early:
                third(T - 2, BT - 2)
            second(T - 1, BT - 1)
            if not third_early:
                third(T - 2, BT - 2)
            third(T - 1, BT - 1)

        def nothing(t, i):
            pass

        def before(i):
            return 2 if i >= 1 else 1

        DIMS = [(2, 4), (4, 4), (4, 2)]
        PASSES = [1, 2, 1]
        FIRST = [0, NB, 3 * NB, 4 * NB]

        @block.sync
        def _(sp):
            sp.wait_ge(filled, 2)
            cut = (P - 1) * EC
            for a, e in ((0, src), (1, dst)):
                for p0, p1 in ((0, 112), (112, P - 1)):
                    sp.dma_start(eint[p0:p1, a, :], e[p0 * EC:p1 * EC].rearrange("(p c) -> p c", c=EC)).then_inc(edges_in, 16)
                sp.dma_start(eint[P - 1:P, a, 0:EDGES - cut], e[cut:EDGES].rearrange("(p c) -> p c", p=1)).then_inc(edges_in, 16)
            sp.dma_start(xrows[:, 0:T - 1, :], x[0:(T - 1) * P, :].rearrange("(t p) d -> p t d", p=P)).then_inc(x_in, 16)
            sp.dma_start(xrows[0:TAIL, T - 1, :], x[(T - 1) * P:N, :]).then_inc(x_in, 16)
            sp.wait_ge(keyT_ready, 1)
            sp.dma_start(key_rows.rearrange("(q r n) -> r q n", q=GQ, n=P), keyT.rearrange("r (q n) -> r q n", q=GQ)).then_inc(key_stored, 16)
            sp.wait_ge(key_stored, 16)
            for s in range(LOOK):
                sp.dma_start(krow[:, s, :], key_rows[s * GE:(s + 1) * GE].partition_broadcast(P)).then_inc(krow_in[s], 16)
            sp.wait_ge(consts_ready, 1)
            tok_pieces = tok_in[0:SLOTS, :].rearrange("(z p r) d -> p z (r d)", z=TZ, p=P)

            def clear_rows(z):
                sp.dma_start(tok_pieces[:, z, :].rearrange("p o e -> p (o e)"), tok_empty.rearrange("p r d -> p (r d)")).then_inc(tok_zeroed, 16)

            with sp.Fori(0, NG // LOOK - 1) as i:
                for s in range(LOOK):
                    sp.wait_ge(compared, LOOK * i + (s + 1))
                    sp.dma_start(krow[:, s, :], key_rows[bass.ds(i * (LOOK * GE) + (s + LOOK) * GE, GE)].partition_broadcast(P)).then_inc(krow_in[s], 16)
                clear_rows(bass.ds(i, 1))
            for z in range(NG // LOOK - 1, TZ):
                clear_rows(bass.ds(z, 1))
            sp.wait_ge(scattered, NG * GQ * 16)

            def load_chunks(table, b, done):
                for q in range(NB):
                    sp.wait_ge(chunk_used[q], done)
                    sp.dma_start(chunk_flat[q], table[:, bass.ds(b, 1), q * BT * BC:(q + 1) * BT * BC].rearrange("p o e -> p (o e)")).then_inc(chunk_in[q], 16)

            for l in range(3):
                with sp.Fori(0, NB) as b:
                    for k in range(PASSES[l]):
                        load_chunks(at, b, b * PASSES[l] + (FIRST[l] + k + 1))
            for s, n in ((0, 3), (1, 2)):
                sp.wait_ge(ad_out[s], 16 * (n * NB + 1))
            for c in range(4):
                with sp.Fori(0, NB) as b:
                    load_chunks(at if c % 2 == 0 else ad, b, b + (FIRST[3] + c * NB + 1))
            for q in range(NB):
                sp.wait_ge(chunk_used[q], FIRST[3] + 4 * NB + 1)
            sp.wait_ge(r_act, 2)
            for k0, k1, c0 in ((0, EK, 0), (EK, EK + 2, 64), (EK + 2, EV, 80)):
                sp.dma_start(evec_rows[:, :, k0:k1].rearrange("e p k -> p e k"),
                             evec[:, c0:c0 + EXPERTS * (k1 - k0)].rearrange("p (e k) -> p e k", e=EXPERTS), allow_slow_non_contiguous=True).then_inc(e_vec_out, 16)
            sp.wait_ge(e_vec_out, 16 * 3)
            sp.wait_ge(c_x, NB)
            sp.dma_start(x_sum[0:T * P, :].rearrange("(t p) d -> p t d", p=P), xrows[:, :, :]).then_inc(x_base, 16)
            sp.dma_start(x_sum[T * P:, :].rearrange("(t p) d -> p t d", p=P), xrows[:, 0:TR // P, :]).then_inc(x_base, 16)
            sp.wait_ge(r_dve, 3)
            def load_rows(c, s):
                e = bass.ds(sp.value_load(ids[:, bass.ds(c, 1)], min_val=0, max_val=EXPERTS - 1), 1)
                sp.dma_start(w1e[s], w["L1_ffn_W1"][e, :, :].rearrange("e (d p) h -> p (e d) h", p=P)).then_inc(w1_in[s], 16)
                sp.dma_start(evc[s], evec_rows[e, :, :].rearrange("e p k -> p (e k)")).then_inc(e_in[s], 16)
                if isinstance(c, int) and c == 0:
                    sp.wait_ge(tok_sorted, 16 * 2 * T)
                sp.dma_start(xin[s], tok_in[bass.ds(c * CAP, CAP), :].rearrange("(i p) d -> p i d", p=P)).then_inc(e_in[s], 16)
                return e

            def load_second(e, s):
                sp.dma_start(w2e[s], w["L1_ffn_W2"][e, :, :].rearrange("e (k p) o -> p (e k) o", p=P)).then_inc(w2e_in[s], 16)
                sp.dma_start(b2e[s], w["L1_ffn_b2"][e, :].rearrange("e o -> (e o)").partition_broadcast(P)).then_inc(w2e_in[s], 16)

            for s in range(2):
                load_second(load_rows(s, s), s)
            with sp.Fori(1, CHUNKS // 2) as g:
                for s in range(2):
                    sp.wait_ge(e_gelu, g * (2 * EK) + (s * EK - EK + 1))
                    sp.nop(nofuse=True)
                    e = load_rows(g * 2 + s, s)
                    sp.wait_ge(e_y, g * 2 + (s + 1))
                    sp.nop(nofuse=True)
                    load_second(e, s)
            sp.wait_ge(y_used, CHUNKS + 2)
            for b in range(NB):
                r = slice(b * BC, min((b + 1) * BC, N))
                sp.dma_start(out[r, :], x_sum[r, :]).then_inc(out_stored, 16)
            sp.wait_ge(out_stored, 16 * NB)

        @block.gpsimd
        def _(pool):
            o = Order(pool, pool_order)
            nc.gpsimd.memset(eint[:, 0:2, :], T * P - 1).then_inc(filled, 1)
            nc.gpsimd.memset(xrows[:, T - 1, :], 0.0).then_inc(filled, 1)
            for q in range(NB):
                pool.sem_inc(chunk_used[q], 1)
            o.mark(nc.gpsimd.memset(ident[:, :], 0.0))
            o.mark(nc.gpsimd.memset(tri[:, :], 1.0))
            o.mark(nc.gpsimd.memset(rowmask[:, :], 1.0))
            o.mark(nc.gpsimd.memset(eweight, float(GE + 1)))
            o.mark(nc.gpsimd.memset(ones[:, :], 1.0))
            o.mark(nc.gpsimd.memset(ones16[:, :], 1.0))
            o.mark(nc.gpsimd.memset(tok_empty, 0.0))
            o.mark(nc.gpsimd.iota(etrash_i, pattern=[[P, GQ]], base=ASIZE, channel_multiplier=1))
            o.settle()
            o.mark(nc.gpsimd.affine_select(out=ident[:, :], in_=ident[:, :], compare_op=ALU.not_equal, fill=1.0, base=0,
                                           pattern=[[-1, P]], channel_multiplier=1))
            o.mark(nc.gpsimd.affine_select(out=tri[:, :], in_=tri[:, :], compare_op=ALU.is_gt, fill=0.0, base=0,
                                           pattern=[[1, P]], channel_multiplier=-1))
            o.mark(nc.gpsimd.affine_select(out=rowmask[:, T - 1:T], in_=rowmask[:, T - 1:T], compare_op=ALU.is_gt, fill=0.0,
                                           base=TAIL, pattern=[[0, 1]], channel_multiplier=-1))
            o.mark(nc.gpsimd.iota(tok_empty[:, :, F].bitcast(i32), pattern=[[1, TR // P]], base=T * P, channel_multiplier=TR // P))
            o.mark(nc.gpsimd.affine_select(out=eweight, in_=eweight, compare_op=ALU.is_gt, fill=1.0, base=GE - P,
                                           pattern=[[-1, 2 * GE - P]], channel_multiplier=1))
            o.settle()
            nc.gpsimd.tensor_copy(ident16[:, :], ident[:, :]).then_inc(consts_ready, 1)
            pool.wait_ge(zeroed, 16 * (NB + 1))
            with pool.Fori(0, NG // LOOK) as i:
                for s in range(LOOK):
                    pool.wait_ge(idx_ready, LOOK * i + (s + 1))
                    pool.nop(nofuse=True)
                    for q in range(GQ):
                        nc.gpsimd.indirect_dma_start(
                            out=at_flat, out_offset=bass.IndirectOffsetOnAxis(ap=eidx[:, s, q:q + 1], axis=0),
                            in_=evalue[:, s, q:q + 1], in_offset=None, compute_op=ALU.add).then_inc(scattered, 16)
                    pool.wait_ge(scattered, i * (LOOK * GQ * 16) + (s + 1) * (GQ * 16))
            pool.wait_ge(ent[0][5], NB * 4 + 1)
            pool.dma_start(wr2, w["L0_gnn_Wr1"].rearrange("(d p) f -> p d f", p=P)).then_inc(wr1_in, 16)
            pool.wait_ge(agg[0][1], NB * 4 + 1)
            pool.dma_start(wl2, w["L0_gnn_Wl1"].rearrange("(d p) f -> p d f", p=P)).then_inc(wl1_in, 16)
            pool.wait_ge(ent[1][5], NB * 8 + 1)
            pool.dma_start(wr3, w["L0_gnn_Wr2"].rearrange("(d p) f -> p d f", p=P)).then_inc(w2_in, 16)
            pool.dma_start(wl3, w["L0_gnn_Wl2"].rearrange("(d p) f -> p d f", p=P)).then_inc(w2_in, 16)
            pool.wait_ge(chunk_used[NB - 1], FIRST[3] + 1)
            pool.wait_ge(agg[2][0], 2 * NB + 2)
            pool.dma_start(wout, w["L0_ffn_W_out"].rearrange("(h c) o -> c h o", c=DH)).then_inc(ffn_w, 16)
            pool.dma_start(wfx, w["L0_ffn_W_fx"].rearrange("(d p) f -> p d f", p=P)).then_inc(ffn_w, 16)
            for k, name in enumerate("qkv"):
                pool.dma_start(wqkv[:, k, :], w[f"L0_ffn_W_{name}"]).then_inc(ffn_w, 16)
            pool.dma_start(bfx, w["L0_ffn_b_fx"].rearrange("(a c) -> a c", a=1)).then_inc(ffn_w, 16)
            pool.dma_start(bout, w["L0_ffn_b_out"].partition_broadcast(P)).then_inc(ffn_w, 16)
            for k in range(2):
                pool.dma_start(wconv[k], w[f"L1_gnn_W{k + 1}"].rearrange("(d p) f -> p d f", p=P)).then_inc(conv_w, 16)
                pool.dma_start(bconv[k], w[f"L1_gnn_b{k + 1}"].partition_broadcast(P)).then_inc(conv_w, 16)
            pool.dma_start(slope, w["L1_gnn_a"].partition_broadcast(P)).then_inc(conv_w, 16)
            pool.dma_start(wroute, w["L1_ffn_Wr"].rearrange("(d p) e -> p d e", p=P)).then_inc(moe_w, 16)
            pool.dma_start(broute, w["L1_ffn_br"].rearrange("(a e) -> a e", a=1)).then_inc(moe_w, 16)
            pool.dma_start(evec_in[0:64, :], w["L1_ffn_b1"].rearrange("e (k p) -> (e k) p", p=P)).then_inc(moe_w, 16)
            pool.dma_start(evec_in[64:80, :], w["L1_ffn_ln_g"].rearrange("e (d p) -> (e d) p", p=P)).then_inc(moe_w, 16)
            pool.dma_start(evec_in[80:96, :], w["L1_ffn_ln_b"].rearrange("e (d p) -> (e d) p", p=P)).then_inc(moe_w, 16)
            nc.gpsimd.memset(weight_sum, 0.0).then_inc(f_sum, 1)
            with pool.Fori(0, NB) as b:
                for i in range(BT):
                    pool.wait_ge(f_sw, b * BT + (i + 1))
                    pool.wait_ge(f_sum, b * BT + (i + 1))
                    pool.nop(nofuse=True)
                    nc.gpsimd.tensor_tensor(weight_sum, weight_sum, sweight[:, i % 3, :], ALU.add).then_inc(f_sum, 1)
            pool.wait_ge(ffn_w, 16 * 7)
            nc.gpsimd.tensor_tensor(xrows[:, :, :], xrows[:, :, :], bout.unsqueeze(1).to_broadcast([P, T, F]), ALU.add).then_inc(f_bias, 1)
            rows, tps = conv[0:2]
            pool.wait_ge(c_h, NB)
            with pool.Fori(0, NB) as b:
                for i in range(BT):
                    pool.wait_ge(tps, b * BT + (T + i + 1))
                    pool.nop(nofuse=True)
                    nc.gpsimd.tensor_copy(urow[:, i:i + 1, :], rows2[:, bass.ds(b * BT + i, 1), :]).then_inc(rows, 1)
            pool.wait_ge(c_x, NB)
            o.mark(nc.gpsimd.iota(trash_i, pattern=[[0, 1]], base=SLOTS, channel_multiplier=1))
            o.mark(nc.gpsimd.iota(xn[:, :, F].bitcast(i32), pattern=[[P, T]], base=0, channel_multiplier=1))
            nc.gpsimd.iota(chunk_no_i, pattern=[[1, CHUNKS]], base=0, channel_multiplier=0).then_inc(r_trash, 1)
            o.settle()
            pool.wait_ge(e_xn, T)
            pool.wait_ge(tok_zeroed, 16 * TZ)
            for k in range(2):
                pool.wait_ge(r_dve, 5 + k)
                for t in range(T):
                    nc.gpsimd.indirect_dma_start(out=tok_in, out_offset=bass.IndirectOffsetOnAxis(ap=slot_in[:, k, t:t + 1], axis=0),
                                                 in_=xn[:, t, :], in_offset=None).then_inc(tok_sorted, 16)
            pool.sem_inc(y_used, 2)
            pool.wait_ge(x_base, 32)
            with pool.Fori(0, CHUNKS // 2) as g:
                for s in range(2):
                    pool.wait_ge(e_y, g * 2 + (s + 3))
                    pool.nop(nofuse=True)
                    for i in range(CT):
                        nc.gpsimd.indirect_dma_start(out=x_sum, out_offset=bass.IndirectOffsetOnAxis(ap=node_weight[s][:, i, 0:1].bitcast(i32), axis=0),
                                                     in_=yrow[s][:, i, :], in_offset=None, compute_op=ALU.add).then_inc(y_added, 16)
                    pool.wait_ge(y_added, g * (32 * CT) + (s + 1) * (16 * CT))
                    pool.nop(nofuse=True)
                    pool.sem_inc(y_used, 1)

        @block.scalar
        def _(act):
            def wait(s, value):
                act.wait_ge(s, value)
                if not isinstance(value, int):
                    act.nop(nofuse=True)

            act.sem_inc(ad_out[0], 16)
            act.sem_inc(ad_out[1], 16)
            act.sem_inc(ad_sb, 1)
            for l in range(3):
                act.sem_inc(ent[l][1], 1)
                act.sem_inc(ent[l][4], 1)
                act.sem_inc(ent[l][6], 1 if l == 0 else 4)
            for l in range(3):
                for k, name in enumerate(("bl", "gamma", "beta")):
                    act.dma_start(vec[l][:, k, 0:DIMS[l][1]], w[f"L0_gnn_{name}{l}"].rearrange("(f p) -> p f", p=P), allow_slow_non_contiguous=True).then_inc(vec_in, 16)
            act.dma_start(wr2[:, 0:2, :], w["L0_gnn_Wr0"].rearrange("(d p) f -> p d f", p=P)).then_inc(wr_in, 16)
            act.dma_start(wl2[:, 0:2, :], w["L0_gnn_Wl0"].rearrange("(d p) f -> p d f", p=P)).then_inc(wl_in, 16)
            act.dma_start(wx_in, w["L0_ffn_W_x"].rearrange("(d p) f -> p d f", p=P)).then_inc(fold_in, 16)
            act.dma_start(wsl, w["L0_ffn_W_slice"]).then_inc(fold_in, 16)
            act.dma_start(bxT, w["L0_ffn_b_x"].rearrange("(h c) -> c h", c=DH), allow_slow_non_contiguous=True).then_inc(fold_in, 16)
            act.dma_start(temp_row, w["L0_ffn_temperature"].rearrange("a h b c -> a (h b c)")).then_inc(fold_in, 16)
            act.dma_start(bsl_row, w["L0_ffn_b_slice"].rearrange("(a g) -> a g", a=1)).then_inc(fold_in, 16)
            act.wait_ge(zero_ready, 1)
            for b in range(NB):
                act.dma_start(at[:, b, :], zeros16).then_inc(zeroed, 16)
            act.dma_start(at_flat[ASIZE:ASIZE + GE, :].rearrange("(p n) a -> p (n a)", p=P), zeros16[:, 0:GE // P]).then_inc(zeroed, 16)

            def ln_sqrt(k):
                wait(ln_var, k)
                nc.scalar.activation(ln_s[:, :], ln_r[:, :], ACT.Sqrt).then_inc(ln_std, 1)

            def bn_sqrt(k, n):
                wait(ln_var, k)
                nc.scalar.activation(bn_k[:, 1, 0:n], bn_k[:, 0, 0:n], ACT.Sqrt).then_inc(ln_std, 1)

            def products_done(b, fo):
                rps, rdone = ent[0][5:7]
                wait(rps, b * 4 + (fo + 2))
                k = 4 + 2 * (fo % 2)
                nc.scalar.activation(two(tfeat[:, fo, nodes(b)]), ps[:, k:k + 2, 0:HB],
                                     ACT.Identity, bias=vec[0][:, 0, fo:fo + 1]).then_inc(rdone, 1)

            def half_nodes(b, h):
                return bass.ds(b * BC + h * HB, HB)

            def half_relu(l, b, h):
                nfo = DIMS[l][1]
                if not isinstance(b, int) or b > 0:
                    wait(ent[l][5], (b - 1) * (2 * nfo) + ((h + 1) * nfo + 1))
                for f in range(4):
                    nc.scalar.activation(feat[:, f, h * HB:(h + 1) * HB], tfeat[:, f, half_nodes(b, h)], ACT.Relu,
                                         bias=bn_k[:, 3, f:f + 1], scale=bn_k[:, 0, f:f + 1]).then_inc(ent[l][0], 1)

            def half_done(l, b, h):
                nfo = DIMS[l][1]
                rps, rdone = ent[l][5:7]
                for fo in range(nfo):
                    n = h * nfo + fo
                    wait(rps, b * (2 * nfo) + (n + 2))
                    nc.scalar.activation(tfeat[:, fo, half_nodes(b, h)], ps[:, 4 + n % 4, 0:HB],
                                         ACT.Identity, bias=vec[l][:, 0, fo:fo + 1]).then_inc(rdone, 1)

            ln_sqrt(1)
            wait(vec_in, 16 * 9)
            wait(zeroed, 16 * (NB + 1))
            wait(fold_dve, 5)
            rows, hi, lo, tps, tcopied, rps, rdone = ent[0]
            hh, _ = halves(F)
            with act.Fori(0, NB) as b:
                for i in range(BT):
                    wait(rows, b * BT + (i + 1))
                    nc.scalar.activation(hh[:, bass.ds(b * BT + i, 1), :], urow[:, i:i + 1, :], ACT.Copy, scale=LN_SCALE).then_inc(hi, 1)
                wait(tps, b + 2)
                wait(rps, b * 4 + 1)
                nc.scalar.activation(feat[:, 0:2, :], ps[:, 0:4, :].rearrange("p (f k) c -> p f (k c)", f=2)[:, :, 0:BC], ACT.Copy).then_inc(tcopied, 1)
                for fo in range(4):
                    products_done(b, fo)
            with act.Fori(0, NB) as b:
                for q in range(NB):
                    store, s = astore[q % 2], q % 2
                    wait(ad_out[s], b * (16 * (3 - s)) + 16 * (q // 2 + 1))
                    for i in range(BT):
                        n = q * BT + i
                        wait(ad_ps, b * (NB * BT) + (n + 1))
                        nc.scalar.activation(store[:, i, :], ps16[:, 6 + n % 2, 0:BC], ACT.Copy).then_inc(ad_sb, 1)
                    wait(ad_sb, b * (NB * BT) + ((q + 1) * BT + 1))
                    act.dma_start(ad[:, q, bass.ds(b * (BT * BC), BT * BC)], store.rearrange("p i c -> p (i c)")).then_inc(ad_out[s], 16)
            bn_sqrt(2, 4)
            for l in (1, 2):
                rows, hi, lo, tps, tcopied, rps, rdone = ent[l]
                nfo = DIMS[l][1]
                hh, _ = halves(HID)
                wait(bn_done, l)
                wait(sc_ready, l)

                def high_rows(b, tiles):
                    for i in tiles:
                        wait(tps, b * BT + (i + 2))
                        t = bass.ds(b * BT + i, 1)
                        if l == 1:
                            nc.scalar.activation(hh[:, t, :], ps[:, i % 4:i % 4 + 1, :], ACT.Copy, scale=sc[:, 0:1]).then_inc(hi, 1)
                        else:
                            nc.scalar.activation(halves(F)[0][:, t, :], ps[:, i % 4:i % 4 + 1, 0:F], ACT.Copy, scale=sc[:, 0:1]).then_inc(hi, 1)

                def enter_block(b, last):
                    half_relu(l, b, 1)
                    high_rows(b, (0, 1))
                    half_done(l, b, 0)
                    high_rows(b, (2, 3))
                    if not last:
                        half_relu(l, b + 1, 0)
                    high_rows(b, (4,))
                    half_done(l, b, 1)

                half_relu(l, 0, 0)
                enter_block(0, False)
                with act.Fori(1, NB - 1) as b:
                    enter_block(b, False)
                enter_block(NB - 1, True)
                bn_sqrt(2 + l, nfo)
                if l == 1:
                    wait(c_sum, 1)
                    nc.scalar.activation(w3norm, ps[:, 7, 200:201], ACT.Sqrt, scale=float(HID)).then_inc(c_norm, 1)
            rows, lo, tps = ent[3]
            wait(bn_done, 3)
            with act.Fori(0, NB) as b:
                wait(tps, b * BT + 1)
                for f in range(2):
                    nc.scalar.activation(feat[:, f, :], tfeat[:, f, nodes(b)], ACT.Relu,
                                         bias=bn_k[:, 3, f:f + 1], scale=bn_k[:, 0, f:f + 1]).then_inc(rows, 1)
            act.sem_inc(f_tcp, 1)
            act.sem_inc(f_swc, 2)
            for s in (conv[2], r_tcp, e_gelu):
                act.sem_inc(s, 1)
            ln_sqrt(5)

            def transposed_copy(b, i, tps, tcp, bank, columns, base=0):
                wait(tps, b * BT + (base + BT + i + 1))
                nc.scalar.activation(columns, ps[:, bank, 0:F].rearrange("p (f c) -> p f c", f=2), ACT.Copy).then_inc(tcp, 1)

            def f_copy(t, i):
                wait(f_tps, t + 1)
                nc.scalar.activation(feat[:, 0:2, i * P:(i + 1) * P], ps[:, 7, 0:F].rearrange("p (f c) -> p f c", f=2), ACT.Copy).then_inc(f_tcp, 1)

            def f_exps(t, i):
                wait(f_sub, t + 2)
                nc.scalar.activation(logit[:, i % 3, :], logit[:, i % 3, :], ACT.Exp).then_inc(f_exp, 1)

            def f_weights(t, i):
                wait(f_used, t + (BT + 1))
                nc.scalar.activation(tfeat[:, :, bass.ds(t * P, P)], ps[:, 2 + i % 2, :].rearrange("p (k c) -> p k c", k=4), ACT.Copy).then_inc(f_swc, 1)

            three_stages(act.Fori(1, NB), f_copy, f_exps, f_weights)
            wait(f_dve, 6)
            nc.scalar.activation(att, att, ACT.Exp, scale=DH ** -0.5).then_inc(f_act, 1)
            wait(f_swc, T + 2)
            with act.Fori(0, NB) as b:
                for i in range(BT):
                    wait(f_rps, b * BT + (i + 1))
                    nc.scalar.activation(feat[:, :, i * P:(i + 1) * P], tfeat[:, :, bass.ds(b * BC + i * P, P)], ACT.Copy).then_inc(f_slot, 1)
            ln_sqrt(6)
            wait(c_sum, 2)
            nc.scalar.activation(wnorm, ps[:, 7, 200:202], ACT.Sqrt, scale=float(F)).then_inc(c_norm, 1)

            def conv_rows(k):
                _, tps, tcp, xps, hi, _ = conv

                def copy(t, i):
                    wait(tps, t + (k * T + BT + 1))
                    nc.scalar.activation(feat[:, 0:2, i * P:(i + 1) * P], ps[:, i % 2, 0:F].rearrange("p (f c) -> p f c", f=2), ACT.Copy).then_inc(tcp, 1)

                def high(t, i):
                    wait(xps, t + (k * T + 1))
                    nc.scalar.activation(conv_halves[0][0][:, bass.ds(t, 1), 0:F], ps[:, 2 + i % 2, 0:F].unsqueeze(1), ACT.Copy, scale=sc[:, 0:1]).then_inc(hi, 1)

                wait(sc_ready, 3 + k)
                three_stages(act.Fori(1, NB), copy, high, nothing)

            for c in range(4):
                if c == 0:
                    wait(c_ones, 2)
                if c % 2 == 0:
                    conv_rows(c // 2)
                    with act.Fori(0, NB) as b:
                        for i in range(BT):
                            wait(c_deg, b * BT + (c // 2 * T + i + 1))
                            nc.scalar.activation(conv_halves[1][0][:, bass.ds(b * BT + i, 1), 0:F], ps[:, i, 0:F].unsqueeze(1),
                                                 ACT.Copy, scale=rdeg[:, i:i + 1]).then_inc(c_hi, 1)
            with act.Fori(0, NB) as b:
                blk = bass.ds(b * BT, BT)
                for k in range(2):
                    wait(ln_var, b * 2 + (7 + k))
                    nc.scalar.activation(ln_s[:, blk], ln_r[:, blk], ACT.Sqrt).then_inc(ln_std, 1)
                for i in range(BT):
                    transposed_copy(b, i, r_tps, r_tcp, 5 + i % 2, feat[:, 0:2, i * P:(i + 1) * P])
            wait(r_dve, 1)
            nc.scalar.activation(gate2, gate2, ACT.Exp).then_inc(r_act, 1)
            wait(r_pe, 1)
            nc.scalar.activation(evec, ps[:, 6, 0:96], ACT.Copy).then_inc(r_act, 1)
            with act.Fori(0, CHUNKS // 2) as g:
                for s in range(2):
                    for k in range(EK):
                        wait(e_hps, g * (2 * EK) + (s * EK + k + 1))
                        nc.scalar.activation(hT[s][:, k, :], ps[:, k % 4, 0:CAP], ACT.Gelu, bias=evc[s][:, k:k + 1]).then_inc(e_gelu, 1)

        @block.vector
        def _(dve):
            o = Order(dve, dve_order)
            V = nc.vector
            V.memset(zeros16, 0.0).then_inc(zero_ready, 1)
            for s in (ent[0][2], ent[1][2], ent[2][2], ent[3][1], degdone):
                dve.sem_inc(s, 1)
            for l in range(3):
                dve.sem_inc(agg[l][0], 2)
                dve.sem_inc(agg[l][2], 1)

            def step(ins):
                o.mark(ins)
                o.settle()

            dve.wait_ge(edges_in, 16 * 6)
            step(V.tensor_scalar(eint[:, 2, :], eint[:, 0, :], 7, None, ALU.arith_shift_right))
            o.mark(V.tensor_copy(eflt[:, 0:3, :], eint[:, 0:3, :]))
            o.settle()
            step(V.tensor_scalar(eflt[:, 3, :], eflt[:, 1, :], float(BC), None, ALU.is_ge))
            for k in range(2, NB):
                step(V.scalar_tensor_tensor(out=eflt[:, 3, :], in0=eflt[:, 1, :], scalar=float(k * BC), in1=eflt[:, 3, :], op0=ALU.is_ge, op1=ALU.add))
            step(V.tensor_scalar(ekey, eflt[:, 0, :], float(AROW), None, ALU.mult))
            step(V.scalar_tensor_tensor(out=ekey, in0=eflt[:, 2, :], scalar=float(BC - P * AROW), in1=ekey, op0=ALU.mult, op1=ALU.add))
            step(V.scalar_tensor_tensor(out=ekey, in0=eflt[:, 3, :], scalar=float(P * AROW - BC), in1=ekey, op0=ALU.mult, op1=ALU.add))
            V.tensor_tensor(ekey, ekey, eflt[:, 1, :], ALU.add).then_inc(key_ready, 1)
            dve.wait_ge(key_ready, 1)
            dve.wait_ge(consts_ready, 1)
            step(V.tensor_copy(etrash, etrash_i))
            o.mark(V.tensor_tensor(espare.rearrange("p (g q) -> p g q", q=GQ), etrash.unsqueeze(1).to_broadcast([P, NG, GQ]),
                                   ekey.rearrange("p (g q) -> p g q", q=GQ), ALU.subtract))
            dve.wait_ge(keyT_psum, 1)
            V.tensor_copy(keyT, ps[0:EC // GQ, 0:GE // 512, :].rearrange("p k c -> p (k c)")).then_inc(keyT_ready, 1)
            dve.wait_ge(fold_in, 16 * 5)
            step(V.tensor_scalar(temp_row, temp_row, 0.1, 5.0, ALU.max, ALU.min))
            V.reciprocal(rtemp[0:1, :], temp_row).then_inc(fold_dve, 1)
            dve.wait_ge(fold_pe, 1)
            V.tensor_copy(wxT.rearrange("p h d -> p (h d)"), ps[0:DH, 1:5, :].rearrange("p k c -> p (k c)")).then_inc(fold_dve, 1)
            dve.wait_ge(fold_pe, 2)
            V.tensor_copy(rtemp, ps[:, 7, 0:HEADS]).then_inc(fold_dve, 1)
            dve.wait_ge(fold_pe, 3)
            dve.wait_ge(fold_dve, 3)
            o.mark(V.tensor_tensor(bias_raw.rearrange("p (h g) -> p h g", h=HEADS), ps[0:1, 7, :].rearrange("p (h g) -> p h g", h=HEADS),
                                   bsl_row.unsqueeze(1).to_broadcast([1, HEADS, G]), ALU.add))
            for d in range(2):
                V.tensor_tensor(wxs[:, d, :].rearrange("p (h g) -> p h g", h=HEADS), ps[:, 5 + d, :].rearrange("p (h g) -> p h g", h=HEADS),
                                rtemp.unsqueeze(2).to_broadcast([P, HEADS, G]), ALU.mult).then_inc(fold_dve, 1)
            o.settle()
            o.mark(V.tensor_tensor(slice_bias[:, :].rearrange("p (h g) -> p h g", h=HEADS), bias_raw.rearrange("p (h g) -> p h g", h=HEADS),
                                   rtemp[0:1, :].unsqueeze(2).to_broadcast([1, HEADS, G]), ALU.mult))

            def norm_variance(tiles):
                st = [ln_st[:, tiles, j] for j in range(6)]
                mean, var = ln_mv[:, tiles, 0], ln_mv[:, tiles, 1]
                o.mark(V.tensor_tensor(mean, st[1], st[4], ALU.add))
                o.mark(V.tensor_tensor(ln_r[:, tiles], st[1], st[4], ALU.subtract))
                o.mark(V.tensor_tensor(var, st[2], st[5], ALU.add))
                o.settle()
                o.mark(V.tensor_scalar(mean, mean, 0.5, None, ALU.mult))
                step(V.scalar_tensor_tensor(out=ln_s[:, tiles], in0=ln_r[:, tiles], scalar=0.25, in1=ln_r[:, tiles], op0=ALU.mult, op1=ALU.mult))
                step(V.scalar_tensor_tensor(out=var, in0=var, scalar=1.0 / F, in1=ln_s[:, tiles], op0=ALU.mult, op1=ALU.add))
                V.tensor_scalar(ln_r[:, tiles], var, EPS, None, ALU.add).then_inc(ln_var, 1)

            def row_stats(t):
                dve.nop(nofuse=True)
                r = bass.ds(t, 1)
                o.mark(V.bn_stats(ln_st[:, r, :].rearrange("p o s -> p (o s)"), xrows[:, r, :].rearrange("p o c -> p (o c)")))

            def layernorm_stats(k):
                o.settle()
                norm_variance(slice(0, T))
                dve.wait_ge(ln_std, k)
                step(V.reciprocal(ln_r[:, :], ln_s[:, :]))

            def normalized(dst_ap, t, rows=xrows):
                return V.tensor_scalar(dst_ap, rows[:, bass.ds(t, 1), :].rearrange("p o c -> p (o c)"), ln_mv[:, bass.ds(t, 1), 0], ln_r[:, bass.ds(t, 1)],
                                       ALU.subtract, ALU.mult)

            def half_scale(k, cols):
                V.tensor_reduce(sc[:, 2:3], amax[:, 0:cols], AX.X, ALU.max).then_inc(sc_col, 1)
                dve.wait_ge(sc_row, k)
                step(V.tensor_reduce(sc1[:, 0:1], ps[0:1, 7, 0:P], AX.X, ALU.max))
                step(V.tensor_scalar(sc1[:, 1:2], sc1[:, 0:1], 1e-30, None, ALU.max))
                V.tensor_scalar(sc1[:, 2:3].bitcast(i32), sc1[:, 1:2].bitcast(i32), 0x7F800000, None, ALU.bitwise_and).then_inc(sc_pow, 1)
                dve.wait_ge(sc_all, k)
                step(V.tensor_scalar(sc[:, 1:2], ps[:, 7, P:P + 1], 2.0 ** -13, None, ALU.mult))
                V.reciprocal(sc[:, 0:1], sc[:, 1:2]).then_inc(sc_ready, 1)

            def bn_bound(l):
                o.mark(V.scalar_tensor_tensor(out=amax[:, 0:4], in0=vec[l][:, 1, :], scalar=-1.0, in1=vec[l][:, 1, :], op0=ALU.mult, op1=ALU.max))
                o.mark(V.scalar_tensor_tensor(out=amax[:, 4:8], in0=vec[l][:, 2, :], scalar=-1.0, in1=vec[l][:, 2, :], op0=ALU.mult, op1=ALU.max))
                o.settle()
                step(V.scalar_tensor_tensor(out=amax[:, 0:4], in0=amax[:, 0:4], scalar=BN_BOUND, in1=amax[:, 4:8], op0=ALU.mult, op1=ALU.add))

            def edges_of(i, first):
                for s in range(LOOK):
                    dve.wait_ge(krow_in[s], 16 * (i + 1) if first else i * 16 + 16)
                    if not first:
                        dve.wait_ge(scattered, i * (LOOK * GQ * 16) + (s + 1 - LOOK) * (GQ * 16))
                    g = i * LOOK + s
                    for q in range(GQ):
                        key1 = ekey[:, g * GQ + q:g * GQ + q + 1] if first else ekey[:, bass.ds(i * (LOOK * GQ) + s * GQ + q, 1)]
                        ins = V.scalar_tensor_tensor(out=ejunk[q], in0=krow[:, s, :], scalar=key1, in1=eweight[:, GE - P - q * P:2 * GE - P - q * P],
                                                     op0=ALU.is_equal, op1=ALU.mult, accum_out=ecount[:, s, q:q + 1])
                    ins.then_inc(compared, 1)
                    four = slice(g * GQ, g * GQ + GQ) if first else bass.ds(i * (LOOK * GQ) + s * GQ, GQ)
                    dve.wait_ge(compared, (s + 1) if first else i * LOOK + (s + 1))
                    step(V.scalar_tensor_tensor(out=eshift[:, s, :], in0=ecount[:, s, :], scalar=float(GE + 1), in1=espare[:, four], op0=ALU.is_ge, op1=ALU.mult))
                    o.mark(V.tensor_scalar(evalue[:, s, :], ecount[:, s, :], float(GE), None, ALU.min))
                    V.tensor_tensor(eidx[:, s, :], eshift[:, s, :], ekey[:, four], ALU.add).then_inc(idx_ready, 1)

            dve.wait_ge(x_in, 32)
            with o.loop(T, 1) as t:
                row_stats(t)
            layernorm_stats(1)
            o.settle()
            edges_of(0, True)
            rows, hi, lo, tps, tcopied, rps, rdone = ent[0]
            hh, hl = halves(F)
            with o.loop_from(1, NB + 1, 2 * LOOK) as i:
                dve.wait_ge(tps, i)
                dve.wait_ge(hi, i * BT - (BT - 1))
                dve.wait_ge(lo, i * BT - (BT - 1))
                for k in range(BT):
                    normalized(urow[:, k, :], i * BT + (k - BT)).then_inc(rows, 1)
                edges_of(i, False)
                for k in range(BT):
                    dve.wait_ge(hi, i * BT + (k + 2 - BT))
                    t = bass.ds(i * BT + (k - BT), 1)
                    V.scalar_tensor_tensor(out=hl[:, t, :], in0=urow[:, k:k + 1, :], scalar=LN_SCALE, in1=hh[:, t, :],
                                           op0=ALU.mult, op1=ALU.subtract).then_inc(lo, 1)
            with o.loop_from(NB + 1, NG // LOOK, 2 * LOOK) as i:
                edges_of(i, False)

            for l in range(3):
                nfi, nfo = DIMS[l]
                np_ = PASSES[l]
                mean, ops, odone = agg[l]
                rdone = ent[l][6]
                dve.wait_ge(rdone, NB * 4 + 1 if l == 0 else NB * 2 * nfo + 4)
                inv = 1.0 / LN_SCALE if l == 0 else sc[:, 1:2]

                def aggregated(b, width):
                    if l == 0:
                        dve.wait_ge(deg, b + 1)
                        d2 = two(deginv[:, nodes(b)])
                        step(V.tensor_scalar(d2, ps[:, 4:6, 0:HB], 1.0, None, ALU.max))
                        dve.nop(nofuse=True)
                        V.reciprocal(deginv[:, nodes(b)], deginv[:, nodes(b)]).then_inc(degdone, 1)
                        dve.wait_ge(degdone, b + 2)
                    if l < 2:
                        dve.wait_ge(ops, b * nfo + 1)
                    for k in range(np_):
                        for j in range(2):
                            if j == 0:
                                dve.wait_ge(first_summed, b * np_ + (FIRST[l] + k + 1))
                            else:
                                dve.wait_ge(chunk_used[NB - 1], b * np_ + (FIRST[l] + k + 2))
                            V.scalar_tensor_tensor(out=two(feat[:, 2 * k + j, :]), in0=ps[:, 2 * j:2 * j + 2, 0:HB], scalar=inv,
                                                   in1=two(deginv[:, nodes(b)]), op0=ALU.mult, op1=ALU.mult).then_inc(mean, 1)
                    for fo in range(nfo):
                        if l < 2:
                            dve.wait_ge(ops, b * nfo + (fo + 2))
                            k = 4 + 2 * (fo % 2)
                            V.tensor_tensor(two(tfeat[:, fo, nodes(b)]), ps[:, k:k + 2, 0:HB], two(tfeat[:, fo, nodes(b)]), ALU.add).then_inc(odone, 1)
                        else:
                            dve.wait_ge(mean, b * 2 + (fo + 3))
                            V.tensor_tensor(tfeat[:, fo, nodes(b)], feat[:, fo, :], tfeat[:, fo, nodes(b)], ALU.add).then_inc(odone, 1)
                    for fo in range(nfo):
                        dve.wait_ge(odone, b * nfo + (fo + 2))
                        for h in range(2):
                            c = HB if h == 0 else width
                            o.mark(V.bn_stats(bn_st[:, fo, bass.ds(b * 2 + h, 1), :].rearrange("p a s -> p (a s)"),
                                              tfeat[:, fo, bass.ds(b * BC + h * HB, c)]))

                with o.loop(NB - 1, 2 * nfo + (1 if l == 0 else 0)) as b:
                    aggregated(b, HB)
                aggregated(NB - 1, N - (NB - 1) * BC - HB)
                o.settle()
                if l == 1:
                    dve.wait_ge(w2_in, 32)
                    V.scalar_tensor_tensor(out=feat[:, :, :].rearrange("p a b -> p (a b)")[:, 0:1024], in0=wr[:, 1024:2048], scalar=1.0, in1=wr[:, 1024:2048],
                                           op0=ALU.mult, op1=ALU.mult, accum_out=w3square).then_inc(c_square, 1)
                    dve.wait_ge(c_square, 1)
                for fo in range(nfo):
                    o.mark(V.bn_aggr(bn_mv[:, fo, :], bn_st[:, fo, :, :].rearrange("p a s -> p (a s)")))
                o.settle()
                V.tensor_scalar(bn_k[:, 0, 0:nfo], bn_mv[:, 0:nfo, 1], EPS, None, ALU.add).then_inc(ln_var, 1)
                dve.wait_ge(ln_std, 2 + l)
                step(V.reciprocal(bn_k[:, 2, 0:nfo], bn_k[:, 1, 0:nfo]))
                step(V.tensor_tensor(bn_k[:, 0, 0:nfo], bn_k[:, 2, 0:nfo], vec[l][:, 1, 0:nfo], ALU.mult))
                step(V.tensor_tensor(bn_k[:, 1, 0:nfo], bn_mv[:, 0:nfo, 0], bn_k[:, 0, 0:nfo], ALU.mult))
                V.tensor_tensor(bn_k[:, 3, 0:nfo], vec[l][:, 2, 0:nfo], bn_k[:, 1, 0:nfo], ALU.subtract).then_inc(bn_done, 1)
                if l == 0:
                    bn_bound(0)
                    half_scale(1, 4)
                    rows, hi, lo, tps, tcopied, rps, rdone = ent[1]
                    hh, hl = halves(HID)
                    dve.wait_ge(sc_ready, 1)
                    for k, n in ((0, 3), (1, 2)):
                        dve.wait_ge(ad_out[k], 16 * (n * NB + 1))
                    with dve.Fori(0, NB) as b:
                        for i in range(BT):
                            dve.wait_ge(hi, b * BT + (i + 2))
                            t = bass.ds(b * BT + i, 1)
                            V.scalar_tensor_tensor(out=hl[:, t, :], in0=ps[:, i % 4:i % 4 + 1, :], scalar=sc[:, 0:1], in1=hh[:, t, :],
                                                   op0=ALU.mult, op1=ALU.subtract).then_inc(lo, 1)
                elif l == 1:
                    rows, hi, lo, tps, tcopied, rps, rdone = ent[2]
                    dve.wait_ge(c_norm, 1)
                    bn_bound(1)
                    step(V.tensor_scalar(amax[:, 0:4], amax[:, 0:4], w3norm, None, ALU.mult))
                    half_scale(2, 4)
                    hh, hl = halves(F)
                    dve.wait_ge(sc_ready, 2)
                    with dve.Fori(0, NB) as b:
                        for i in range(BT):
                            dve.wait_ge(hi, b * BT + (i + 2))
                            t = bass.ds(b * BT + i, 1)
                            V.scalar_tensor_tensor(out=hl[:, t, :], in0=ps[:, i % 4:i % 4 + 1, 0:F], scalar=sc[:, 0:1], in1=hh[:, t, :],
                                                   op0=ALU.mult, op1=ALU.subtract).then_inc(lo, 1)
                else:
                    rows, lo, tps = ent[3]

                    def add_gnn(t, i):
                        dve.wait_ge(tps, t + 2)
                        r = bass.ds(t, 1)
                        V.tensor_tensor(xrows[:, r, :], ps[:, i % 4:i % 4 + 1, 0:F], xrows[:, r, :], ALU.add).then_inc(lo, 1)

                    def gnn_stats(t, i):
                        dve.wait_ge(lo, t + 2)
                        row_stats(t)

                    three_stages(o.loop_from(1, NB, BT), add_gnn, gnn_stats, nothing)
            H8 = "p (h g) -> p h g"
            dve.sem_inc(f_sub, 1)
            dve.sem_inc(f_x, 1)
            dve.sem_inc(c_read, BT)
            dve.sem_inc(conv[5], 1)
            dve.sem_inc(r_lgc, 1)
            dve.sem_inc(e_y, 2)
            dve.wait_ge(ent[3][1], T + 1)
            dve.wait_ge(chunk_used[NB - 1], FIRST[3] + 1)
            V.memset(zero_row, 0.0).then_inc(f_zero, 1)
            layernorm_stats(5)

            def f_normal(t, i):
                dve.wait_ge(f_used, t + 1)
                normalized(urow[:, i, :], t).then_inc(f_rows, 1)

            def f_shift(t, i):
                s = i % 3
                dve.wait_ge(f_lg, t + 2)
                step(V.tensor_tensor(logit[:, s, :], ps[:, i % 2, :], bias_rep, ALU.add))
                step(V.tensor_reduce(hmax[:, s, :], logit[:, s, :].rearrange(H8, h=HEADS), AX.X, ALU.max))
                V.tensor_tensor(logit[:, s, :].rearrange(H8, h=HEADS), logit[:, s, :].rearrange(H8, h=HEADS),
                                hmax[:, s, :].unsqueeze(2).to_broadcast([P, HEADS, G]), ALU.subtract).then_inc(f_sub, 1)

            def f_softmax(t, i):
                s = i % 3
                dve.wait_ge(f_exp, t + 1)
                step(V.tensor_reduce(hsum[:, s, :], logit[:, s, :].rearrange(H8, h=HEADS), AX.X, ALU.add))
                step(V.reciprocal(hrec[:, s, :], hsum[:, s, :]))
                if not isinstance(t, int) or t >= 2:
                    dve.wait_ge(f_sum, t)
                dve.wait_ge(f_used, t + (BT - 1))
                V.scalar_tensor_tensor(out=sweight[:, s, :].rearrange(H8, h=HEADS), in0=logit[:, s, :].rearrange(H8, h=HEADS),
                                       scalar=rowmask[:, bass.ds(t, 1)], in1=hrec[:, s, :].unsqueeze(2).to_broadcast([P, HEADS, G]),
                                       op0=ALU.mult, op1=ALU.mult).then_inc(f_sw, 1)

            dve.wait_ge(f_lg, 1)
            step(V.tensor_copy(bias_rep, ps[:, 0, :]))
            three_stages(o.loop_from(1, NB, 4 * BT), f_normal, f_shift, f_softmax, third_early=True)
            dve.wait_ge(f_pe, 1)
            o.mark(V.tensor_copy(tokT, ps[:, 4:6, :]))
            o.mark(V.tensor_copy(norm, ps[0:DH, 6, :]))
            step(V.tensor_scalar(rnorm, ps[0:DH, 6, :], 1e-5, None, ALU.add))
            V.reciprocal(rnorm, rnorm).then_inc(f_dve, 1)
            dve.wait_ge(f_pe, 2)
            dve.wait_ge(f_dve, 1)
            V.tensor_tensor(slT, ps[0:DH, 0, :], rnorm, ALU.mult).then_inc(f_dve, 1)
            dve.wait_ge(f_pe, 3)
            for k, part in enumerate((qT, kT, vS)):
                V.tensor_copy(part, ps[0:DH, 1 + k, :]).then_inc(f_dve, 1)
            dve.wait_ge(f_pe, 4)
            lg4 = ps[0:DH, 0, :].rearrange(H8, h=HEADS)
            a4 = att.rearrange(H8, h=HEADS)
            step(V.tensor_reduce(hmax[0:DH, 0, :], lg4, AX.X, ALU.max))
            V.tensor_tensor(a4, lg4, hmax[0:DH, 0, :].unsqueeze(2).to_broadcast([DH, HEADS, G]), ALU.subtract).then_inc(f_dve, 1)
            dve.wait_ge(f_act, 1)
            step(V.tensor_reduce(hsum[0:DH, 0, :], a4, AX.X, ALU.add))
            step(V.reciprocal(hrec[0:DH, 0, :], hsum[0:DH, 0, :]))
            V.tensor_tensor(a4, a4, hrec[0:DH, 0, :].unsqueeze(2).to_broadcast([DH, HEADS, G]), ALU.mult).then_inc(f_dve, 1)
            dve.wait_ge(f_pe, 5)
            V.tensor_copy(attT, ps[0:DH, 1, :]).then_inc(f_dve, 1)
            dve.wait_ge(f_pe, 6)
            V.tensor_copy(outT, ps[0:DH, 2, :]).then_inc(f_dve, 1)
            dve.wait_ge(f_pe, 7)
            for k in range(2):
                half = slice(k * DH, (k + 1) * DH)
                V.tensor_copy(pmat[half, :, :].rearrange("p k o -> p (k o)"), ps[half, 3 + 2 * k:5 + 2 * k, :].rearrange("p k c -> p (k c)")).then_inc(f_dve, 1)
            dve.wait_ge(f_bias, 1)

            def add_ffn(t, i):
                dve.wait_ge(f_rps, t + (BT + 1))
                r = bass.ds(t, 1)
                V.tensor_tensor(xrows[:, r, :], ps[:, i % 4:i % 4 + 1, 0:F], xrows[:, r, :], ALU.add).then_inc(f_x, 1)

            def ffn_stats(t, i):
                dve.wait_ge(f_x, t + 2)
                row_stats(t)

            three_stages(o.loop_from(1, NB, BT), add_ffn, ffn_stats, nothing)

            dve.wait_ge(f_x, T + 1)
            layernorm_stats(6)
            for hh, _ in conv_halves:
                V.memset(hh[:, :, F:F + 2], 1.0).then_inc(c_ones, 1)
            dve.wait_ge(conv_w, 16 * 5)
            for k in range(2):
                V.scalar_tensor_tensor(out=late[:, 1024:1536], in0=wr[:, 1024 + k * 512:1536 + k * 512], scalar=1.0, in1=wr[:, 1024 + k * 512:1536 + k * 512],
                                       op0=ALU.mult, op1=ALU.mult, accum_out=wsquare[:, k:k + 1]).then_inc(c_square, 1)
                dve.wait_ge(c_square, k + 2)
            dve.wait_ge(c_norm, 2)
            step(V.tensor_copy(amax[:, 0:1], wnorm[:, 0:1]))
            half_scale(3, 1)

            def conv_normal(t, i):
                dve.wait_ge(conv[1], t + 1)
                normalized(urow[:, i, :], t).then_inc(conv[0], 1)

            def conv_low(k):
                hh, hl = conv_halves[0]

                def low(t, i):
                    dve.wait_ge(conv[4], t + (k * T + 1))
                    V.scalar_tensor_tensor(out=hl[:, bass.ds(t, 1), :], in0=ps[:, 2 + i % 2, 0:F].unsqueeze(1), scalar=sc[:, 0:1],
                                           in1=hh[:, bass.ds(t, 1), 0:F], op0=ALU.mult, op1=ALU.subtract).then_inc(conv[5], 1)
                return low

            def edge_degree(b, c, i):
                if i < BT - 1:
                    dve.wait_ge(c_bank, b * (BT - 1) + (c * NB * (BT - 1) + i + 1))
                else:
                    dve.wait_ge(chunk_used[NB - 1], b + (FIRST[3] + c * NB + 2))
                step(V.tensor_scalar(rdeg[:, i:i + 1], ps[:, i, F:F + 1], 1.0, None, ALU.max))

            def edge_means(b, c):
                for i in range(BT):
                    r = rdeg[:, i:i + 1]
                    edge_degree(b, c, i)
                    step(V.reciprocal(r, r))
                    step(V.tensor_scalar(r, r, sc[:, 1:2], None, ALU.mult))
                    V.scalar_tensor_tensor(out=zrows[:, i, :], in0=ps[:, i, 0:F], scalar=r, in1=bconv[c // 2],
                                           op0=ALU.mult, op1=ALU.add).then_inc(c_read, 1)
                dve.wait_ge(c_read, b * BT + (c * T + 2 * BT))

            dve.wait_ge(sc_ready, 3)
            three_stages(dve.Fori(1, NB), conv_normal, nothing, conv_low(0))
            for c in range(4):
                if c == 2:
                    o.settle()
                    step(V.tensor_scalar(amax[:, :], amax[:, :], wnorm[:, 1:2], None, ALU.mult))
                    half_scale(4, T)
                    dve.wait_ge(sc_ready, 4)
                    three_stages(dve.Fori(1, NB), nothing, nothing, conv_low(1))
                if c == 3:
                    break
                with o.loop(NB, (BT, 3 * BT + 2, BT)[c]) as b:
                    blk = bass.ds(b * BT, BT)
                    if c % 2 == 0:
                        hh, hl = conv_halves[1]
                        for i in range(BT):
                            edge_degree(b, c, i)
                            dve.nop(nofuse=True)
                            V.reciprocal(rdeg[:, i:i + 1], rdeg[:, i:i + 1]).then_inc(c_deg, 1)
                            dve.wait_ge(c_hi, b * BT + (c // 2 * T + i + 1))
                            t = bass.ds(b * BT + i, 1)
                            V.scalar_tensor_tensor(out=hl[:, t, :], in0=ps[:, i, 0:F].unsqueeze(1), scalar=rdeg[:, i:i + 1], in1=hh[:, t, 0:F],
                                                   op0=ALU.mult, op1=ALU.subtract).then_inc(c_read, 1)
                    else:
                        edge_means(b, c)
                        step(V.tensor_scalar(negrows, zrows, 0.0, slope, ALU.min, ALU.mult))
                        V.scalar_tensor_tensor(out=rows2[:, blk, :], in0=zrows, scalar=0.0, in1=negrows, op0=ALU.max, op1=ALU.add).then_inc(c_h, 1)
                        dve.wait_ge(c_h, b + 1)
                        o.mark(V.tensor_reduce(amax[:, blk], rows2[:, blk, :], AX.X, ALU.max, apply_absolute_value=True))

            def block_norm(b, rows, k):
                blk = bass.ds(b * BT, BT)
                dve.nop(nofuse=True)
                for i in range(BT):
                    t = bass.ds(b * BT + i, 1)
                    o.mark(V.bn_stats(ln_st[:, t, :].rearrange("p o s -> p (o s)"), rows[:, t, :].rearrange("p o c -> p (o c)")))
                o.settle()
                norm_variance(blk)
                dve.wait_ge(ln_std, b * 2 + (7 + k))
                dve.nop(nofuse=True)
                step(V.reciprocal(ln_r[:, blk], ln_s[:, blk]))

            def router_logits(t0, n):
                dve.wait_ge(r_lg, n)
                V.tensor_copy(lgt[:, bass.ds(t0, BT), :], ps[:, 7, 0:BT * EXPERTS].rearrange("p (t e) -> p t e", t=BT)).then_inc(r_lgc, 1)

            def output_block(b):
                blk = bass.ds(b * BT, BT)
                edge_means(b, 3)
                for i in range(BT):
                    o.mark(normalized(urows[:, i, :], b * BT + i))
                o.settle()
                step(V.tensor_tensor(zrows, zrows, urows, ALU.add))
                step(V.tensor_scalar(negrows, zrows, 0.0, slope, ALU.min, ALU.mult))
                step(V.scalar_tensor_tensor(out=zrows, in0=zrows, scalar=0.0, in1=negrows, op0=ALU.max, op1=ALU.add))
                V.tensor_tensor(xrows[:, blk, :], xrows[:, blk, :], zrows, ALU.add).then_inc(c_x, 1)
                dve.wait_ge(c_x, b + 1)
                block_norm(b, xrows, 0)
                for i in range(BT):
                    dve.wait_ge(r_tps, b * BT + (i + 1))
                    normalized(urow[:, i, :], b * BT + i).then_inc(r_rows, 1)
                    o.mark(normalized(rows2[:, bass.ds(b * BT + i, 1), :].rearrange("p o c -> p (o c)"), b * BT + i))
                o.settle()
                block_norm(b, rows2, 1)
                for i in range(BT):
                    normalized(xn[:, bass.ds(b * BT + i, 1), 0:F].rearrange("p o c -> p (o c)"), b * BT + i, rows2).then_inc(e_xn, 1)

            o.settle()
            output_block(0)
            with o.loop_from(1, NB, 3 * BT + 37) as b:
                output_block(b)
                router_logits(b * BT - BT, b)
            router_logits(T - BT, NB)
            dve.wait_ge(r_lgc, NB + 1)
            dve.wait_ge(c_x, NB)
            for e in range(EXPERTS):
                o.mark(V.memset(rank[:, e:e + 1], float(EXPERTS - e)))

            def each(ap):
                return ap.unsqueeze(2).to_broadcast([P, T, EXPERTS])

            for top, sel in ((top1, sel1), (top2, sel2)):
                step(V.tensor_reduce(top, lgt, AX.X, ALU.max))
                step(V.tensor_tensor(pri, lgt, each(top), ALU.is_equal))
                step(V.tensor_tensor(pri, pri, rank.unsqueeze(1).to_broadcast([P, T, EXPERTS]), ALU.mult))
                step(V.tensor_reduce(first, pri, AX.X, ALU.max))
                step(V.tensor_tensor(sel, pri, each(first), ALU.is_equal))
                if sel is sel1:
                    step(V.scalar_tensor_tensor(out=lgt, in0=sel, scalar=-3e38, in1=lgt, op0=ALU.mult, op1=ALU.add))
            V.tensor_tensor(gate2, top2, top1, ALU.subtract).then_inc(r_dve, 1)
            dve.wait_ge(r_act, 1)
            step(V.tensor_scalar(gate1, gate2, 1.0, None, ALU.add))
            step(V.reciprocal(gate1, gate1))
            step(V.tensor_tensor(gate2, gate2, gate1, ALU.mult))
            real = each(rowmask[:, :])
            o.mark(V.tensor_tensor(sel1, sel1, real, ALU.mult))
            step(V.tensor_tensor(sel2, sel2, real, ALU.mult))
            V.tensor_tensor(picked, sel1, sel2, ALU.add).then_inc(r_dve, 1)
            dve.wait_ge(r_trash, 1)
            o.mark(V.tensor_copy(trash[:, 0:1], trash_i))
            o.mark(V.tensor_copy(chunk_no, chunk_no_i))
            seg, cnt, plc = (a.rearrange("p t e -> p (t e)").rearrange("p (e t) -> p e t", e=EXPERTS) for a in (seg_start, count, place))
            step(V.memset(seg, 1.0))
            step(V.memset(seg[:, :, 0:1], 0.0))
            dve.wait_ge(r_pe, 2)
            per_tile = ps[:, 5, 0:T * EXPERTS].rearrange("p (t e) -> p e t", e=EXPERTS)
            step(V.tensor_copy(cnt, per_tile))
            step(V.tensor_tensor_scan(plc.rearrange("p e t -> p (e t)"), seg.rearrange("p e t -> p (e t)"), cnt.rearrange("p e t -> p (e t)"),
                                      0.0, ALU.mult, ALU.add))
            step(V.tensor_copy(chunks_i, plc[:, :, T - 1]))
            step(V.tensor_tensor(plc, plc, cnt, ALU.subtract))
            step(V.tensor_scalar(chunks_i, chunks_i, CAP - 1, None, ALU.add))
            step(V.tensor_scalar(chunks_i, chunks_i, CAP.bit_length() - 1, None, ALU.arith_shift_right))
            step(V.tensor_copy(total, chunks_i))
            step(V.tensor_tensor_scan(ends, seg[:, 0, 1:1 + EXPERTS], total, 0.0, ALU.mult, ALU.add))
            step(V.tensor_tensor(starts, ends, total, ALU.subtract))
            step(V.tensor_scalar(starts, starts, float(CAP), None, ALU.mult))
            step(V.tensor_tensor(plc, plc, starts.unsqueeze(2).to_broadcast([P, EXPERTS, T]), ALU.add))
            step(V.tensor_tensor(plc, plc, ps[:, 4, 0:T * EXPERTS].rearrange("p (t e) -> p e t", e=EXPERTS), ALU.add))
            step(V.tensor_tensor(passed, chunk_no.unsqueeze(2).to_broadcast([1, CHUNKS, EXPERTS]),
                                 ends[0:1, :].unsqueeze(1).to_broadcast([1, CHUNKS, EXPERTS]), ALU.is_ge))
            step(V.tensor_reduce(chunk_of, passed, AX.X, ALU.add))
            V.tensor_scalar(ids, chunk_of, float(EXPERTS - 1), None, ALU.min).then_inc(r_dve, 1)
            for k, sel in enumerate((sel1, sel2)):
                step(V.tensor_tensor(pri, sel, plc.rearrange("p e t -> p t e"), ALU.mult))
                step(V.tensor_reduce(slot_at[:, k, :], pri, AX.X, ALU.add))
            o.mark(V.tensor_scalar(trash[:, 1:2], trash[:, 0:1], float(P), None, ALU.add))
            step(V.tensor_scalar(trash[:, 2:3], rowmask[:, T - 1:T], -1.0, 1.0, ALU.mult, ALU.add))
            step(V.scalar_tensor_tensor(out=slot_at[:, :, T - 1], in0=trash[:, 0:2], scalar=trash[:, 2:3], in1=slot_at[:, :, T - 1], op0=ALU.mult, op1=ALU.add))
            V.tensor_copy(slot_in, slot_at).then_inc(r_dve, 1)
            V.tensor_copy(xn[:, :, F + 1], gate1).then_inc(r_dve, 1)
            dve.wait_ge(tok_sorted, 16 * T)
            V.tensor_copy(xn[:, :, F + 1], gate2).then_inc(r_dve, 1)
            def expert_rows(c, uses, s):
                dve.wait_ge(e_tps, c + 1)
                dve.wait_ge(e_in[s], uses)
                dve.wait_ge(y_used, c + 1)
                V.tensor_copy(node_weight[s], xin[s][:, :, F:F + 2]).then_inc(e_n, 1)
                for d in range(2):
                    V.tensor_scalar(xeT[s][:, d, :], ps[:, 6 + s, d * CAP:(d + 1) * CAP], evc[s][:, EK + d:EK + d + 1],
                                    evc[s][:, EK + 2 + d:EK + 3 + d], ALU.mult, ALU.add).then_inc(e_xe, 1)

            def chunk_out(c, s):
                dve.wait_ge(e_yps, c + 3)
                dve.wait_ge(e_n, c + 1)
                V.tensor_tensor(yrow[s], ps[:, 4 + s, :].rearrange("p (i c) -> p i c", i=CT), b2e[s].unsqueeze(1).to_broadcast([P, CT, F]), ALU.add).then_inc(e_b, 1)
                dve.wait_ge(e_b, c + 1)
                V.tensor_tensor(yrow[s], yrow[s], node_weight[s][:, :, 1:2].to_broadcast([P, CT, F]), ALU.mult).then_inc(e_y, 1)

            expert_rows(0, 32, 0)
            with dve.Fori(0, CHUNKS // 2 - 1) as g:
                expert_rows(g * 2 + 1, g * 32 + 32, 1)
                chunk_out(g * 2, 0)
                expert_rows(g * 2 + 2, g * 32 + 64, 0)
                chunk_out(g * 2 + 1, 1)
            expert_rows(CHUNKS - 1, CHUNKS // 2 * 32, 1)
            chunk_out(CHUNKS - 2, 0)
            chunk_out(CHUNKS - 1, 1)

        @block.tensor
        def _(pe):
            M = nc.tensor.matmul
            pe.sem_inc(ent[3][2], 1)
            for l in range(3):
                pe.sem_inc(ent[l][3], 1)
                pe.sem_inc(ent[l][5], 1)
            for l in range(3):
                pe.sem_inc(agg[l][1], 1)

            pe.wait_ge(consts_ready, 1)
            pe.wait_ge(key_ready, 1)
            for q in range(GQ):
                ins = nc.tensor.transpose(ps[0:NG, q // 4, (q % 4) * P:(q % 4 + 1) * P], ekey[:, q * NG:(q + 1) * NG], ident[:, :])
            ins.then_inc(keyT_psum, 1)
            pe.wait_ge(fold_in, 16 * 5)
            pe.wait_ge(keyT_ready, 1)
            for h in range(HEADS):
                for d in range(2):
                    n = 2 * h + d
                    ins = nc.tensor.transpose(ps[0:DH, 1 + n // 4, (n % 4) * P:(n % 4 + 1) * P], wx_in[:, d, h * DH:(h + 1) * DH], ident[:, :])
            ins.then_inc(fold_pe, 1)
            pe.wait_ge(fold_dve, 1)
            M(ps[:, 7, 0:HEADS], ones[0:1, :], rtemp[0:1, :], start=True, stop=True).then_inc(fold_pe, 1)
            pe.wait_ge(fold_dve, 3)
            for d in range(2):
                for h in range(HEADS):
                    M(ps[:, 5 + d, h * G:(h + 1) * G], wxT[:, h, d * P:(d + 1) * P], wsl, start=True, stop=True)
            for h in range(HEADS):
                ins = M(ps[0:1, 7, h * G:(h + 1) * G], bxT[:, h:h + 1], wsl, start=True, stop=True)
            ins.then_inc(fold_pe, 1)

            def products(b):
                rps, rdone = ent[0][5:7]
                for fo in range(4):
                    k = 4 + 2 * (fo % 2)
                    pe.wait_ge(rdone, b * 4 + (fo if fo >= 2 else 1))
                    for h in range(2):
                        for d in range(2):
                            ins = M(ps[:, k + h, 0:HB], wr2[:, d, fo * P:(fo + 1) * P], feat[:, d, h * HB:(h + 1) * HB], start=(d == 0), stop=(d == 1))
                    ins.then_inc(rps, 1)

            def half_products(l, b, h, weights):
                nfo = DIMS[l][1]
                rps, rdone = ent[l][5:7]
                for fo in range(nfo):
                    n = h * nfo + fo
                    pe.wait_ge(rdone, b * (2 * nfo) + (n + 1))
                    for d in range(4):
                        ins = M(ps[:, 4 + n % 4, 0:HB], weights[:, d, fo * P:(fo + 1) * P], feat[:, d, h * HB:(h + 1) * HB], start=(d == 0), stop=(d == 3))
                    ins.then_inc(rps, 1)

            def enter_block(l, b, tile_rows, weights):
                rows, _, lo = ent[l][0:3]
                for h, tiles in ((0, (0, 1)), (1, (2, 3, 4))):
                    pe.wait_ge(rows, b * 8 + (4 * h + 4))
                    for i in tiles:
                        pe.wait_ge(lo, b * BT + (2 if i == 4 else 1))
                        tile_rows(i)
                    half_products(l, b, h, weights)

            rows, hi, lo, tps, tcopied, rps, rdone = ent[0]
            pe.wait_ge(wr_in, 16)
            pe.wait_ge(fold_dve, 5)
            with pe.Fori(0, NB) as b:
                pe.wait_ge(rows, b * BT + BT)
                pe.wait_ge(tcopied, b + 1)
                for i in range(BT):
                    for f in range(2):
                        c = i * P
                        ins = nc.tensor.transpose(ps[:, 2 * f + c // 512, c % 512:c % 512 + P], urow[:, i, f * P:(f + 1) * P], ident[:, :])
                ins.then_inc(tps, 1)
                pe.wait_ge(tcopied, b + 2)
                products(b)

            def aggregate(l, b, k, width):
                n = b * PASSES[l] + (FIRST[l] + k)
                hh, hl = halves(width)
                if l == 0:
                    pe.wait_ge(agg[0][2], b * 4 + 1)
                for q in range(NB):
                    pe.wait_ge(chunk_in[q], n * 16 + 16)
                    order = [(s, f) for s in range(BT) for f in range(2)]
                    for s, f in (sorted(order, key=lambda sf: sf[1]) if q in (0, NB - 1) else order):
                        t = q * BT + s
                        if l == 0 and f == 0:
                            pe.wait_ge(ad_sb, b * (NB * BT) + (t if t >= 2 else 1))
                            for j in range(BT):
                                ins = nc.tensor.transpose(ps16[:, 6 + t % 2, j * P:(j + 1) * P], chunk[q][:, j, s * P:(s + 1) * P], ident16[:, :])
                            ins.then_inc(ad_ps, 1)
                            if t == 0:
                                pe.wait_ge(degdone, b + 1)
                            if s == 0:
                                for j in range(BT):
                                    for h in range(2):
                                        ins = M(ps[:, 4 + h, 0:HB], ones16[:, :], chunk[q][:, j, h * HB:(h + 1) * HB],
                                                start=(t + j == 0), stop=(t + j == T - 1))
                                if q == NB - 1:
                                    ins.then_inc(deg, 1)
                        if t == 0:
                            pe.wait_ge(agg[l][0], b * (2 * PASSES[l]) + (2 * k + f + 1))
                        for part in (hh, hl):
                            for h in range(2):
                                ins = M(ps[:, 2 * f + h, 0:HB], part[:, t, (2 * k + f) * P:(2 * k + f + 1) * P], chunk[q][:, s, h * HB:(h + 1) * HB],
                                        start=(t == 0 and part is hh), stop=(t == T - 1 and part is hl))
                        if t == T - 1 and f == 0:
                            ins.then_inc(first_summed, 1)
                    ins.then_inc(chunk_used[q], 1)

            def mean_products(l, b, nfi, nfo):
                mean, ops, odone = agg[l]
                pe.wait_ge(mean, (b + 1) * (2 * PASSES[l]) + 2)
                if l == 0:
                    pe.wait_ge(degdone, b + 2)
                    pe.wait_ge(ad_sb, (b + 1) * (NB * BT) + 1)
                for fo in range(nfo):
                    pe.wait_ge(odone, b * nfo + (fo if fo >= 2 else 1))
                    k = 4 + 2 * (fo % 2)
                    for h in range(2):
                        for d in range(nfi):
                            ins = M(ps[:, k + h, 0:HB], wl2[:, d, fo * P:(fo + 1) * P], feat[:, d, h * HB:(h + 1) * HB],
                                    start=(d == 0), stop=(d == nfi - 1))
                    ins.then_inc(ops, 1)

            def half_scale(k):
                pe.wait_ge(sc_col, k)
                M(ps[0:1, 7, 0:P], sc[:, 2:3], ident[:, :], start=True, stop=True).then_inc(sc_row, 1)
                pe.wait_ge(sc_pow, k)
                M(ps[:, 7, P:P + 1], ones[0:1, :], sc1[:, 2:3], start=True, stop=True).then_inc(sc_all, 1)

            pe.wait_ge(ent[0][1], T + 1)
            pe.wait_ge(ent[0][2], T + 1)
            pe.wait_ge(ent[0][6], NB * 4 + 1)
            pe.wait_ge(wl_in, 16)
            with pe.Fori(0, NB) as b:
                aggregate(0, b, 0, F)
                mean_products(0, b, 2, 4)

            pe.wait_ge(agg[0][2], NB * 4 + 1)
            half_scale(1)
            rows, hi, lo, tps, tcopied, rps, rdone = ent[1]
            pe.wait_ge(wr1_in, 16)
            pe.wait_ge(sc_ready, 1)

            def turned_rows(i):
                for f in range(4):
                    ins = nc.tensor.transpose(ps[:, i % 4, f * P:(f + 1) * P], feat[:, f, i * P:(i + 1) * P], ident[:, :])
                ins.then_inc(ent[1][3], 1)

            with pe.Fori(0, NB) as b:
                enter_block(1, b, turned_rows, wr2)
            pe.wait_ge(lo, T + 1)
            pe.wait_ge(rdone, NB * 8 + 4)
            pe.wait_ge(wl1_in, 16)
            with pe.Fori(0, NB) as b:
                aggregate(1, b, 0, HID)
                aggregate(1, b, 1, HID)
                mean_products(1, b, 4, 4)
            rows, hi, lo, tps, tcopied, rps, rdone = ent[2]
            pe.wait_ge(w2_in, 32)
            pe.wait_ge(agg[1][2], NB * 4 + 1)
            pe.wait_ge(c_square, 1)
            M(ps[:, 7, 200:201], ones[:, :], w3square, start=True, stop=True).then_inc(c_sum, 1)
            half_scale(2)
            pe.wait_ge(sc_ready, 2)

            def weighted_rows(i):
                for d in range(4):
                    ins = M(ps[:, i % 4, 0:F], feat[:, d, i * P:(i + 1) * P], wl3[:, d, :], start=(d == 0), stop=(d == 3))
                ins.then_inc(ent[2][3], 1)

            with pe.Fori(0, NB) as b:
                enter_block(2, b, weighted_rows, wr3)
            pe.wait_ge(rdone, NB * 4 + 4)
            pe.wait_ge(lo, T + 1)
            with pe.Fori(0, NB) as b:
                aggregate(2, b, 0, F)
            rows, lo, tps = ent[3]
            pe.wait_ge(agg[2][0], NB * 2 + 2)
            with pe.Fori(0, NB) as b:
                pe.wait_ge(rows, b * 2 + 2)
                for i in range(BT):
                    pe.wait_ge(lo, b * BT + (2 if i == 4 else 1))
                    for f in range(2):
                        ins = nc.tensor.transpose(ps[:, i % 4, f * P:(f + 1) * P], feat[:, f, i * P:(i + 1) * P], ident[:, :])
                    ins.then_inc(tps, 1)

            pe.sem_inc(f_used, BT)
            pe.sem_inc(f_rps, BT)
            pe.sem_inc(conv[1], BT)
            pe.sem_inc(r_tps, BT)
            pe.sem_inc(e_yps, 2)
            pe.wait_ge(f_zero, 1)
            pe.wait_ge(lo, T + 1)
            for k in range(2):
                M(ps[:, 4 + k, :], zero_row[:, 0:P], zero_row, start=True, stop=False)
            M(ps[:, 0, :], ones[0:1, :], slice_bias[:, :], start=True, stop=True).then_inc(f_lg, 1)

            def f_turn(t, i):
                pe.wait_ge(f_rows, t + 1)
                pe.wait_ge(f_tcp, t + 1)
                for f in range(2):
                    ins = nc.tensor.transpose(ps[:, 7, f * P:(f + 1) * P], urow[:, i, f * P:(f + 1) * P], ident[:, :])
                ins.then_inc(f_tps, 1)

            def f_logits(t, i):
                pe.wait_ge(f_tcp, t + 2)
                pe.wait_ge(f_sub, t + (2 - before(i)))
                for d in range(2):
                    ins = M(ps[:, i % 2, :], feat[:, d, i * P:(i + 1) * P], wxs[:, d, :], start=(d == 0), stop=(d == 1))
                ins.then_inc(f_lg, 1)

            def f_tokens(t, i):
                pe.wait_ge(f_sw, t + 1)
                pe.wait_ge(f_swc, t + (3 - before(i)))
                for k in range(2):
                    M(ps[:, 4 + k, :], urow[:, i, k * P:(k + 1) * P], sweight[:, i % 3, :], start=False, stop=False)
                for k in range(4):
                    ins = nc.tensor.transpose(ps[:, 2 + i % 2, k * P:(k + 1) * P], sweight[:, i % 3, k * P:(k + 1) * P], ident[:, :])
                ins.then_inc(f_used, 1)

            three_stages(pe.Fori(1, NB), f_turn, f_logits, f_tokens)
            for k in range(2):
                M(ps[:, 4 + k, :], zero_row[:, 0:P], zero_row, start=False, stop=True)
            pe.wait_ge(f_sum, T + 1)
            M(ps[0:DH, 6, :], ones[:, 0:DH], weight_sum, start=True, stop=True).then_inc(f_pe, 1)

            def head(h):
                return slice(h * G, (h + 1) * G)

            pe.wait_ge(ffn_w, 16 * 7)
            pe.wait_ge(f_dve, 1)
            pe.wait_ge(f_swc, T + 2)
            for h in range(HEADS):
                for d in range(2):
                    M(ps[0:DH, 0, head(h)], wfx[:, d, head(h)], tokT[:, d, head(h)], start=(d == 0), stop=False)
                ins = M(ps[0:DH, 0, head(h)], bfx[:, head(h)], norm[0:1, head(h)], start=False, stop=True)
            ins.then_inc(f_pe, 1)
            pe.wait_ge(f_dve, 2)
            for k in range(2):
                M(ps[0:DH, 1 + k, :], wqkv[:, k, :], slT, start=True, stop=True)
            for h in range(HEADS):
                ins = M(ps[0:DH, 3, head(h)], slT[:, head(h)], wqkv[:, 2, :], start=True, stop=True)
            ins.then_inc(f_pe, 1)
            pe.wait_ge(f_dve, 5)
            for h in range(HEADS):
                ins = M(ps[0:DH, 0, head(h)], qT[:, head(h)], kT[:, head(h)], start=True, stop=True)
            ins.then_inc(f_pe, 1)
            pe.wait_ge(f_dve, 7)
            for h in range(HEADS):
                ins = nc.tensor.transpose(ps[0:DH, 1, head(h)], att[:, head(h)], ident[0:DH, 0:DH])
            ins.then_inc(f_pe, 1)
            pe.wait_ge(f_dve, 8)
            for h in range(HEADS):
                ins = M(ps[0:DH, 2, head(h)], vS[:, head(h)], attT[:, head(h)], start=True, stop=True)
            ins.then_inc(f_pe, 1)
            pe.wait_ge(f_dve, 9)
            for h in range(HEADS):
                c = (h // 2) * F
                ins = M(ps[:, 3 + 2 * (h % 2) + c // 512, c % 512:c % 512 + F], outT[:, (h // 2) * P:(h // 2 + 1) * P], wout[:, h, :], start=True, stop=True)
            ins.then_inc(f_pe, 1)
            pe.wait_ge(f_dve, 11)
            with pe.Fori(0, NB) as b:
                for i in range(BT):
                    pe.wait_ge(f_slot, b * BT + (i + 1))
                    pe.wait_ge(f_x, b * BT + (2 if i == 4 else 1))
                    for k in range(4):
                        ins = M(ps[:, i % 4, 0:F], feat[:, k, i * P:(i + 1) * P], pmat[:, k, :], start=(k == 0), stop=(k == 3))
                    ins.then_inc(f_rps, 1)

            def conv_rows(k):
                rows, tps, tcp, xps, _, lo = conv

                def turn(t, i):
                    pe.wait_ge(rows, t + (k * T + 1))
                    pe.wait_ge(tcp, t + (k * T + 2 - before(i)))
                    for f in range(2):
                        ins = nc.tensor.transpose(ps[:, i % 2, f * P:(f + 1) * P], urow[:, i, f * P:(f + 1) * P], ident[:, :])
                    ins.then_inc(tps, 1)

                def product(t, i):
                    pe.wait_ge(tcp, t + (k * T + 2))
                    pe.wait_ge(lo, t + (k * T + 2 - before(i)))
                    for d in range(2):
                        ins = M(ps[:, 2 + i % 2, 0:F], feat[:, d, i * P:(i + 1) * P], wconv[k][:, d, :], start=(d == 0), stop=(d == 1))
                    ins.then_inc(xps, 1)

                three_stages(pe.Fori(1, NB), turn, product, nothing)

            pe.wait_ge(f_x, T + 1)
            pe.wait_ge(c_square, 3)
            M(ps[:, 7, 200:202], ones[:, :], wsquare, start=True, stop=True).then_inc(c_sum, 1)

            def conv_sums(b, c):
                hh, hl = conv_halves[c % 2]
                for q in range(NB):
                    pe.wait_ge(chunk_in[q], b * 16 + 16 * (FIRST[3] + c * NB + 1))
                    order = [(s, i) for s in range(BT) for i in range(BT)]
                    for s, i in (sorted(order, key=lambda si: si[1]) if q in (0, NB - 1) else order):
                        t = q * BT + s
                        if t == 0:
                            pe.wait_ge(c_read, b * BT + (c * T + i + 1))
                        lhs = chunk[q][:, s, i * P:(i + 1) * P]
                        M(ps[:, i, 0:F + 1], lhs, hh[:, t, 0:F + 1], start=(t == 0), stop=False)
                        ins = M(ps[:, i, 0:F], lhs, hl[:, t, :], start=False, stop=(t == T - 1))
                        if t == T - 1 and i < BT - 1:
                            ins.then_inc(c_bank, 1)
                    ins.then_inc(chunk_used[q], 1)

            for c in range(4):
                if c % 2 == 0:
                    half_scale(3 + c // 2)
                    conv_rows(c // 2)
                    pe.wait_ge(conv[5], (c // 2 + 1) * T + 1)
                if c < 3:
                    with pe.Fori(0, NB) as b:
                        conv_sums(b, c)
            pe.wait_ge(moe_w, 16 * 5)

            def route(t0, n):
                for i in range(BT + 1):
                    if i < BT:
                        pe.wait_ge(r_rows, t0 + (i + 1))
                        pe.wait_ge(r_tcp, t0 + (i + 2 - before(i)))
                        for f in range(2):
                            ins = nc.tensor.transpose(ps[:, 5 + i % 2, f * P:(f + 1) * P], urow[:, i, f * P:(f + 1) * P], ident[:, :])
                        ins.then_inc(r_tps, 1)
                    if i >= 1:
                        j = i - 1
                        pe.wait_ge(r_tcp, t0 + (j + 2))
                        if j == 0:
                            pe.wait_ge(r_lgc, n)
                        logits = ps[:, 7, j * EXPERTS:(j + 1) * EXPERTS]
                        for d in range(2):
                            M(logits, feat[:, d, j * P:(j + 1) * P], wroute[:, d, :], start=(d == 0), stop=False)
                        ins = M(logits, ones[0:1, :], broute, start=False, stop=True)
                ins.then_inc(r_lg, 1)

            conv_sums(0, 3)
            with pe.Fori(1, NB) as b:
                conv_sums(b, 3)
                route(b * BT - BT, b)
            route(T - BT, NB)
            nc.tensor.transpose(ps[:, 6, 0:96], evec_in, ident[0:96, 0:96]).then_inc(r_pe, 1)
            pe.wait_ge(r_dve, 2)
            flat = picked.rearrange("p t e -> p (t e)")
            M(ps[:, 4, 0:T * EXPERTS], tri[:, :], flat, start=True, stop=True)
            M(ps[:, 5, 0:T * EXPERTS], ones[:, :], flat, start=True, stop=True).then_inc(r_pe, 1)
            pe.wait_ge(r_dve, 4)
            pe.wait_ge(r_act, 2)

            def turn_rows(c, s):
                pe.wait_ge(e_in[s], c)
                for i in range(CT):
                    for d in range(2):
                        ins = nc.tensor.transpose(ps[:, 6 + s, d * CAP + i * P:d * CAP + (i + 1) * P], xin[s][:, i, d * P:(d + 1) * P], ident[:, :])
                ins.then_inc(e_tps, 1)

            def hidden(xe, gelu, wi, s):
                pe.wait_ge(w1_in[s], wi)
                pe.wait_ge(e_xe, xe)
                for k in range(EK):
                    if k >= 4:
                        pe.wait_ge(e_gelu, gelu + (k - 3))
                    for d in range(2):
                        ins = M(ps[:, k % 4, 0:CAP], w1e[s][:, d, k * P:(k + 1) * P], xeT[s][:, d, :], start=(d == 0), stop=(d == 1))
                    ins.then_inc(e_hps, 1)

            def outputs(gelu, y, wi, s):
                pe.wait_ge(w2e_in[s], wi)
                pe.wait_ge(e_gelu, gelu)
                pe.wait_ge(e_y, y)
                for i in range(CT):
                    for k in range(EK):
                        ins = M(ps[:, 4 + s, i * F:(i + 1) * F], hT[s][:, k, i * P:(i + 1) * P], w2e[s][:, k, :], start=(k == 0), stop=(k == EK - 1))
                ins.then_inc(e_yps, 1)

            turn_rows(32, 0)
            hidden(2, 1, 16, 0)
            with pe.Fori(0, CHUNKS // 2 - 1) as g:
                turn_rows(g * 32 + 32, 1)
                outputs(g * (2 * EK) + (EK + 1), g * 2 + 1, g * 32 + 32, 0)
                hidden(g * 4 + 4, g * (2 * EK) + (EK + 1), g * 16 + 16, 1)
                turn_rows(g * 32 + 64, 0)
                outputs(g * (2 * EK) + (2 * EK + 1), g * 2 + 2, g * 32 + 32, 1)
                hidden(g * 4 + 6, g * (2 * EK) + (2 * EK + 1), g * 16 + 32, 0)
            turn_rows(32 * (CHUNKS // 2), 1)
            outputs((CHUNKS - 1) * EK + 1, CHUNKS - 1, 32 * (CHUNKS // 2), 0)
            hidden(2 * CHUNKS, (CHUNKS - 1) * EK + 1, 16 * (CHUNKS // 2), 1)
            outputs(CHUNKS * EK + 1, CHUNKS, 32 * (CHUNKS // 2), 1)


_INS = ["x", "src", "dst"]


def kernel(**inputs):
    import numpy as _np
    import concourse.bacc as _bacc
    from concourse import mybir as _mybir
    from concourse.bass_utils import run_bass_kernel_spmd as _run

    nc = _bacc.Bacc("TRN2", target_bir_lowering=False, num_devices=1)
    arrays, aps = {}, {}
    for name, value in inputs.items():
        a = _np.ascontiguousarray(value)
        arrays[name] = a
        aps[name] = nc.dram_tensor(name, a.shape, _mybir.dt.from_np(a.dtype), kind="ExternalInput").ap()
    out = nc.dram_tensor("out", (N, F), _mybir.dt.float32, kind="ExternalOutput").ap()
    weights = {k: v for k, v in aps.items() if k not in _INS}
    build(nc, aps["x"], aps["src"], aps["dst"], weights, out)
    r = _run(nc, [arrays], core_ids=[0])
    return r.results[0]["out"]
```
